# Optimizing a Trainium2 kernel written in Bass

```python
import numpy as np
import jax
import jax.numpy as jnp

def _softmax(x, axis=-1):
    return jax.nn.softmax(x, axis=axis)

def _gelu(x):
    return jax.nn.gelu(x, approximate=True)

def _silu(x):
    return jax.nn.silu(x)

def _sigmoid(x):
    return jax.nn.sigmoid(x)

def _layernorm(x, axis=-1, eps=1e-05):
    m = jnp.mean(x, axis=axis, keepdims=True)
    v = jnp.var(x, axis=axis, keepdims=True)
    return (x - m) / jnp.sqrt(v + eps)

def _scatter_add(tgt, idx, src, axis=0):
    return tgt.at[idx].add(src)

def _segment_sum(src, seg, n):
    return jax.ops.segment_sum(src, seg, n)
kernel_name = 'mk_prb_d2_jaxref_r8_8b8ce5'

def setup_inputs(seed: int=0):
    np.random.seed(seed)
    _w = jnp.asarray

    def _L0_attn_setup():
        import jax, jax.numpy as jnp
        import numpy as np
        D_MODEL = 128
        N_HEADS = 16
        HEAD_DIM = D_MODEL // N_HEADS
        NEG_INF = jnp.float32(-1e+30)

        def _alibi_causal_mask(S, dtype):
            q = jnp.arange(S)[:, None]
            k = jnp.arange(S)[None, :]
            return jnp.where(k <= q, -(q - k).astype(dtype), NEG_INF)
        key = jax.random.key(seed)
        ks = jax.random.split(key, 5)
        B, S, D = (4, 256, D_MODEL)
        scale = 1.0 / np.sqrt(D)
        x = jax.random.normal(ks[0], (B, S, D), dtype=jnp.float32)
        w_qkv = jax.random.normal(ks[1], (3 * D, D), dtype=jnp.float32) * scale
        b_qkv = jnp.zeros((3 * D,), dtype=jnp.float32)
        w_out = jax.random.normal(ks[2], (D, D), dtype=jnp.float32) * scale
        b_out = jnp.zeros((D,), dtype=jnp.float32)
        return {'x': x, 'w_qkv': w_qkv, 'b_qkv': b_qkv, 'w_out': w_out, 'b_out': b_out}
    _L0_attn_in = _L0_attn_setup()

    def _L0_ffn_setup():
        import jax, jax.numpy as jnp
        import numpy as np
        D_MODEL = 128
        EXPERT_DIM = 64
        N_EXPERTS = 8
        TOP_K = 2

        def _sq_relu(h):
            return jnp.square(jax.nn.relu(h))
        key = jax.random.key(seed)
        ks = jax.random.split(key, 6)
        s = 0.02
        x = jax.random.normal(ks[0], (2, 256, D_MODEL), dtype=jnp.float32)
        Ws1 = jax.random.normal(ks[1], (D_MODEL, EXPERT_DIM), dtype=jnp.float32) * s
        Ws2 = jax.random.normal(ks[2], (EXPERT_DIM, D_MODEL), dtype=jnp.float32) * s
        W1 = jax.random.normal(ks[3], (N_EXPERTS, D_MODEL, EXPERT_DIM), dtype=jnp.float32) * s
        W2 = jax.random.normal(ks[4], (N_EXPERTS, EXPERT_DIM, D_MODEL), dtype=jnp.float32) * s
        Wr = jax.random.normal(ks[5], (D_MODEL, N_EXPERTS), dtype=jnp.float32) * s
        return {'x': x, 'Ws1': Ws1, 'Ws2': Ws2, 'W1': W1, 'W2': W2, 'Wr': Wr}
    _L0_ffn_in = _L0_ffn_setup()

    def _L1_attn_setup():
        import jax, jax.numpy as jnp
        import numpy as np
        D_MODEL = 128
        N_HEADS = 16
        ORDER = 6
        M = 2 * ORDER - 1
        D_HEAD = D_MODEL // N_HEADS

        def _collapsed_beta() -> np.ndarray:
            j = np.arange(ORDER, dtype=np.float64)
            alpha = (j + 1.0) ** (-1.5)
            tail = np.cumsum(alpha[::-1])[::-1]
            beta = np.concatenate([[0.0], tail[1:], np.zeros(ORDER - 1)])
            return (beta / beta.sum()).astype(np.float32)

        def _cheb_features(x, m):
            ts = [jnp.ones_like(x), x]
            for _ in range(m - 2):
                ts.append(2.0 * x * ts[-1] - ts[-2])
            return jnp.stack(ts[:m], axis=-1)
        key = jax.random.key(seed)
        k1, k2, k3 = jax.random.split(key, 3)
        B, S = (2, 512)
        x = jax.random.normal(k1, (B, S, D_MODEL), dtype=jnp.float32)
        w_in = jax.random.normal(k2, (3 * D_MODEL, D_MODEL), dtype=jnp.float32) * D_MODEL ** (-0.5)
        w_out = jax.random.normal(k3, (D_MODEL, D_MODEL), dtype=jnp.float32) * D_MODEL ** (-0.5)
        beta = jnp.tile(jnp.asarray(_collapsed_beta())[None, :], (N_HEADS, 1))
        return {'x': x, 'w_in': w_in, 'w_out': w_out, 'beta': beta}
    _L1_attn_in = _L1_attn_setup()

    def _L1_ffn_setup():
        import jax, jax.numpy as jnp
        import numpy as np
        B, N, D = (4, 1024, 128)
        HEADS, DH = (8, 64)
        HID = HEADS * DH
        WIN = 128
        NQ, NKV = (128, 256)
        EPS, N_ITERS, FETCH_K = (1.0, 50, 9.0 / 8.0)
        SCALE = DH ** (-0.5)

        def rmsnorm(x, gamma):
            norm = jnp.maximum(jnp.linalg.norm(x, axis=-1, keepdims=True), 1e-12)
            return x / norm * x.shape[-1] ** 0.5 * gamma

        def coor_descent(s, k):
            logk = jnp.log(jnp.asarray(k, s.dtype))

            def body(_, ab):
                a, b = ab
                a = EPS * (logk - jax.nn.logsumexp((s + b) / EPS, axis=-1, keepdims=True))
                b = -jax.nn.relu(s + a)
                return (a, b)
            a, b = jax.lax.fori_loop(0, N_ITERS, body, (jnp.zeros_like(s[..., :1]), -s))
            return jnp.exp((s + a + b) / EPS)

        def route(x, routing_token, num_tokens):
            s = jnp.einsum('bnd,d->bn', x, routing_token)
            k = min(num_tokens * FETCH_K, x.shape[1])
            scores = coor_descent(s, k)
            sel_scores, sel_idx = jax.lax.top_k(scores, num_tokens)
            sel_scores = sel_scores + jax.lax.stop_gradient(1.0 - sel_scores)
            return (sel_scores, sel_idx)

        def light_local_attn(x, gamma, wq, wkv, wo):
            b, n, d = x.shape
            xn = rmsnorm(x, gamma)
            q = xn @ wq
            k, v = jnp.split(xn @ wkv, 2, axis=-1)

            def win(t):
                return t.reshape(b, n // WIN, WIN, HEADS, DH).transpose(0, 1, 3, 2, 4)
            q, k, v = (win(q) * SCALE, win(k), win(v))
            attn = jax.nn.softmax(jnp.einsum('bwhid,bwhjd->bwhij', q, k), axis=-1)
            out = jnp.einsum('bwhij,bwhjd->bwhid', attn, v)
            out = out.transpose(0, 1, 3, 2, 4).reshape(b, n, HID)
            return out @ wo

        def heavy_attn(xq, context, scores_kv, gamma, wq, wkv_t, wo):
            b, nq, d = xq.shape
            nkv = context.shape[1]
            xqn = rmsnorm(xq, gamma)
            ctx = rmsnorm(context, gamma)[:, None]
            q = (xqn @ wq).reshape(b, nq, HEADS, DH).transpose(0, 2, 1, 3) * SCALE
            kvw = wkv_t.reshape(1, HEADS, 2 * DH, d)
            kv = jnp.einsum('rhdi,brni->brhnd', kvw, ctx)
            k, v = jnp.split(kv, 2, axis=-1)
            v = v * scores_kv[:, None, None, :, None]
            k = k.reshape(b, HEADS, nkv, DH)
            v = v.reshape(b, HEADS, nkv, DH)
            attn = jax.nn.softmax(jnp.einsum('bhid,bhjd->bhij', q, k), axis=-1)
            out = jnp.einsum('bhij,bhjd->bhid', attn, v)
            out = out.transpose(0, 2, 1, 3).reshape(b, nq, HID)
            return out @ wo
        key = jax.random.key(seed)
        ks = jax.random.split(key, 10)
        lin = lambda k, shape, fan: jax.random.normal(k, shape, jnp.float32) * fan ** (-0.5)
        return dict(x=jax.random.normal(ks[0], (B, N, D), jnp.float32), gamma_light=jnp.ones((D,), jnp.float32), wq_light=lin(ks[1], (D, HID), D), wkv_light=lin(ks[2], (D, 2 * HID), D), wo_light=lin(ks[3], (HID, D), HID), q_routing_token=jax.random.normal(ks[4], (D,), jnp.float32), kv_routing_token=jax.random.normal(ks[5], (D,), jnp.float32), gamma_heavy=jnp.ones((D,), jnp.float32), wq_heavy=lin(ks[6], (D, HID), D), wkv_heavy=lin(ks[7], (2 * HID, D), D), wo_heavy=lin(ks[8], (HID, D), HID))
    _L1_ffn_in = _L1_ffn_setup()
    _d = {'L0_attn_x': _L0_attn_in['x'], 'L0_attn_w_qkv': _L0_attn_in['w_qkv'], 'L0_attn_b_qkv': _L0_attn_in['b_qkv'], 'L0_attn_w_out': _L0_attn_in['w_out'], 'L0_attn_b_out': _L0_attn_in['b_out'], 'L0_ffn_Ws1': _L0_ffn_in['Ws1'], 'L0_ffn_Ws2': _L0_ffn_in['Ws2'], 'L0_ffn_W1': _L0_ffn_in['W1'], 'L0_ffn_W2': _L0_ffn_in['W2'], 'L0_ffn_Wr': _L0_ffn_in['Wr'], 'L1_attn_w_in': _L1_attn_in['w_in'], 'L1_attn_w_out': _L1_attn_in['w_out'], 'L1_attn_beta': _L1_attn_in['beta'], 'L1_ffn_gamma_light': _L1_ffn_in['gamma_light'], 'L1_ffn_wq_light': _L1_ffn_in['wq_light'], 'L1_ffn_wkv_light': _L1_ffn_in['wkv_light'], 'L1_ffn_wo_light': _L1_ffn_in['wo_light'], 'L1_ffn_q_routing_token': _L1_ffn_in['q_routing_token'], 'L1_ffn_kv_routing_token': _L1_ffn_in['kv_routing_token'], 'L1_ffn_gamma_heavy': _L1_ffn_in['gamma_heavy'], 'L1_ffn_wq_heavy': _L1_ffn_in['wq_heavy'], 'L1_ffn_wkv_heavy': _L1_ffn_in['wkv_heavy'], 'L1_ffn_wo_heavy': _L1_ffn_in['wo_heavy']}
    _x0 = _d['L0_attn_x']
    _d['L0_attn_x'] = jax.random.normal(jax.random.fold_in(jax.random.key(seed), 1), (8, 512, 128), dtype=_x0.dtype)
    del _x0
    return _d

def reference(L0_attn_x, L0_attn_w_qkv, L0_attn_b_qkv, L0_attn_w_out, L0_attn_b_out, L0_ffn_Ws1, L0_ffn_Ws2, L0_ffn_W1, L0_ffn_W2, L0_ffn_Wr, L1_attn_w_in, L1_attn_w_out, L1_attn_beta, L1_ffn_gamma_light, L1_ffn_wq_light, L1_ffn_wkv_light, L1_ffn_wo_light, L1_ffn_q_routing_token, L1_ffn_kv_routing_token, L1_ffn_gamma_heavy, L1_ffn_wq_heavy, L1_ffn_wkv_heavy, L1_ffn_wo_heavy):

    def _L0_attn_ref(x, w_qkv, b_qkv, w_out, b_out):
        import jax, jax.numpy as jnp
        import numpy as np
        D_MODEL = 128
        N_HEADS = 16
        HEAD_DIM = D_MODEL // N_HEADS
        NEG_INF = jnp.float32(-1e+30)

        def _alibi_causal_mask(S, dtype):
            q = jnp.arange(S)[:, None]
            k = jnp.arange(S)[None, :]
            return jnp.where(k <= q, -(q - k).astype(dtype), NEG_INF)
        B, S, D = x.shape
        H, hd = (N_HEADS, HEAD_DIM)
        qkv = x @ w_qkv.T + b_qkv
        q, k, v = jnp.split(qkv, 3, axis=-1)
        q = q.reshape(B, S, H, hd).transpose(0, 2, 1, 3)
        k = k.reshape(B, S, H, hd).transpose(0, 2, 1, 3)
        v = v.reshape(B, S, H, hd).transpose(0, 2, 1, 3)
        scores = jnp.einsum('bhqd,bhkd->bhqk', q, k) / np.sqrt(hd)
        scores = scores + _alibi_causal_mask(S, scores.dtype)
        probs = jax.nn.softmax(scores, axis=-1)
        out = jnp.einsum('bhqk,bhkd->bhqd', probs, v)
        out = out.transpose(0, 2, 1, 3).reshape(B, S, D)
        return out @ w_out.T + b_out

    def _L0_ffn_ref(x, Ws1, Ws2, W1, W2, Wr):
        import jax, jax.numpy as jnp
        import numpy as np
        D_MODEL = 128
        EXPERT_DIM = 64
        N_EXPERTS = 8
        TOP_K = 2

        def _sq_relu(h):
            return jnp.square(jax.nn.relu(h))
        shape = x.shape
        xf = x.reshape(-1, D_MODEL)
        out_shared = _sq_relu(xf @ Ws1) @ Ws2
        logits = xf @ Wr
        top_vals, top_idx = jax.lax.top_k(logits, TOP_K)
        rw = jax.nn.softmax(top_vals.astype(jnp.float32), axis=-1).astype(x.dtype)
        onehot = jax.nn.one_hot(top_idx, N_EXPERTS, dtype=x.dtype)
        prob = jnp.einsum('tk,tke->te', rw, onehot)
        prob = jnp.trunc(prob)
        h = _sq_relu(jnp.einsum('td,edf->tef', xf, W1))
        y = jnp.einsum('tef,efd->ted', h, W2)
        out_routed = jnp.einsum('ted,te->td', y, prob)
        return (out_shared + out_routed).reshape(shape)

    def _L1_attn_ref(x, w_in, w_out, beta):
        import jax, jax.numpy as jnp
        import numpy as np
        D_MODEL = 128
        N_HEADS = 16
        ORDER = 6
        M = 2 * ORDER - 1
        D_HEAD = D_MODEL // N_HEADS

        def _collapsed_beta() -> np.ndarray:
            j = np.arange(ORDER, dtype=np.float64)
            alpha = (j + 1.0) ** (-1.5)
            tail = np.cumsum(alpha[::-1])[::-1]
            beta = np.concatenate([[0.0], tail[1:], np.zeros(ORDER - 1)])
            return (beta / beta.sum()).astype(np.float32)

        def _cheb_features(x, m):
            ts = [jnp.ones_like(x), x]
            for _ in range(m - 2):
                ts.append(2.0 * x * ts[-1] - ts[-2])
            return jnp.stack(ts[:m], axis=-1)
        B, S, _ = x.shape
        qkv = x @ w_in.T
        q, k, v = jnp.split(qkv, 3, axis=-1)

        def to_heads(t):
            return t.reshape(B, S, N_HEADS, D_HEAD).transpose(0, 2, 1, 3)
        q, k, v = (to_heads(q), to_heads(k), to_heads(v))
        scale = D_HEAD ** (-0.5)
        q = jnp.clip(q * scale, -1.0, 1.0)
        k = jnp.clip(k * scale, -1.0, 1.0)
        tq = _cheb_features(q, M)
        tk = _cheb_features(k, M)
        tq = tq * beta[None, :, None, None, :]
        kv = jnp.einsum('bhskm,bhsv->bhkmv', tk, v)
        out = jnp.einsum('bhsdm,bhdmv->bhsv', tq, kv)
        out = out.transpose(0, 2, 1, 3).reshape(B, S, D_MODEL)
        return out @ w_out.T

    def _L1_ffn_ref(x, gamma_light, wq_light, wkv_light, wo_light, q_routing_token, kv_routing_token, gamma_heavy, wq_heavy, wkv_heavy, wo_heavy):
        import jax, jax.numpy as jnp
        import numpy as np
        B, N, D = (4, 1024, 128)
        HEADS, DH = (8, 64)
        HID = HEADS * DH
        WIN = 128
        NQ, NKV = (128, 256)
        EPS, N_ITERS, FETCH_K = (1.0, 50, 9.0 / 8.0)
        SCALE = DH ** (-0.5)

        def rmsnorm(x, gamma):
            norm = jnp.maximum(jnp.linalg.norm(x, axis=-1, keepdims=True), 1e-12)
            return x / norm * x.shape[-1] ** 0.5 * gamma

        def coor_descent(s, k):
            logk = jnp.log(jnp.asarray(k, s.dtype))

            def body(_, ab):
                a, b = ab
                a = EPS * (logk - jax.nn.logsumexp((s + b) / EPS, axis=-1, keepdims=True))
                b = -jax.nn.relu(s + a)
                return (a, b)
            a, b = jax.lax.fori_loop(0, N_ITERS, body, (jnp.zeros_like(s[..., :1]), -s))
            return jnp.exp((s + a + b) / EPS)

        def route(x, routing_token, num_tokens):
            s = jnp.einsum('bnd,d->bn', x, routing_token)
            k = min(num_tokens * FETCH_K, x.shape[1])
            scores = coor_descent(s, k)
            sel_scores, sel_idx = jax.lax.top_k(scores, num_tokens)
            sel_scores = sel_scores + jax.lax.stop_gradient(1.0 - sel_scores)
            return (sel_scores, sel_idx)

        def light_local_attn(x, gamma, wq, wkv, wo):
            b, n, d = x.shape
            xn = rmsnorm(x, gamma)
            q = xn @ wq
            k, v = jnp.split(xn @ wkv, 2, axis=-1)

            def win(t):
                return t.reshape(b, n // WIN, WIN, HEADS, DH).transpose(0, 1, 3, 2, 4)
            q, k, v = (win(q) * SCALE, win(k), win(v))
            attn = jax.nn.softmax(jnp.einsum('bwhid,bwhjd->bwhij', q, k), axis=-1)
            out = jnp.einsum('bwhij,bwhjd->bwhid', attn, v)
            out = out.transpose(0, 1, 3, 2, 4).reshape(b, n, HID)
            return out @ wo

        def heavy_attn(xq, context, scores_kv, gamma, wq, wkv_t, wo):
            b, nq, d = xq.shape
            nkv = context.shape[1]
            xqn = rmsnorm(xq, gamma)
            ctx = rmsnorm(context, gamma)[:, None]
            q = (xqn @ wq).reshape(b, nq, HEADS, DH).transpose(0, 2, 1, 3) * SCALE
            kvw = wkv_t.reshape(1, HEADS, 2 * DH, d)
            kv = jnp.einsum('rhdi,brni->brhnd', kvw, ctx)
            k, v = jnp.split(kv, 2, axis=-1)
            v = v * scores_kv[:, None, None, :, None]
            k = k.reshape(b, HEADS, nkv, DH)
            v = v.reshape(b, HEADS, nkv, DH)
            attn = jax.nn.softmax(jnp.einsum('bhid,bhjd->bhij', q, k), axis=-1)
            out = jnp.einsum('bhij,bhjd->bhid', attn, v)
            out = out.transpose(0, 2, 1, 3).reshape(b, nq, HID)
            return out @ wo
        b = x.shape[0]
        light_out = light_local_attn(x, gamma_light, wq_light, wkv_light, wo_light)
        scores_q, idx_q = route(x, q_routing_token, NQ)
        scores_kv, idx_kv = route(x, kv_routing_token, NKV)
        routed_q = jnp.take_along_axis(x, idx_q[..., None], axis=1)
        routed_kv = jnp.take_along_axis(x, idx_kv[..., None], axis=1)
        routed_out = heavy_attn(routed_q, routed_kv, scores_kv, gamma_heavy, wq_heavy, wkv_heavy, wo_heavy)
        routed_out = routed_out * scores_q[..., None]
        heavy_out = jnp.zeros_like(x).at[jnp.arange(b)[:, None], idx_q].set(routed_out)
        return light_out + heavy_out
    x = L0_attn_x
    xn = _layernorm(x, axis=-1)
    x = x + _L0_attn_ref(xn, L0_attn_w_qkv, L0_attn_b_qkv, L0_attn_w_out, L0_attn_b_out) + _L0_ffn_ref(xn, L0_ffn_Ws1, L0_ffn_Ws2, L0_ffn_W1, L0_ffn_W2, L0_ffn_Wr)
    xn = _layernorm(x, axis=-1)
    x = x + _L1_attn_ref(xn, L1_attn_w_in, L1_attn_w_out, L1_attn_beta) + _L1_ffn_ref(xn, L1_ffn_gamma_light, L1_ffn_wq_light, L1_ffn_wkv_light, L1_ffn_wo_light, L1_ffn_q_routing_token, L1_ffn_kv_routing_token, L1_ffn_gamma_heavy, L1_ffn_wq_heavy, L1_ffn_wkv_heavy, L1_ffn_wo_heavy)
    return x

_drawn_inputs = setup_inputs


def setup_inputs(seed=0):
    import zlib

    import numpy as np

    out = dict(_drawn_inputs(seed))
    spreads = {'L0_attn_b_qkv': (0.0, 0.1),
     'L0_attn_b_out': (0.0, 0.1),
     'L1_ffn_gamma_light': (1.0, 0.6),
     'L1_ffn_gamma_heavy': (1.0, 0.6)}
    factors = {'L0_ffn_Ws1': 8.0,
     'L1_ffn_wq_light': 8.0,
     'L1_ffn_wkv_light': 8.0,
     'L1_ffn_wo_light': 8.0,
     'L1_ffn_q_routing_token': 8.0,
     'L1_ffn_kv_routing_token': 8.0,
     'L1_ffn_wq_heavy': 8.0,
     'L1_ffn_wkv_heavy': 8.0,
     'L1_ffn_wo_heavy': 8.0}
    for name, (base, spread) in spreads.items():
        noise = np.random.default_rng([zlib.crc32(name.encode()), seed]).standard_normal(out[name].shape)
        drawn = base * np.exp(spread * noise) if base else spread * noise
        out[name] = jnp.asarray(drawn.astype(out[name].dtype))
    for name, factor in factors.items():
        out[name] = (out[name] * factor).astype(out[name].dtype)
    return out
```

```python
import math
from contextlib import ExitStack

import concourse.bass as bass
from concourse import mybir
from concourse.alu_op_type import AluOpType as ALU

ACT = mybir.ActivationFunctionType
F32 = mybir.dt.float32
BF16 = mybir.dt.bfloat16
I32 = mybir.dt.int32
AX = mybir.AxisListType

P = 128
B, S, D = 8, 512, 128
T = S // P
H0, HD0 = 16, 8
NEG = -1e30
EPS = 1e-5

Q_PART = (0, 0, 1, 1, 0, 2)
K_PART = (0, 1, 0, 1, 2, 0)
ROW_POS = HD0 * len(Q_PART)
ROW_MAX = ROW_POS + 1
ROWS = ROW_MAX + 3


class Chain:

    def __init__(self, eng, sem, turn=0, per=0):
        self.eng, self.sem, self.base, self.per, self.n = eng, sem, turn * per, per, 0

    def __call__(self, ins, held=None):
        self.n += 1
        ins.then_inc(self.sem, 1)
        self.eng.wait_ge(self.sem, self.base + self.n)
        if held is not None:
            self.eng.sem_inc(held, 1)

    def close(self):
        assert self.per in (0, self.n), (self.per, self.n)


def inv_sqrt(dve, link, v, y, t, steps=4):
    link(dve.tensor_scalar(y.bitcast(I32), v.bitcast(I32), 1, None, ALU.logical_shift_right))
    link(dve.tensor_scalar(y.bitcast(I32), y.bitcast(I32), -1.0, float(0x5F3759DF), ALU.mult, ALU.add))
    for _ in range(steps):
        link(dve.tensor_tensor(t, y, y, ALU.mult))
        link(dve.scalar_tensor_tensor(t, t, -0.5, v, ALU.mult, ALU.mult))
        link(dve.scalar_tensor_tensor(y, t, 1.5, y, ALU.add, ALU.mult))


class Mem:

    def __init__(self, nc, ctx, phase=""):
        self.nc, self.ctx, self.phase = nc, ctx, phase

    def sb(self, name, shape, dt=F32):
        return self.ctx.enter_context(self.nc.sbuf_tensor(self.phase + name, shape, dt))

    def sem(self, name):
        return self.ctx.enter_context(self.nc.semaphore(self.phase + name))


def setup(nc, g, w):
    with ExitStack() as ctx:
        m = Mem(nc, ctx)
        nat = m.sb("nat", [P, 16, P])
        loaded, w_loaded, ident_made, ident_b, turned, moved, made, beta_ld, mb = (m.sem(n) for n in (
            "loaded", "w_loaded", "ident_made", "ident_b", "turned", "moved", "made", "beta_ld", "mb"))
        betac = m.sb("betac", [P, 11])
        block = ctx.enter_context(nc.Block())
        ps = g.ps

        @block.sync
        def _(sp):
            with nc.allow_non_contiguous_dma(reason="columns of small vectors"):
                sp.dma_start(nat[:, 0:3, :], w["L0_attn_w_qkv"].rearrange("(c p) d -> p c d", p=P)).then_inc(w_loaded, 16)
                sp.dma_start(nat[:, 3, :], w["L0_attn_w_out"]).then_inc(w_loaded, 16)
                sp.dma_start(nat[:, 4:7, :], w["L1_attn_w_in"].rearrange("(c p) d -> p c d", p=P)).then_inc(w_loaded, 16)
                sp.dma_start(nat[:, 7, :], w["L1_attn_w_out"]).then_inc(w_loaded, 16)
                sp.dma_start(nat[:, 8:16, :], w["L1_ffn_wkv_heavy"].rearrange("(c p) d -> p c d", p=P)).then_inc(w_loaded, 16)
                n = 0
                for dst, src in (
                    (g.xs[:], w["L0_attn_x"].rearrange("b (t p) d -> p (b t) d", p=P)),
                    (g.ws1[:], w["L0_ffn_Ws1"]), (g.ws2[:], w["L0_ffn_Ws2"]), (g.wr[:], w["L0_ffn_Wr"]),
                    (g.w1[:], w["L0_ffn_W1"].rearrange("e d f -> d e f")),
                    (g.w2[:], w["L0_ffn_W2"].rearrange("(c e) f d -> (e f) c d", e=2)),
                    (g.bqkv[:], w["L0_attn_b_qkv"].rearrange("(c p) -> p c", p=P)),
                    (g.bv[:], w["L0_attn_b_qkv"][2 * P:3 * P].rearrange("(a d) -> a d", a=1).to_broadcast([P, P])),
                    (g.bo[:], w["L0_attn_b_out"].rearrange("(a d) -> a d", a=1).to_broadcast([P, P])),
                    (g.gl[:], w["L1_ffn_gamma_light"].rearrange("(p a) -> p a", a=1)),
                    (g.gh[:], w["L1_ffn_gamma_heavy"].rearrange("(p a) -> p a", a=1)),
                    (g.tok[:, 0:1], w["L1_ffn_kv_routing_token"].rearrange("(p a) -> p a", a=1)),
                    (g.tok[:, 1:2], w["L1_ffn_q_routing_token"].rearrange("(p a) -> p a", a=1)),
                    (g.wql[:], w["L1_ffn_wq_light"]), (g.wkvl[:], w["L1_ffn_wkv_light"]),
                    (g.wol[:], w["L1_ffn_wo_light"].rearrange("(c p) d -> p c d", p=P)),
                    (g.wqh[:], w["L1_ffn_wq_heavy"]),
                    (g.woh[:], w["L1_ffn_wo_heavy"].rearrange("(c p) d -> p c d", p=P)),
                ):
                    sp.dma_start(dst, src).then_inc(loaded, 16)
                    n += 1
                for h in range(H0):
                    sp.dma_start(betac[HD0 * h:HD0 * h + HD0, :],
                                 w["L1_attn_beta"][h:h + 1, :].to_broadcast([HD0, 11])).then_inc(beta_ld, 16)
            sp.wait_ge(loaded, 16 * n)

        @block.gpsimd
        def _(pool):
            pool.memset(g.ident[:], 1.0).then_inc(made, 1)
            pool.memset(g.maskb[:], 0.0).then_inc(made, 1)
            pool.memset(g.ones[:], 1.0).then_inc(made, 1)
            pool.memset(g.blk[:], 1.0).then_inc(made, 1)
            pool.wait_ge(made, 4)
            pool.affine_select(out=g.ident[:], in_=g.ident[:], compare_op=ALU.is_equal, fill=0.0, base=0,
                               pattern=[[-1, P]], channel_multiplier=1).then_inc(ident_made, 1)
            pool.affine_select(out=g.maskb[:, 0, :], in_=g.maskb[:, 0, :], compare_op=ALU.is_ge, fill=NEG, base=0,
                               pattern=[[-1, P]], channel_multiplier=1).then_inc(made, 1)
            pool.affine_select(out=g.maskb[:, 1, :], in_=g.maskb[:, 1, :], compare_op=ALU.is_ge, fill=NEG, base=0,
                               pattern=[[1, P]], channel_multiplier=-1).then_inc(made, 1)
            pool.affine_select(out=g.blk[:], in_=g.blk[:], compare_op=ALU.is_ge, fill=0.0, base=0,
                               pattern=[[-HD0, H0], [0, HD0]], channel_multiplier=1).then_inc(made, 1)
            pool.wait_ge(made, 7)
            pool.affine_select(out=g.blk[:], in_=g.blk[:], compare_op=ALU.is_ge, fill=0.0, base=HD0 - 1,
                               pattern=[[HD0, H0], [0, HD0]], channel_multiplier=-1).then_inc(made, 1)
            pool.iota(g.iota[:], pattern=[[1, 256]], base=0, channel_multiplier=0,
                      allow_small_or_imprecise_dtypes=True).then_inc(made, 1)
            pool.memset(g.selm[:], 0.0).then_inc(made, 1)
            for c in range(3):
                pool.wait_ge(made, 10 + c)
                pool.affine_select(out=g.selm[:], in_=g.selm[:], compare_op=ALU.not_equal, fill=-1.0, base=-8 * c,
                                   pattern=[[-1, 8], [0, P]], channel_multiplier=1).then_inc(made, 1)
            pool.wait_ge(made, 13)
            pool.wait_ge(ident_made, 1)
            pool.tensor_copy(g.identb[:], g.ident[:]).then_inc(ident_b, 1)
            pool.wait_ge(made, 9)
            pool.wait_ge(ident_b, 1)

        @block.tensor
        def _(pe):
            pe.wait_ge(ident_made, 1)
            pe.wait_ge(w_loaded, 80)
            for c in range(16):
                ins = pe.transpose(ps[:, c // 4, (c % 4) * P:(c % 4 + 1) * P], nat[:, c, :], g.ident[:])
            ins.then_inc(turned, 1)

        @block.vector
        def _(dve):
            dve.wait_ge(turned, 1)
            dve.tensor_copy(g.wt[:, 0:4, :], ps[:, 0, :]).then_inc(moved, 1)
            dve.tensor_copy(g.wt[:, 4:8, :], ps[:, 1, :]).then_inc(moved, 1)
            for c in (0, 1):
                heads = ps[:, 2 + c, :].rearrange("p (h k d) -> p h k d", h=4, k=2)
                for k, dst in ((0, g.wkh), (1, g.wvh)):
                    dve.tensor_copy(dst[:, c * 256:c * 256 + 256].rearrange("p (h d) -> p h d", h=4),
                                    heads[:, :, k, :]).then_inc(moved, 1)
            dve.wait_ge(made, 9)
            dve.wait_ge(beta_ld, 16 * H0)
            for k in range(11):
                dve.tensor_scalar(g.mbeta[:, k, :], g.blk[:], betac[:, k:k + 1], None, ALU.mult).then_inc(mb, 1)
            dve.wait_ge(mb, 11)
            dve.wait_ge(moved, 6)



def layer0(nc, g, w):
    PAIRS = H0 // 2
    UNITS = T * PAIRS
    with ExitStack() as ctx:
        m = Mem(nc, ctx, "l0_")
        ps = g.ps
        st = m.sb("bn_parts", [P, T, 6])
        mv = m.sb("mean_var", [P, T, 2])
        rstd = m.sb("rstd", [P, 3, T])
        xn = m.sb("xn", [P, T, P])
        xnT = m.sb("xnT", [P, S])
        full = m.sb("full", [P, 2, S])
        rest = m.sb("rest", [P, 2, S])
        part = m.sb("part", [P, 2, 3, S], BF16)
        qS = m.sb("qS", [ROWS, H0, S], BF16)
        kS = m.sb("kS", [ROWS, H0, S], BF16)
        pos = m.sb("pos", [1, S], BF16)
        va = m.sb("va", [P, T, H0, HD0 + 1])
        bq = m.sb("bq", [P, 1])
        hr = m.sb("hr", [64, S])
        h2 = m.sb("h2", [64, S])
        mx = m.sb("mx", [P, T, H0])
        mrest = m.sb("mrest", [P, T, H0])
        mpart = m.sb("mpart", [P, T, 3, H0], BF16)
        mT = m.sb("mT", [3 * H0, S], BF16)
        PT = m.sb("PT", [P, 2, 2, S])
        rsum = m.sb("rsum", [P, T, H0])
        o = m.sb("o", [P, T, P])
        oT = m.sb("oT", [P, S])
        (x_seen, xn_made, turned, xnT_made, qk_proj, v_proj, h_proj, evac, split, laid, mlaid, v_made, relu, squared,
         scored, maxed, m_made, m_turned, mT_made, st_made, exped, pv_done, o_made, o_turned, oT_made, acc_made, x_made,
         x_bias, dch, pch, rows_set, pos_laid, bq_made, stored,
         l_proj, xnT_kept, dve_held, pool_held, pe_held, sp_held) = (m.sem(n) for n in (
            "x_seen xn_made turned xnT_made qk_proj v_proj h_proj evac split laid mlaid v_made relu squared "
            "scored maxed m_made m_turned mT_made st_made exped pv_done o_made o_turned oT_made acc_made x_made "
            "x_bias dch pch rows_set pos_laid bq_made stored l_proj xnT_kept dve_held pool_held pe_held sp_held").split())
        by_feature = nc.dram_tensor("by_feature", [2, 3, P, S], BF16).ap()
        BANK_T, BANK_V, BANK_H, BANK_O = 7, 2, 3, 6
        block = ctx.enter_context(nc.Block())

        @block.sync
        def _(sp):
            for turns in (acc_made, l_proj, mlaid, pv_done, split, squared, stored, x_made, xnT_kept):
                sp.sem_inc(turns, 1)
            sp.wait_ge(rows_set, 3)
            sp.dma_start(kS[ROW_POS:ROW_POS + 1, :, :], pos[:].rearrange("p (a s) -> p a s", a=1).to_broadcast([1, H0, S])).then_inc(pos_laid, 16)
            sp.wait_ge(pos_laid, 16)
            with sp.Fori(0, B) as i:
                for side, rows, parts in ((0, qS, Q_PART), (1, kS, K_PART)):
                    sp.wait_ge(split, i * 2 + side + 2)
                    sp.dma_start(by_feature[side].rearrange("c p s -> p c s"), part[:, side, :, :]).then_inc(stored, 16)
                    sp.wait_ge(stored, i * 32 + side * 16 + 16 + 1)
                    sp.sem_inc(sp_held, 1)
                    sp.wait_ge(pv_done, i * UNITS + 1)
                    for r, c in enumerate(parts):
                        sp.dma_start(rows[HD0 * r:HD0 * r + HD0, :, :],
                                     by_feature[side, c].rearrange("(h d) s -> d h s", d=HD0)).then_inc(laid, 16)
                sp.wait_ge(mT_made, i + 1)
                for c in range(3):
                    sp.dma_start(qS[ROW_MAX + c:ROW_MAX + c + 1, :, :], mT[c * H0:(c + 1) * H0, :]).then_inc(mlaid, 16)
            sp.wait_ge(mlaid, 48 * B + 1)

        @block.gpsimd
        def _(pool):
            pool.memset(kS[:], -1.0).then_inc(rows_set, 1)
            pool.memset(qS[:], 1.0).then_inc(rows_set, 1)
            pool.iota(pos[:], pattern=[[1, S]], base=-S // 2, channel_multiplier=0,
                      allow_small_or_imprecise_dtypes=True).then_inc(rows_set, 1)
            with pool.Fori(0, B) as i:
                link = Chain(pool, pch, i, 8)
                for side in range(2):
                    pool.wait_ge(evac, i * 2 + side + 1)
                    pool.wait_ge(stored, i * 32 + 1)
                    pool.sem_inc(pool_held, 1)
                    f, r, p3 = full[:, side, :], rest[:, side, :], part[:, side]
                    link(pool.tensor_copy(p3[:, 0, :], f), pool_held)
                    link(pool.tensor_tensor(r, f, p3[:, 0, :], ALU.subtract), pool_held)
                    link(pool.tensor_copy(p3[:, 1, :], r), pool_held)
                    link(pool.tensor_tensor(p3[:, 2, :], r, p3[:, 1, :], ALU.subtract))
                    pool.sem_inc(split, 1)
                pool.wait_ge(xnT_made, i + 1)
                pool.sem_inc(pool_held, 1)
                pool.tensor_copy(g.xnT_all[:, bass.ds(i * S, S)], xnT[:]).then_inc(xnT_kept, 1)
                pool.wait_ge(relu, i + 1)
                pool.wait_ge(acc_made, i + 1)
                pool.tensor_tensor(h2[:], hr[:], hr[:], ALU.mult).then_inc(squared, 1)
                pool.wait_ge(xn_made, i + 1)
                x_b = g.xs[:, bass.ds(i * T, T), :]
                pool.tensor_tensor(x_b, x_b, g.bo[:].rearrange("p (a d) -> p a d", a=1).to_broadcast([P, T, P]),
                                   ALU.add).then_inc(x_bias, 1)
                link.close()

        @block.tensor
        def _(pe):
            pe.wait_ge(pos_laid, 16)

            def front(i):
                pe.wait_ge(xn_made, i + 1)
                pe.wait_ge(x_made, i + 1)
                for t in range(T):
                    ins = pe.transpose(ps[:, BANK_T, t * P:(t + 1) * P], xn[:, t, :], g.ident[:])
                ins.then_inc(turned, 1)
                pe.wait_ge(xnT_made, i + 1)
                for c in range(2):
                    pe.matmul(ps[:, c, :], lhsT=g.wt[:, c, :], rhs=xnT[:], start=True, stop=True).then_inc(qk_proj, 1)
                for t in range(T):
                    ins = pe.matmul(ps[:, BANK_V, t * P:(t + 1) * P], lhsT=xnT[:, t * P:(t + 1) * P], rhs=g.wt[:, 2, :],
                                    start=True, stop=True)
                ins.then_inc(v_proj, 1)
                pe.matmul(ps[0:64, BANK_H, :], lhsT=g.ws1[:], rhs=xnT[:], start=True, stop=True).then_inc(h_proj, 1)
                for t in range(T):
                    ins = pe.matmul(ps[:, 4, t * 8:(t + 1) * 8], lhsT=xnT[:, t * P:(t + 1) * P], rhs=g.wr[:],
                                    start=True, stop=True)
                ins.then_inc(l_proj, 1)

            def scores(i, u):
                qt, h = divmod(u, H0)
                n = (qt + 1) * P
                if u == 0:
                    pe.wait_ge(evac, i * 2 + 2)
                    pe.wait_ge(laid, (i + 1) * (16 * 2 * len(Q_PART)))
                pe.wait_ge(maxed, i * (T * H0) + u + 1)
                pe.matmul(ps[:, u % 2, 0:n], lhsT=qS[0:ROW_MAX, h, qt * P:(qt + 1) * P], rhs=kS[0:ROW_MAX, h, 0:n],
                          start=True, stop=False)
                pe.matmul(ps[:, u % 2, n - P:n], lhsT=g.identb[:], rhs=g.maskb[:, 0, :],
                          start=False, stop=True).then_inc(scored, 1)

            def turned_scores(i, u):
                qt, pair = divmod(u, PAIRS)
                if u == 0:
                    pe.wait_ge(mlaid, (i + 1) * 48 + 1)
                    pe.wait_ge(v_made, i + 1)
                    pe.wait_ge(relu, i + 1)
                pe.wait_ge(exped, i * UNITS + u + 1)
                for j in range(2):
                    h = 2 * pair + j
                    for kt in range(qt + 1):
                        out = ps[:, 2 + 2 * (u % 2) + j, kt * P:(kt + 1) * P]
                        ins = pe.matmul(out, lhsT=kS[:, h, kt * P:(kt + 1) * P], rhs=qS[:, h, qt * P:(qt + 1) * P],
                                        start=True, stop=kt < qt)
                    ins = pe.matmul(out, lhsT=g.identb[:], rhs=g.maskb[:, 1, :], start=False, stop=True)
                ins.then_inc(st_made, 1)

            def weigh(i, u):
                qt, pair = divmod(u, PAIRS)
                pe.wait_ge(exped, i * UNITS + u + 3)
                if pair == 0:
                    pe.wait_ge(o_made, i * T + qt + 1)
                for j in range(2):
                    h = 2 * pair + j
                    c = h * (HD0 + 1)
                    for kt in range(qt + 1):
                        ins = pe.matmul(ps[:, BANK_O, c:c + HD0 + 1], lhsT=PT[:, u % 2, j, kt * P:(kt + 1) * P],
                                        rhs=va[:, kt, h, :], start=kt == 0, stop=kt == qt)
                ins.then_inc(pv_done, 1)

            def tail(i):
                pe.wait_ge(o_made, i * T + T + 1)
                for t in range(T):
                    ins = pe.transpose(ps[:, BANK_T, t * P:(t + 1) * P], o[:, t, :], g.ident[:])
                ins.then_inc(o_turned, 1)
                pe.wait_ge(oT_made, i + 1)
                pe.wait_ge(squared, i + 2)
                for t in range(T):
                    out = ps[:, BANK_T, t * P:(t + 1) * P]
                    pe.matmul(out, lhsT=oT[:, t * P:(t + 1) * P], rhs=g.wt[:, 3, :], start=True, stop=False)
                    ins = pe.matmul(out, lhsT=h2[:, t * P:(t + 1) * P], rhs=g.ws2[:], start=False, stop=True)
                ins.then_inc(acc_made, 1)

            with pe.Fori(0, B) as i:
                front(i)
                for u in range(T * H0):
                    scores(i, u)
                pe.wait_ge(m_made, i + 1)
                pe.sem_inc(pe_held, 1)
                for t in range(T):
                    ins = pe.transpose(ps[:, BANK_T, :].bitcast(BF16)[0:3 * H0, t * P:(t + 1) * P],
                                       mpart[:, t, :, :], g.identb[:])
                ins.then_inc(m_turned, 1)
                turned_scores(i, 0)
                for u in range(UNITS):
                    if u + 1 < UNITS:
                        turned_scores(i, u + 1)
                    weigh(i, u)
                tail(i)

        @block.scalar
        def _(act):
            act.mul(bq[:], g.bqkv[:, 0:1], HD0 ** -0.5).then_inc(bq_made, 1)
            act.wait_ge(bq_made, 1)
            act.sem_inc(exped, 2)
            with act.Fori(0, B) as i:
                act.wait_ge(turned, i + 1)
                act.wait_ge(l_proj, i + 1)
                act.wait_ge(xnT_kept, i + 1)
                act.copy(xnT[:], ps[:, BANK_T, :]).then_inc(xnT_made, 1)
                act.wait_ge(qk_proj, i * 2 + 1)
                act.wait_ge(split, i * 2 + 1)
                act.activation(full[:, 0, :], ps[:, 0, :], ACT.Identity, bias=bq[:], scale=HD0 ** -0.5).then_inc(evac, 1)
                act.wait_ge(qk_proj, i * 2 + 2)
                act.activation(full[:, 1, :], ps[:, 1, :], ACT.Identity, bias=g.bqkv[:, 1:2]).then_inc(evac, 1)
                act.wait_ge(h_proj, i + 1)
                act.wait_ge(squared, i + 1)
                act.activation(hr[:], ps[0:64, BANK_H, :], ACT.Relu).then_inc(relu, 1)
                act.wait_ge(m_turned, i + 1)
                act.wait_ge(mlaid, i * 48 + 1)
                act.copy(mT[:], ps[:, BANK_T, :].bitcast(BF16)[0:3 * H0, 0:S]).then_inc(mT_made, 1)
                for u in range(UNITS):
                    n = (u // PAIRS + 1) * P
                    act.wait_ge(st_made, i * UNITS + u + 1)
                    if u >= 2:
                        act.wait_ge(pv_done, i * UNITS + u )
                    else:
                        act.wait_ge(pv_done, i * UNITS + 1)
                    b0 = 2 + 2 * (u % 2)
                    act.activation(PT[:, u % 2, :, 0:n], ps[:, b0:b0 + 2, 0:n], ACT.Exp).then_inc(exped, 1)
                act.wait_ge(o_turned, i + 1)
                act.wait_ge(acc_made, i + 1)
                act.copy(oT[:], ps[:, BANK_T, :]).then_inc(oT_made, 1)

        @block.vector
        def _(dve):
            dve.memset(va[:], 1.0).then_inc(x_seen, 1)
            dve.wait_ge(x_seen, 1)
            dve.sem_inc(maxed, 2)
            dve.sem_inc(o_made, 1)
            with dve.Fori(0, B) as i:
                link = Chain(dve, dch, i, 25)
                x_b = g.xs[:, bass.ds(i * T, T), :]
                for t in range(T):
                    ins = dve.bn_stats(st[:, t, :], g.xs[:, bass.ds(i * T + t, 1), :])
                link(ins, dve_held)
                for t in range(T):
                    ins = dve.bn_aggr(mv[:, t, :], st[:, t, :])
                link(ins)
                link(dve.tensor_scalar(rstd[:, 0, :], mv[:, :, 1], EPS, None, ALU.add))
                inv_sqrt(dve, link, rstd[:, 0, :], rstd[:, 1, :], rstd[:, 2, :])
                for t in range(T):
                    ins = dve.tensor_scalar(xn[:, t, :], g.xs[:, bass.ds(i * T + t, 1), :], mv[:, t, 0:1],
                                            rstd[:, 1, t:t + 1], ALU.subtract, ALU.mult)
                ins.then_inc(xn_made, 1)
                dve.wait_ge(l_proj, i + 2)
                dve.tensor_copy(g.logits[:, bass.ds(i * T, T), :], ps[:, 4, 0:T * 8].rearrange("p (t e) -> p t e", t=T))
                dve.wait_ge(pv_done, i * UNITS + 1)
                for t in range(T):
                    ins = dve.tensor_tensor(va[:, t, :, 0:HD0],
                                            ps[:, BANK_V, t * P:(t + 1) * P].rearrange("p (h d) -> p h d", h=H0),
                                            g.bv[:].rearrange("p (h d) -> p h d", h=H0), ALU.add)
                ins.then_inc(v_made, 1)
                for u in range(T * H0):
                    qt, h = divmod(u, H0)
                    dve.wait_ge(scored, i * (T * H0) + u + 1)
                    dve.tensor_reduce(mx[:, qt, h:h + 1], ps[:, u % 2, 0:(qt + 1) * P], AX.X, ALU.max).then_inc(maxed, 1)
                dve.wait_ge(maxed, (i + 1) * (T * H0) + 2)
                link(dve.tensor_copy(mpart[:, :, 0, :], mx[:]))
                link(dve.tensor_tensor(mrest[:], mx[:], mpart[:, :, 0, :], ALU.subtract))
                link(dve.tensor_copy(mpart[:, :, 1, :], mrest[:]))
                link(dve.tensor_tensor(mpart[:, :, 2, :], mrest[:], mpart[:, :, 1, :], ALU.subtract))
                dve.sem_inc(m_made, 1)
                for qt in range(T):
                    c = 0
                    O = ps[:, BANK_O, c:c + H0 * (HD0 + 1)].rearrange("p (h d) -> p h d", h=H0)
                    dve.wait_ge(pv_done, i * UNITS + (qt + 1) * PAIRS + 1)
                    link(dve.reciprocal(rsum[:, qt, :], O[:, :, HD0]))
                    dve.tensor_tensor(o[:, qt, :].rearrange("p (h d) -> p h d", h=H0), O[:, :, 0:HD0],
                                      rsum[:, qt, :].rearrange("p (h a) -> p h a", a=1).to_broadcast([P, H0, HD0]),
                                      ALU.mult).then_inc(o_made, 1)
                dve.wait_ge(acc_made, i + 2)
                dve.wait_ge(x_bias, i + 1)
                dve.tensor_tensor(x_b, ps[:, BANK_T, :].rearrange("p (t d) -> p t d", t=T), x_b, ALU.add).then_inc(x_made, 1)
                link.close()
            dve.wait_ge(x_made, B + 1)



def gates(nc, g):
    N = B * T
    with ExitStack() as ctx:
        m = Mem(nc, ctx, "gt_")
        top = m.sb("top8", [P, N, 8])
        d = m.sb("gate_d", [P, 4, N])
        total = m.sb("gate_total", [P, 1])
        topped, exped, dch, counted, summed, flagged = (m.sem(n) for n in "topped exped dch counted summed flagged".split())
        block = ctx.enter_context(nc.Block())

        @block.vector
        def _(dve):
            link = Chain(dve, dch)
            for t in range(N):
                ins = dve.max(top[:, t, :], g.logits[:, t, :])
            link(ins)
            dve.tensor_tensor(d[:, 0, :], top[:, :, 1], top[:, :, 0], ALU.subtract).then_inc(topped, 1)
            dve.wait_ge(exped, 1)
            link(dve.tensor_scalar(d[:, 2, :], d[:, 1, :], 1.0, None, ALU.add))
            link(dve.reciprocal(d[:, 3, :], d[:, 2, :]))
            link(dve.tensor_scalar(d[:, 3, :], d[:, 3, :], 1.0, None, ALU.is_ge))
            link(dve.tensor_tensor(g.gate[:], g.logits[:], top[:, :, 0:1].to_broadcast([P, N, 8]), ALU.is_equal))
            link(dve.tensor_tensor(g.gate[:], g.gate[:],
                                   d[:, 3, :].rearrange("p (n a) -> p n a", a=1).to_broadcast([P, N, 8]), ALU.mult))
            dve.tensor_reduce(total[:], g.gate[:], AX.XY, ALU.add).then_inc(counted, 1)
            dve.wait_ge(summed, 1)
            dve.tensor_copy(g.any_gate[:], g.ps[:, 0, 0:1]).then_inc(flagged, 1)
            dve.wait_ge(flagged, 1)

        @block.scalar
        def _(act):
            act.wait_ge(topped, 1)
            act.activation(d[:, 1, :], d[:, 0, :], ACT.Exp).then_inc(exped, 1)

        @block.tensor
        def _(pe):
            pe.wait_ge(counted, 1)
            pe.matmul(g.ps[:, 0, 0:1], lhsT=g.ones[:], rhs=total[:], start=True, stop=True).then_inc(summed, 1)


def routed_experts(nc, g):
    with ExitStack() as ctx:
        m = Mem(nc, ctx, "ex_")
        ps = g.ps
        gate = m.sb("gate_now", [P, T, 8])
        gT = m.sb("gT", [8, S])
        esel = m.sb("esel", [8, 4, 2, 64])
        r = m.sb("r", [P, 4, S])
        r2 = m.sb("r2", [P, 4, S])
        (e_set, gate_copied, g_turned, gT_made, h_made, spread, relu_made, squared, gated, y_made, added) = (
            m.sem(n) for n in (
                "e_set gate_copied g_turned gT_made h_made spread relu_made squared gated y_made added").split())
        block = ctx.enter_context(nc.Block())

        @block.sync
        def _(sp):
            for turns in (added, g_turned, gated, squared, y_made):
                sp.sem_inc(turns, 1)

        @block.gpsimd
        def _(pool):
            with pool.If(pool.value_load(g.any_gate[0:1, 0:1]) > 0):
                pool.memset(esel[:], 1.0).then_inc(e_set, 1)
                pool.wait_ge(e_set, 1)
                pool.affine_select(out=esel[:], in_=esel[:], compare_op=ALU.is_equal, fill=0.0, base=0,
                                   pattern=[[-2, 4], [-1, 2], [0, 64]], channel_multiplier=1).then_inc(e_set, 1)

        @block.tensor
        def _(pe):
            with pe.If(pe.value_load(g.any_gate[0:1, 0:1]) > 0):
                pe.wait_ge(e_set, 2)
                with pe.Fori(0, B) as i:
                    pe.wait_ge(gate_copied, i + 1)
                    for t in range(T):
                        ins = pe.transpose(ps[0:8, 0, t * P:(t + 1) * P], gate[:, t, :], g.ident[:])
                    ins.then_inc(g_turned, 1)
                    pe.wait_ge(gT_made, i + 1)
                    for c in range(4):
                        pe.wait_ge(squared, i * 4 + c + 1)
                        pe.matmul(ps[:, 1 + c % 2, :], lhsT=g.w1[:, 2 * c:2 * c + 2, :],
                                  rhs=g.xnT_all[:, bass.ds(i * S, S)], start=True, stop=True).then_inc(h_made, 1)
                        pe.wait_ge(gated, i * 4 + c + 1)
                        pe.matmul(ps[:, 3 + c % 2, :], lhsT=esel[:, c, :, :], rhs=gT[:], start=True,
                                  stop=True).then_inc(spread, 1)
                    pe.wait_ge(gated, i * 4 + 4 + 1)
                    pe.wait_ge(added, i + 1)
                    for t in range(T):
                        for c in range(4):
                            ins = pe.matmul(ps[:, 5, t * P:(t + 1) * P], lhsT=r2[:, c, t * P:(t + 1) * P], rhs=g.w2[:, c, :],
                                            start=c == 0, stop=c == 3)
                    ins.then_inc(y_made, 1)

        @block.scalar
        def _(act):
            with act.If(act.value_load(g.any_gate[0:1, 0:1]) > 0):
                with act.Fori(0, B) as i:
                    act.wait_ge(g_turned, i + 2)
                    act.copy(gT[:], ps[0:8, 0, :]).then_inc(gT_made, 1)
                    for c in range(4):
                        act.wait_ge(h_made, i * 4 + c + 1)
                        act.wait_ge(gated, i * 4 + 1)
                        act.activation(r[:, c, :], ps[:, 1 + c % 2, :], ACT.Relu).then_inc(relu_made, 1)

        @block.vector
        def _(dve):
            with dve.If(dve.value_load(g.any_gate[0:1, 0:1]) > 0):
                with dve.Fori(0, B) as i:
                    dve.wait_ge(g_turned, i + 1)
                    dve.tensor_copy(gate[:], g.gate[:, bass.ds(i * T, T), :]).then_inc(gate_copied, 1)
                    dve.wait_ge(y_made, i + 1)
                    for c in range(4):
                        dve.wait_ge(relu_made, i * 4 + c + 1)
                        dve.tensor_tensor(r2[:, c, :], r[:, c, :], r[:, c, :], ALU.mult).then_inc(squared, 1)
                        dve.wait_ge(spread, i * 4 + c + 1)
                        dve.wait_ge(squared, i * 4 + c + 2)
                        dve.tensor_tensor(r2[:, c, :], r2[:, c, :], ps[:, 3 + c % 2, :], ALU.mult).then_inc(gated, 1)
                    dve.wait_ge(y_made, i + 2)
                    x_b = g.xs[:, bass.ds(i * T, T), :]
                    dve.tensor_tensor(x_b, ps[:, 5, :].rearrange("p (t d) -> p t d", t=T), x_b, ALU.add).then_inc(added, 1)
                dve.wait_ge(added, B + 1)



def layer1(nc, g):
    HL, HDL = 8, 64
    with ExitStack() as ctx:
        m = Mem(nc, ctx, "l1_")
        ps = g.ps
        st = m.sb("bn_parts", [P, T, 6])
        mv = m.sb("mean_var", [P, T, 2])
        sm = m.sb("small", [P, 8, T])
        xn = m.sb("xn", [P, T, P])
        xr_now = m.sb("xr_now", [P, T, P])
        sq = m.sb("squares", [P, P])
        xnT = m.sb("xnT", [P, S])
        xlT = m.sb("xlT", [P, S])
        s_row = m.sb("s_row", [2, S])
        raw = m.sb("raw", [P, 2, S])
        tq = m.sb("tq", [P, 11, S])
        tk = m.sb("tk", [P, 11, T, P])
        vc = m.sb("vc", [P, T, P])
        kvm = m.sb("kvm", [P, 11, P])
        cT = m.sb("cT", [P, S])
        lq = m.sb("lq", [P, 4, S])
        lk = m.sb("lk", [P, 4, S])
        lv = m.sb("lv", [P, T, HL, HDL + 1])
        mx = m.sb("mx", [P, 8])
        mrest = m.sb("mrest", [P, 8])
        mpart = m.sb("mpart", [P, 3, 8], BF16)
        mT = m.sb("mT", [24, P], BF16)
        PT = m.sb("PT", [P, 2, S])
        rsum = m.sb("rsum", [P, 2, 4])
        o = m.sb("o", [P, 4, 2, HDL])
        oT = m.sb("oT", [P, 4, P])
        (dve_held, pool_held, dch, pch, ones_set, xn_made, turned, xnT_made, xlT_made, c_proj, s_proj, s_out, s_stored, raw_made, vc_made,
         tq1, tk1, tq_made, tk_made, kv_prod, kv_made, c_out, cT_made, lq_proj, lk_proj, lv_proj, lqk_made, lk_made, lv_made,
         scored, maxed, m_turned, mT_made, st_made, exped, pv_done, o_made, o_turned, oT_made, y_made, x_made) = (
            m.sem(n) for n in (
                "dve_held pool_held dch pch ones_set xn_made turned xnT_made xlT_made c_proj s_proj s_out s_stored raw_made vc_made "
                "tq1 tk1 tq_made tk_made kv_prod kv_made c_out cT_made lq_proj lk_proj lv_proj lqk_made lk_made lv_made "
                "scored maxed m_turned mT_made st_made exped pv_done o_made o_turned oT_made y_made x_made").split())
        block = ctx.enter_context(nc.Block())
        STEPS = [(n, n // 2, n - n // 2) for n in range(2, 11)]

        @block.sync
        def _(sp):
            for turns in (c_out, kv_prod, lv_proj, oT_made, o_made, pv_done, s_proj, s_stored, st_made, tk1, tq1, x_made, y_made):
                sp.sem_inc(turns, 1)
            with sp.Fori(0, B) as i:
                sp.wait_ge(s_out, i + 1)
                sp.dma_start(g.s_dram[:, bass.ds(i, 1), :], s_row[:].rearrange("r (a s) -> r a s", a=1)).then_inc(s_stored, 16)
            sp.wait_ge(s_stored, 16 * B + 1)

        @block.gpsimd
        def _(pool):
            pool.memset(tk[:, 0, :, :], 1.0).then_inc(ones_set, 1)
            pool.memset(tq[:, 0, :], 1.0).then_inc(ones_set, 1)
            pool.memset(lv[:], 1.0).then_inc(ones_set, 1)
            pool.wait_ge(ones_set, 3)
            with pool.Fori(0, B) as i:
                link = Chain(pool, pch, i, 22)
                pool.wait_ge(tk1, i + 2)
                pool.wait_ge(kv_prod, i * 3 + 1)
                x = tk[:, 1, :, :]
                for n, a, b in STEPS:
                    t = tk[:, n, :, :]
                    link(pool.tensor_tensor(t, tk[:, a, :, :], tk[:, b, :, :], ALU.mult), pool_held)
                    if n % 2 == 0:
                        link(pool.tensor_scalar(t, t, 2.0, -1.0, ALU.mult, ALU.add))
                    else:
                        link(pool.tensor_scalar(t, t, 2.0, 0.0, ALU.mult, ALU.add))
                        link(pool.tensor_tensor(t, t, x, ALU.subtract))
                pool.sem_inc(tk_made, 1)
                link.close()

        @block.tensor
        def _(pe):
            pe.wait_ge(ones_set, 3)
            with pe.Fori(0, B) as i:
                pe.wait_ge(xn_made, i * 2 + 2)
                for t in range(T):
                    pe.transpose(ps[:, 0, t * P:(t + 1) * P], xn[:, t, :], g.ident[:])
                for t in range(T):
                    ins = pe.transpose(ps[:, 1, t * P:(t + 1) * P], xr_now[:, t, :], g.ident[:])
                ins.then_inc(turned, 1)
                pe.wait_ge(xnT_made, i + 1)
                pe.wait_ge(oT_made, i * T + 1)
                pe.matmul(ps[:, 2, :], lhsT=g.wt[:, 4, :], rhs=xnT[:], start=True, stop=True)
                for t in range(T):
                    ins = pe.matmul(ps[:, 3 + t // 2, (t % 2) * 256:(t % 2) * 256 + 256], lhsT=xnT[:, t * P:(t + 1) * P],
                                    rhs=g.wt[:, 5:7, :], start=True, stop=True)
                ins.then_inc(c_proj, 1)
                pe.matmul(ps[0:2, 5, :], lhsT=g.tok[:], rhs=xnT[:], start=True, stop=True).then_inc(s_proj, 1)
                pe.wait_ge(xlT_made, i + 1)
                BK = (0, 1, 6, 7)
                pe.wait_ge(x_made, i + 1)
                for c in range(4):
                    ins = pe.matmul(ps[:, BK[c], :], lhsT=g.wql[:, c * P:(c + 1) * P], rhs=xlT[:], start=True, stop=True)
                ins.then_inc(lq_proj, 1)
                pe.wait_ge(lqk_made, i * 2 + 1)
                for c in range(4):
                    ins = pe.matmul(ps[:, BK[c], :], lhsT=g.wkvl[:, c * P:(c + 1) * P], rhs=xlT[:], start=True, stop=True)
                ins.then_inc(lk_proj, 1)
                pe.wait_ge(lqk_made, i * 2 + 2)
                for t in range(T):
                    ins = pe.matmul(ps[:, BK[t], :], lhsT=xlT[:, t * P:(t + 1) * P], rhs=g.wkvl[:, 512:1024],
                                    start=True, stop=True)
                ins.then_inc(lv_proj, 1)
                pe.wait_ge(tk_made, i + 1)
                pe.wait_ge(raw_made, i * 2 + 2)
                pe.wait_ge(vc_made, i + 1)
                for n in range(11):
                    for t in range(T):
                        ins = pe.matmul(ps[:, 2 + n // 4, (n % 4) * P:(n % 4 + 1) * P], lhsT=tk[:, n, t, :], rhs=vc[:, t, :],
                                        start=t == 0, stop=t == T - 1)
                    if n % 4 == 3 or n == 10:
                        ins.then_inc(kv_prod, 1)
                    if n == 7:
                        pe.wait_ge(s_out, i + 1)
                        pe.wait_ge(lv_made, i + 1)
                pe.wait_ge(kv_made, i * 3 + 3)
                pe.wait_ge(tq_made, i + 1)
                for n in range(11):
                    ins = pe.matmul(ps[:, 5, :], lhsT=kvm[:, n, :], rhs=tq[:, n, :], start=n == 0, stop=n == 10)
                ins.then_inc(c_out, 1)
                for w in range(T):
                    u = i * T + w
                    tok = slice(w * P, (w + 1) * P)
                    for h in range(HL):
                        c, par = divmod(h, 2)
                        rows = slice(64 * par, 64 * par + 64)
                        ins = pe.matmul(ps[:, par, c * P:(c + 1) * P], lhsT=lq[rows, c, tok], rhs=lk[rows, c, tok],
                                        start=True, stop=True)
                    ins.then_inc(scored, 1)
                    pe.wait_ge(maxed, u + 1)
                    pe.wait_ge(oT_made, u + 1)
                    pe.transpose(ps[:, 6, 0:64].bitcast(BF16)[0:24, 0:P], mpart[:], g.identb[:]).then_inc(m_turned, 1)
                    pe.wait_ge(mT_made, u + 1)
                    pe.wait_ge(kv_made, i * 3 + 3)
                    for h in range(HL):
                        c, par = divmod(h, 2)
                        rows = slice(64 * par, 64 * par + 64)
                        out = ps[:, 2 + par, c * P:(c + 1) * P]
                        pe.matmul(out, lhsT=lk[rows, c, tok], rhs=lq[rows, c, tok], start=True, stop=False)
                        ins = pe.matmul(out, lhsT=g.selm[:, par * 4 + c, :], rhs=mT[:], start=False, stop=True)
                    ins.then_inc(st_made, 1)
                    pe.wait_ge(exped, u + 1)
                    pe.wait_ge(cT_made, i + 1)
                    pe.wait_ge(o_made, u + 1)
                    for h in range(HL):
                        c, par = divmod(h, 2)
                        ins = pe.matmul(ps[:, 4 + par, c * (HDL + 1):(c + 1) * (HDL + 1)], lhsT=PT[:, par, c * P:(c + 1) * P],
                                        rhs=lv[:, w, h, :], start=True, stop=True)
                    ins.then_inc(pv_done, 1)
                    pe.wait_ge(o_made, u + 2)
                    for c in range(4):
                        ins = pe.transpose(ps[:, 6, c * P:(c + 1) * P], o[:, c, :, :], g.ident[:])
                    ins.then_inc(o_turned, 1)
                    pe.wait_ge(oT_made, u + 2)
                    out = ps[:, 7, w * P:(w + 1) * P]
                    pe.matmul(out, lhsT=cT[:, tok], rhs=g.wt[:, 7, :], start=True, stop=False)
                    for c in range(4):
                        ins = pe.matmul(out, lhsT=oT[:, c, :], rhs=g.wol[:, c, :], start=False, stop=c == 3)
                ins.then_inc(y_made, 1)

        @block.scalar
        def _(act):
            with act.Fori(0, B) as i:
                act.wait_ge(turned, i + 1)
                act.wait_ge(lv_proj, i + 1)
                act.wait_ge(s_proj, i + 1)
                act.copy(xnT[:], ps[:, 0, :]).then_inc(xnT_made, 1)
                act.activation(xlT[:], ps[:, 1, :], ACT.Identity, bias=0.0, scale=g.gl[:]).then_inc(xlT_made, 1)
                act.wait_ge(c_proj, i + 1)
                act.wait_ge(tq1, i + 1)
                act.wait_ge(tk1, i + 1)
                act.mul(raw[:, 0, :], ps[:, 2, :], HD0 ** -0.5).then_inc(raw_made, 1)
                kv = ps[:, 3:5, :].rearrange("p b (t s d) -> p (b t) s d", t=2, s=2)
                act.mul(raw[:, 1, :].rearrange("p (t d) -> p t d", t=T), kv[:, :, 0, :], HD0 ** -0.5).then_inc(raw_made, 1)
                act.wait_ge(kv_prod, i * 3 + 1)
                act.copy(vc[:], kv[:, :, 1, :]).then_inc(vc_made, 1)
                act.wait_ge(s_proj, i + 2)
                act.wait_ge(s_stored, i * 16 + 1)
                act.copy(s_row[:], ps[0:2, 5, :]).then_inc(s_out, 1)
                act.wait_ge(lq_proj, i + 1)
                act.wait_ge(st_made, i * T + 1)
                act.mul(lq[:, 0:2, :], ps[:, 0:2, :], HDL ** -0.5)
                act.mul(lq[:, 2:4, :], ps[:, 6:8, :], HDL ** -0.5).then_inc(lqk_made, 1)
                act.wait_ge(lk_proj, i + 1)
                act.copy(lk[:, 0:2, :], ps[:, 0:2, :])
                act.copy(lk[:, 2:4, :], ps[:, 6:8, :]).then_inc(lqk_made, 1)
                act.wait_ge(c_out, i + 2)
                act.wait_ge(y_made, i + 1)
                act.copy(cT[:], ps[:, 5, :]).then_inc(cT_made, 1)
                for w in range(T):
                    u = i * T + w
                    act.wait_ge(m_turned, u + 1)
                    act.wait_ge(st_made, u + 1)
                    act.copy(mT[:], ps[:, 6, 0:64].bitcast(BF16)[0:24, 0:P]).then_inc(mT_made, 1)
                    act.wait_ge(st_made, u + 2)
                    act.wait_ge(pv_done, u + 1)
                    act.activation(PT[:], ps[:, 2:4, :], ACT.Exp).then_inc(exped, 1)
                    act.wait_ge(o_turned, u + 1)
                    if w == 0:
                        act.wait_ge(y_made, i + 1)
                    act.copy(oT[:], ps[:, 6, :]).then_inc(oT_made, 1)

        @block.vector
        def _(dve):
            dve.wait_ge(ones_set, 3)
            with dve.Fori(0, B) as i:
                link = Chain(dve, dch, i, 76)
                x_b = g.xs[:, bass.ds(i * T, T), :]
                for t in range(T):
                    ins = dve.bn_stats(st[:, t, :], g.xs[:, bass.ds(i * T + t, 1), :])
                link(ins, dve_held)
                for t in range(T):
                    ins = dve.bn_aggr(mv[:, t, :], st[:, t, :])
                link(ins)
                link(dve.tensor_scalar(sm[:, 0, :], mv[:, :, 1], EPS, None, ALU.add))
                inv_sqrt(dve, link, sm[:, 0, :], sm[:, 1, :], sm[:, 2, :])
                for t in range(T):
                    ins = dve.tensor_scalar(xn[:, t, :], g.xs[:, bass.ds(i * T + t, 1), :], mv[:, t, 0:1],
                                            sm[:, 1, t:t + 1], ALU.subtract, ALU.mult)
                ins.then_inc(xn_made, 1)
                dve.wait_ge(xn_made, i * 2 + 1)
                for t in range(T):
                    link(dve.tensor_tensor_reduce(sq[:], xn[:, t, :], xn[:, t, :], 1.0, 0.0, ALU.mult, ALU.add, sm[:, 3, t:t + 1]))
                link(dve.tensor_scalar(sm[:, 3, :], sm[:, 3, :], 1e-24, None, ALU.max))
                inv_sqrt(dve, link, sm[:, 3, :], sm[:, 4, :], sm[:, 5, :])
                link(dve.tensor_scalar(sm[:, 4, :], sm[:, 4, :], float(D) ** 0.5, None, ALU.mult))
                for t in range(T):
                    ins = dve.tensor_scalar(xr_now[:, t, :], xn[:, t, :], sm[:, 4, t:t + 1], None, ALU.mult)
                ins.then_inc(xn_made, 1)
                dve.wait_ge(xn_made, i * 2 + 2)
                link(dve.tensor_copy(g.xr[:, bass.ds(i * T, T), :], xr_now[:]))
                dve.wait_ge(raw_made, i * 2 + 2)
                dve.wait_ge(kv_prod, i * 3 + 1)
                dve.wait_ge(c_out, i + 1)
                tk_x = tk[:, 1, :, :].rearrange("p t d -> p (t d)")
                dve.tensor_scalar(tk_x, raw[:, 1, :], 1.0, -1.0, ALU.min, ALU.max).then_inc(tk1, 1)
                dve.tensor_scalar(tq[:, 1, :], raw[:, 0, :], 1.0, -1.0, ALU.min, ALU.max).then_inc(tq1, 1)
                dve.wait_ge(tq1, i + 2)
                for n, a, b in STEPS:
                    link(dve.scalar_tensor_tensor(tq[:, n, :], tq[:, a, :], 2.0, tq[:, b, :], ALU.mult, ALU.mult))
                    if n % 2 == 0:
                        link(dve.tensor_scalar(tq[:, n, :], tq[:, n, :], -1.0, None, ALU.add))
                    else:
                        link(dve.tensor_tensor(tq[:, n, :], tq[:, n, :], tq[:, 1, :], ALU.subtract))
                dve.sem_inc(tq_made, 1)
                dve.wait_ge(lv_proj, i + 2)
                dve.wait_ge(pv_done, i * T + 1)
                for t in range(T):
                    bank = (0, 1, 6, 7)[t]
                    ins = dve.tensor_copy(lv[:, t, :, 0:HDL], ps[:, bank, :].rearrange("p (h d) -> p h d", h=HL))
                ins.then_inc(lv_made, 1)
                for j in range(3):
                    n = 4 if j < 2 else 3
                    dve.wait_ge(kv_prod, i * 3 + j + 2)
                    dve.tensor_tensor(kvm[:, 4 * j:4 * j + n, :],
                                      ps[:, 2 + j, 0:n * P].rearrange("p (n d) -> p n d", n=n),
                                      g.mbeta[:, 4 * j:4 * j + n, :], ALU.mult).then_inc(kv_made, 1)
                for w in range(T):
                    u = i * T + w
                    dve.wait_ge(scored, u + 1)
                    link(dve.tensor_reduce(mx[:], ps[:, 0:2, :].rearrange("p b (c k) -> p (b c) k", c=4), AX.X, ALU.max))
                    link(dve.tensor_copy(mpart[:, 0, :], mx[:]))
                    link(dve.tensor_tensor(mrest[:], mx[:], mpart[:, 0, :], ALU.subtract))
                    link(dve.tensor_copy(mpart[:, 1, :], mrest[:]))
                    dve.tensor_tensor(mpart[:, 2, :], mrest[:], mpart[:, 1, :], ALU.subtract).then_inc(maxed, 1)
                    dve.wait_ge(pv_done, u + 2)
                    O = ps[:, 4:6, 0:4 * (HDL + 1)].rearrange("p b (c d) -> p b c d", c=4)
                    link(dve.reciprocal(rsum[:], O[:, :, :, HDL]))
                    for par in range(2):
                        ins = dve.tensor_tensor(o[:, :, par, :], O[:, par, :, 0:HDL],
                                                rsum[:, par, :].rearrange("p (c a) -> p c a", a=1).to_broadcast([P, 4, HDL]),
                                                ALU.mult)
                    ins.then_inc(o_made, 1)
                dve.wait_ge(y_made, i + 2)
                dve.tensor_tensor(x_b, ps[:, 7, :].rearrange("p (t d) -> p t d", t=T), x_b, ALU.add).then_inc(x_made, 1)
                link.close()
            dve.wait_ge(x_made, B + 1)



KEEP = (256, 128)
FETCH = tuple(min(k * 9.0 / 8.0, S) for k in KEEP)
N_ITERS = 50
OUTER, INNER = 7, 7
CAP = 80.0
ROUTES = 2 * B


def routing(nc, g):
    with ExitStack() as ctx:
        m = Mem(nc, ctx, "rt_")
        ps = g.ps
        s = m.sb("s", [P, 64])
        E = m.sb("E", [P, 64])
        low = m.sb("low", [P, 64])
        part = m.sb("part", [P, 1])
        col = m.sb("col", [P, 8])
        cols_i = m.sb("cols_i", [P, 2], I32)
        row = m.sb("row", [1, P])
        rmax = m.sb("rmax", [1, ROUTES])
        kblk = m.sb("kblk", [P, P])
        sc = m.sb("sc", [ROUTES, S])
        work = m.sb("work", [ROUTES, S])
        work2 = m.sb("work2", [ROUTES, S])
        top = m.sb("top", [ROUTES, 8])
        picked = m.sb("picked", [ROUTES, S])
        count = m.sb("count", [ROUTES, S])
        ones = m.sb("ones", [ROUTES, S])
        kept = m.sb("kept", [ROUTES, S])
        (loaded, dch, dch_loop, dch_end, maxed, max_turned, row_made, max_spread, r_made, exped, summed, parted, score_made, score_out,
         score_in, pos_made, pos_turned, ones_set) = (m.sem(n) for n in (
            "loaded dch dch_loop dch_end maxed max_turned row_made max_spread r_made exped summed parted score_made score_out "
            "score_in pos_made pos_turned ones_set").split())
        NA, NA1, C, NEG_R, RC, MX = range(6)
        block = ctx.enter_context(nc.Block())

        @block.sync
        def _(sp):
            for turns in (summed,):
                sp.sem_inc(turns, 1)
            sp.dma_start(s[:], g.s_dram.rearrange("r b (e n) -> (r b e) n", e=8)).then_inc(loaded, 16)
            sp.wait_ge(score_made, 1)
            sp.dma_start(g.sc_dram.rearrange("r (e n) -> (r e) n", e=8), E[:]).then_inc(score_out, 16)
            sp.wait_ge(score_out, 16)
            sp.dma_start(sc[:], g.sc_dram).then_inc(score_in, 16)

        @block.gpsimd
        def _(pool):
            pool.memset(ones[:], 1.0).then_inc(ones_set, 1)

        @block.tensor
        def _(pe):
            pe.wait_ge(maxed, 1)
            pe.transpose(ps[0:1, 0, 0:P], col[:, MX:MX + 1], g.ident[:]).then_inc(max_turned, 1)
            pe.wait_ge(row_made, 1)
            pe.matmul(ps[:, 1, 0:1], lhsT=row[:], rhs=g.ones[0:1, 0:1], start=True, stop=True).then_inc(max_spread, 1)
            with pe.Fori(0, OUTER) as i:
                for j in range(INNER):
                    pe.wait_ge(parted, i * INNER + j + 1)
                    pe.matmul(ps[:, 2, 0:1], lhsT=kblk[:], rhs=part[:], start=True, stop=True).then_inc(summed, 1)
            pe.wait_ge(pos_made, 2)
            for t in range(T):
                pe.transpose(ps[:, 3, t * ROUTES:(t + 1) * ROUTES], count[:, t * P:(t + 1) * P],
                             g.ident[0:ROUTES, 0:ROUTES])
                ins = pe.transpose(ps[:, 4, t * ROUTES:(t + 1) * ROUTES], kept[:, t * P:(t + 1) * P],
                                   g.ident[0:ROUTES, 0:ROUTES])
            ins.then_inc(pos_turned, 1)

        @block.scalar
        def _(act):
            act.wait_ge(r_made, 1)
            act.activation(col[:, C:C + 1], col[:, NA:NA + 1], ACT.Exp)
            act.activation(E[:], low[:], ACT.Exp).then_inc(exped, 1)
            with act.Fori(0, OUTER) as i:
                act.wait_ge(r_made, i + 2)
                act.activation(E[:], low[:], ACT.Exp).then_inc(exped, 1)

        @block.vector
        def _(dve):
            link = Chain(dve, dch)
            half = P // 2
            for rows, k in ((slice(0, half), FETCH[0]), (slice(half, P), FETCH[1])):
                dve.memset(col[rows, NA1:NA1 + 1], math.log(S) - math.log(k))
                link(dve.tensor_scalar(kblk[rows, :], g.blk[rows, :], 1.0 / k, None, ALU.mult))
            dve.wait_ge(loaded, 16)
            dve.tensor_reduce(col[:, MX:MX + 1], s[:], AX.X, ALU.max).then_inc(maxed, 1)
            dve.wait_ge(max_turned, 1)
            link(dve.tensor_reduce(rmax[:], ps[0:1, 0, 0:P].rearrange("p (r e) -> p r e", e=8), AX.X, ALU.max))
            dve.tensor_copy(row[:].rearrange("p (r e) -> p r e", e=8),
                            rmax[:].rearrange("p (r a) -> p r a", a=1).to_broadcast([1, ROUTES, 8])).then_inc(row_made, 1)
            dve.wait_ge(max_spread, 1)
            neg_r = col[:, NEG_R:NEG_R + 1]
            link(dve.tensor_scalar(neg_r, ps[:, 1, 0:1], col[:, NA1:NA1 + 1], -1.0, ALU.min, ALU.mult))
            dve.tensor_scalar(col[:, NA:NA + 1], col[:, NA1:NA1 + 1], neg_r, CAP, ALU.add, ALU.min)
            dve.tensor_scalar(low[:], s[:], neg_r, CAP, ALU.add, ALU.min).then_inc(r_made, 1)
            dve.wait_ge(exped, 1)
            with dve.Fori(0, OUTER) as i:
                link = Chain(dve, dch_loop, i, 4)
                for j in range(INNER):
                    if j == 0:
                        dve.wait_ge(exped, i + 1)
                        c = col[:, C:C + 1]
                    else:
                        dve.wait_ge(summed, i * INNER + j + 1)
                        c = ps[:, 2, 0:1]
                    dve.tensor_scalar(low[:], E[:], c, 0.0, ALU.min, ALU.add, accum_out=part[:]).then_inc(parted, 1)
                dve.wait_ge(summed, i * INNER + INNER + 1)
                link(dve.tensor_copy(col[:, RC:RC + 1], ps[:, 2, 0:1]))
                bits = col[:, RC:RC + 1].bitcast(I32)
                dve.tensor_scalar(cols_i[:, 0:1], bits, 23, None, ALU.logical_shift_right)
                link(dve.tensor_scalar(col[:, C:C + 1].bitcast(I32), bits, 0x7FFFFF, 0x3F800000, ALU.bitwise_and,
                                       ALU.bitwise_or))
                link(dve.tensor_scalar(col[:, NA:NA + 1], cols_i[:, 0:1], 127.0, math.log(2.0), ALU.subtract, ALU.mult))
                link(dve.tensor_tensor(neg_r, neg_r, col[:, NA:NA + 1], ALU.subtract))
                dve.tensor_scalar(low[:], s[:], neg_r, CAP, ALU.add, ALU.min).then_inc(r_made, 1)
            link = Chain(dve, dch_end)
            link(dve.reciprocal(col[:, RC:RC + 1], col[:, C:C + 1]))
            dve.wait_ge(exped, OUTER + 1)
            dve.tensor_scalar(E[:], E[:], col[:, RC:RC + 1], 1.0, ALU.mult, ALU.min).then_inc(score_made, 1)
            dve.wait_ge(score_in, 16)
            src = sc
            for k in range(KEEP[0] // 8):
                rows = slice(0, ROUTES) if k < KEEP[1] // 8 else slice(0, B)
                link(dve.max(top[rows, :], src[rows, :]))
                link(dve.match_replace(work[rows, :], top[rows, :], src[rows, :], -1.0))
                src = work
            link(dve.tensor_scalar(picked[:], work[:], 0.0, None, ALU.is_lt))
            dve.wait_ge(ones_set, 1)
            link(dve.tensor_tensor_scan(count[:], ones[:], picked[:], 0.0, ALU.mult, ALU.add))
            link(dve.tensor_tensor(count[:], count[:], picked[:], ALU.mult))
            dve.tensor_scalar(count[:], count[:], -1.0, None, ALU.add).then_inc(pos_made, 1)
            link(dve.tensor_scalar(kept[:], sc[:], -1.0, 1.0, ALU.mult, ALU.add))
            dve.tensor_tensor(kept[:], kept[:], sc[:], ALU.add).then_inc(pos_made, 1)
            dve.wait_ge(pos_turned, 1)
            link(dve.tensor_copy(g.place[:], ps[:, 3, 0:T * ROUTES].rearrange("p (t r) -> p t r", t=T)))
            link(dve.tensor_copy(g.weight[:], ps[:, 4, 0:T * ROUTES].rearrange("p (t r) -> p t r", t=T)))


def heavy(nc, g, out):
    HL, HDL = 8, 64
    NK, NQ = KEEP
    KT = NK // P
    with ExitStack() as ctx:
        m = Mem(nc, ctx, "hv_")
        ps = g.ps
        pick = m.sb("pick", [P, T, NK + NQ])
        xg = m.sb("xg", [P, NK + NQ])
        wk = m.sb("wk", [P, KT])
        xgT = m.sb("xgT", [P, NK + NQ])
        q = m.sb("q", [P, 4, NQ])
        k = m.sb("k", [P, 4, NK])
        v = m.sb("v", [P, KT, HL, HDL + 1])
        mx = m.sb("mx", [P, 8])
        mrest = m.sb("mrest", [P, 8])
        mpart = m.sb("mpart", [P, 3, 8], BF16)
        mT = m.sb("mT", [24, P], BF16)
        PT = m.sb("PT", [P, 2, KT, S])
        rsum = m.sb("rsum", [P, 2, 4])
        o = m.sb("o", [P, 4, 2, HDL])
        oT = m.sb("oT", [P, 4, P])
        y = m.sb("y", [P, P])
        pickT = m.sb("pickT", [P, S])
        (dch, ones_set, picked, gathered, xg_made, xg_turned, xgT_made, projected, qkv_made, scored, maxed, m_turned,
         mT_made, st_made, exped, pv_done, o_made, o_turned, oT_made, y_done, y_made, scattered, x_made, stored) = (
            m.sem(n) for n in (
                "dch ones_set picked gathered xg_made xg_turned xgT_made projected qkv_made scored maxed m_turned "
                "mT_made st_made exped pv_done o_made o_turned oT_made y_done y_made scattered x_made stored").split())
        block = ctx.enter_context(nc.Block())

        @block.sync
        def _(sp):
            for turns in (x_made, xg_turned):
                sp.sem_inc(turns, 1)
            with sp.Fori(0, B) as i:
                sp.wait_ge(x_made, i + 2)
                sp.dma_start(out[bass.ds(i, 1)].rearrange("b (t p) d -> p (b t) d", p=P),
                             g.xs[:, bass.ds(i * T, T), :]).then_inc(stored, 16)
            sp.wait_ge(stored, 16 * B)

        @block.tensor
        def _(pe):
            with pe.Fori(0, B) as i:
                pe.wait_ge(picked, i + 1)
                pe.wait_ge(x_made, i + 1)
                for j in range(KT + 1):
                    for t in range(T):
                        pe.matmul(ps[:, 0, j * P:(j + 1) * P], lhsT=pick[:, t, j * P:(j + 1) * P],
                                  rhs=g.xr[:, bass.ds(i * T + t, 1), :], start=t == 0, stop=t == T - 1)
                for j in range(KT):
                    for t in range(T):
                        ins = pe.matmul(ps[:, 1, j:j + 1], lhsT=pick[:, t, j * P:(j + 1) * P],
                                        rhs=g.weight[:, t, bass.ds(i, 1)], start=t == 0, stop=t == T - 1)
                ins.then_inc(gathered, 1)
                pe.wait_ge(xg_made, i + 1)
                for j in range(KT + 1):
                    pe.transpose(ps[:, 2, j * P:(j + 1) * P], xg[:, j * P:(j + 1) * P], g.ident[:])
                for t in range(T):
                    ins = pe.transpose(ps[:, 7, t * P:(t + 1) * P], pick[:, t, NK:NK + NQ], g.ident[:])
                ins.then_inc(xg_turned, 1)
                pe.wait_ge(xgT_made, i + 1)
                for c in range(4):
                    pe.matmul(ps[:, 3, c * NQ:(c + 1) * NQ], lhsT=g.wqh[:, c * P:(c + 1) * P], rhs=xgT[:, NK:NK + NQ],
                              start=True, stop=True)
                for c in range(4):
                    pe.matmul(ps[:, c // 2, (c % 2) * NK:(c % 2 + 1) * NK], lhsT=g.wkh[:, c * P:(c + 1) * P],
                              rhs=xgT[:, 0:NK], start=True, stop=True)
                for j in range(KT):
                    ins = pe.matmul(ps[:, 4 + j, :], lhsT=xgT[:, j * P:(j + 1) * P], rhs=g.wvh[:], start=True, stop=True)
                ins.then_inc(projected, 1)
                pe.wait_ge(qkv_made, i * 3 + 3)
                for h in range(HL):
                    c, par = divmod(h, 2)
                    rows = slice(64 * par, 64 * par + 64)
                    ins = pe.matmul(ps[:, 2 * par + c // 2, (c % 2) * NK:(c % 2 + 1) * NK], lhsT=q[rows, c, :],
                                    rhs=k[rows, c, :], start=True, stop=True)
                ins.then_inc(scored, 1)
                pe.wait_ge(maxed, i + 1)
                pe.transpose(ps[:, 6, 0:64].bitcast(BF16)[0:24, 0:P], mpart[:], g.identb[:]).then_inc(m_turned, 1)
                pe.wait_ge(mT_made, i + 1)
                for j in range(KT):
                    for h in range(HL):
                        c, par = divmod(h, 2)
                        rows = slice(64 * par, 64 * par + 64)
                        dst = ps[:, 2 * par + j, c * P:(c + 1) * P]
                        pe.matmul(dst, lhsT=k[rows, c, j * P:(j + 1) * P], rhs=q[rows, c, :], start=True, stop=False)
                        ins = pe.matmul(dst, lhsT=g.selm[:, par * 4 + c, :], rhs=mT[:], start=False, stop=True)
                ins.then_inc(st_made, 1)
                pe.wait_ge(exped, i + 1)
                for h in range(HL):
                    c, par = divmod(h, 2)
                    for j in range(KT):
                        ins = pe.matmul(ps[:, 4 + par, c * (HDL + 1):(c + 1) * (HDL + 1)],
                                        lhsT=PT[:, par, j, c * P:(c + 1) * P], rhs=v[:, j, h, :],
                                        start=j == 0, stop=j == KT - 1)
                ins.then_inc(pv_done, 1)
                pe.wait_ge(o_made, i + 1)
                for c in range(4):
                    ins = pe.transpose(ps[:, 6, c * P:(c + 1) * P], o[:, c, :, :], g.ident[:])
                ins.then_inc(o_turned, 1)
                pe.wait_ge(oT_made, i + 1)
                for c in range(4):
                    ins = pe.matmul(ps[:, 0, 0:P], lhsT=oT[:, c, :], rhs=g.woh[:, c, :], start=c == 0, stop=c == 3)
                ins.then_inc(y_done, 1)
                pe.wait_ge(y_made, i + 1)
                for t in range(T):
                    ins = pe.matmul(ps[:, 1, t * P:(t + 1) * P], lhsT=pickT[:, t * P:(t + 1) * P], rhs=y[:],
                                    start=True, stop=True)
                ins.then_inc(scattered, 1)

        @block.scalar
        def _(act):
            with act.Fori(0, B) as i:
                act.wait_ge(gathered, i + 1)
                act.copy(wk[:], ps[:, 1, 0:KT])
                act.copy(xg[:], ps[:, 0, 0:NK + NQ]).then_inc(xg_made, 1)
                act.wait_ge(xg_turned, i + 2)
                act.activation(xgT[:], ps[:, 2, 0:NK + NQ], ACT.Identity, bias=0.0, scale=g.gh[:]).then_inc(xgT_made, 1)
                act.copy(pickT[:], ps[:, 7, :])
                act.wait_ge(projected, i + 1)
                act.mul(q[:], ps[:, 3, :].rearrange("p (c n) -> p c n", c=4), HDL ** -0.5).then_inc(qkv_made, 1)
                act.copy(k[:], ps[:, 0:2, :].rearrange("p b (c n) -> p (b c) n", c=2)).then_inc(qkv_made, 1)
                act.wait_ge(m_turned, i + 1)
                act.copy(mT[:], ps[:, 6, 0:64].bitcast(BF16)[0:24, 0:P]).then_inc(mT_made, 1)
                act.wait_ge(st_made, i + 1)
                act.activation(PT[:], ps[:, 0:4, :].rearrange("p (a j) n -> p a j n", a=2), ACT.Exp).then_inc(exped, 1)
                act.wait_ge(o_turned, i + 1)
                act.copy(oT[:], ps[:, 6, :]).then_inc(oT_made, 1)
                act.wait_ge(y_done, i + 1)
                act.copy(y[:], ps[:, 0, 0:P]).then_inc(y_made, 1)

        @block.vector
        def _(dve):
            link = Chain(dve, ones_set)
            link(dve.memset(v[:], 1.0))
            with dve.Fori(0, B) as i:
                link = Chain(dve, dch, i, 5)
                dve.wait_ge(xg_turned, i + 1)
                for t in range(T):
                    dve.tensor_scalar(pick[:, t, 0:NK], g.iota[:], g.place[:, t, bass.ds(i, 1)], None, ALU.is_equal)
                    ins = dve.tensor_scalar(pick[:, t, NK:NK + NQ], g.iota[:, 0:NQ], g.place[:, t, bass.ds(i + B, 1)],
                                            None, ALU.is_equal)
                ins.then_inc(picked, 1)
                dve.wait_ge(projected, i + 1)
                dve.wait_ge(xg_made, i + 1)
                for j in range(KT):
                    ins = dve.tensor_scalar(v[:, j, :, 0:HDL], ps[:, 4 + j, :].rearrange("p (h d) -> p h d", h=HL),
                                            wk[:, j:j + 1], None, ALU.mult)
                ins.then_inc(qkv_made, 1)
                dve.wait_ge(scored, i + 1)
                link(dve.tensor_reduce(mx[:], ps[:, 0:4, :].rearrange("p b (c k) -> p (b c) k", c=2), AX.X, ALU.max))
                link(dve.tensor_copy(mpart[:, 0, :], mx[:]))
                link(dve.tensor_tensor(mrest[:], mx[:], mpart[:, 0, :], ALU.subtract))
                link(dve.tensor_copy(mpart[:, 1, :], mrest[:]))
                dve.tensor_tensor(mpart[:, 2, :], mrest[:], mpart[:, 1, :], ALU.subtract).then_inc(maxed, 1)
                dve.wait_ge(pv_done, i + 1)
                O = ps[:, 4:6, 0:4 * (HDL + 1)].rearrange("p b (c d) -> p b c d", c=4)
                link(dve.reciprocal(rsum[:], O[:, :, :, HDL]))
                for par in range(2):
                    ins = dve.tensor_tensor(o[:, :, par, :], O[:, par, :, 0:HDL],
                                            rsum[:, par, :].rearrange("p (c a) -> p c a", a=1).to_broadcast([P, 4, HDL]),
                                            ALU.mult)
                ins.then_inc(o_made, 1)
                dve.wait_ge(scattered, i + 1)
                for t in range(T):
                    x_t = g.xs[:, bass.ds(i * T + t, 1), :]
                    ins = dve.scalar_tensor_tensor(x_t, ps[:, 1, t * P:(t + 1) * P].rearrange("p (a d) -> p a d", a=1),
                                                   g.weight[:, t, bass.ds(i + B, 1)], x_t, ALU.mult, ALU.add)
                ins.then_inc(x_made, 1)
                link.close()
            dve.wait_ge(x_made, B + 1)


class Shared:

    def __init__(self, nc, ctx):
        m = Mem(nc, ctx)
        self.ps = ctx.enter_context(nc.psum_tensor("ps", [P, 8, 512], F32))
        self.xs = m.sb("xs", [P, B * T, P])
        self.ident = m.sb("ident", [P, P])
        self.identb = m.sb("identb", [P, P], BF16)
        self.maskb = m.sb("maskb", [P, 2, P], BF16)
        self.ones = m.sb("ones", [P, P])
        self.blk = m.sb("blk", [P, P])
        self.iota = m.sb("iota", [P, 256])
        self.selm = m.sb("selm", [24, 8, P], BF16)
        self.mbeta = m.sb("mbeta", [P, 11, P])
        self.wt = m.sb("wt", [P, 8, P])
        self.wkh, self.wvh = m.sb("wkh", [P, 512]), m.sb("wvh", [P, 512])
        self.ws1, self.ws2, self.wr = m.sb("ws1", [P, 64]), m.sb("ws2", [64, P]), m.sb("wr", [P, 8])
        self.w1, self.w2 = m.sb("w1", [P, 8, 64]), m.sb("w2", [P, 4, P])
        self.bqkv, self.bv, self.bo = m.sb("bqkv", [P, 3]), m.sb("bv", [P, P]), m.sb("bo", [P, P])
        self.gl, self.gh, self.tok = m.sb("gl", [P, 1]), m.sb("gh", [P, 1]), m.sb("tok", [P, 2])
        self.wql, self.wkvl, self.wol = m.sb("wql", [P, 512]), m.sb("wkvl", [P, 1024]), m.sb("wol", [P, 4, P])
        self.wqh, self.woh = m.sb("wqh", [P, 512]), m.sb("woh", [P, 4, P])
        self.logits = m.sb("logits", [P, B * T, 8])
        self.gate = m.sb("gate", [P, B * T, 8])
        self.any_gate = m.sb("any_gate", [P, 1], I32)
        self.xnT_all = m.sb("kept_x", [P, B * S])
        self.xr = self.xnT_all[:].rearrange("p (n d) -> p n d", d=D)
        self.place = m.sb("place", [P, T, 2 * B])
        self.weight = m.sb("weight", [P, T, 2 * B])
        self.s_dram = nc.dram_tensor("s_dram", [2, B, S], F32).ap()
        self.sc_dram = nc.dram_tensor("sc_dram", [2 * B, S], F32).ap()


def build(nc, w, out):
    with ExitStack() as ctx:
        g = Shared(nc, ctx)
        setup(nc, g, w)
        layer0(nc, g, w)
        gates(nc, g)
        routed_experts(nc, g)
        layer1(nc, g)
        routing(nc, g)
        heavy(nc, g, out)


_INS = ['L0_attn_x', 'L0_attn_w_qkv', 'L0_attn_b_qkv', 'L0_attn_w_out', 'L0_attn_b_out', 'L0_ffn_Ws1', 'L0_ffn_Ws2',
        'L0_ffn_W1', 'L0_ffn_W2', 'L0_ffn_Wr', 'L1_attn_w_in', 'L1_attn_w_out', 'L1_attn_beta', 'L1_ffn_gamma_light',
        'L1_ffn_wq_light', 'L1_ffn_wkv_light', 'L1_ffn_wo_light', 'L1_ffn_q_routing_token',
        'L1_ffn_kv_routing_token', 'L1_ffn_gamma_heavy', 'L1_ffn_wq_heavy', 'L1_ffn_wkv_heavy', 'L1_ffn_wo_heavy']


def kernel(**inputs):
    import numpy as _np
    import concourse.bacc as _bacc
    from concourse.bass_utils import run_bass_kernel_spmd as _run

    nc = _bacc.Bacc("TRN2", target_bir_lowering=False, num_devices=1)
    arrays, args = {}, {}
    for name in _INS:
        a = _np.ascontiguousarray(inputs[name])
        arrays[f"in_{name}_dram"] = a
        args[name] = nc.dram_tensor(f"in_{name}_dram", a.shape, mybir.dt.from_np(a.dtype), kind="ExternalInput").ap()
    out = nc.dram_tensor("out_0_dram", (B, S, D), F32, kind="ExternalOutput").ap()
    build(nc, args, out)
    r = _run(nc, [arrays], core_ids=[0])
    return r.results[0]["out_0_dram"]
```

```python
import math
from contextlib import ExitStack

import concourse.bass as bass
from concourse import mybir
from concourse.alu_op_type import AluOpType as ALU

ACT = mybir.ActivationFunctionType
F32 = mybir.dt.float32
BF16 = mybir.dt.bfloat16
I32 = mybir.dt.int32
AX = mybir.AxisListType

P = 128
B, S, D = 8, 512, 128
T = S // P
H0, HD0 = 16, 8
NEG = -1e30
EPS = 1e-5

Q_PART = (0, 0, 1, 1, 0, 2)
K_PART = (0, 1, 0, 1, 2, 0)
ROW_POS = HD0 * len(Q_PART)
ROW_MAX = ROW_POS + 1
ROWS = ROW_MAX + 3


class Chain:

    def __init__(self, eng, sem, turn=0, per=0):
        self.eng, self.sem, self.base, self.per, self.n = eng, sem, turn * per, per, 0

    def __call__(self, ins, held=None):
        self.n += 1
        ins.then_inc(self.sem, 1)
        self.eng.wait_ge(self.sem, self.base + self.n)
        if held is not None:
            self.eng.sem_inc(held, 1)

    def close(self):
        assert self.per in (0, self.n), (self.per, self.n)


def inv_sqrt(dve, link, v, y, t, steps=4):
    link(dve.tensor_scalar(y.bitcast(I32), v.bitcast(I32), 1, None, ALU.logical_shift_right))
    link(dve.tensor_scalar(y.bitcast(I32), y.bitcast(I32), -1.0, float(0x5F3759DF), ALU.mult, ALU.add))
    for _ in range(steps):
        link(dve.tensor_tensor(t, y, y, ALU.mult))
        link(dve.scalar_tensor_tensor(t, t, -0.5, v, ALU.mult, ALU.mult))
        link(dve.scalar_tensor_tensor(y, t, 1.5, y, ALU.add, ALU.mult))


class Mem:

    def __init__(self, nc, ctx, phase=""):
        self.nc, self.ctx, self.phase = nc, ctx, phase

    def sb(self, name, shape, dt=F32):
        return self.ctx.enter_context(self.nc.sbuf_tensor(self.phase + name, shape, dt))

    def sem(self, name):
        return self.ctx.enter_context(self.nc.semaphore(self.phase + name))


def setup(nc, g, w):
    with ExitStack() as ctx:
        m = Mem(nc, ctx)
        nat = m.sb("nat", [P, 16, P])
        loaded, w_loaded, ident_made, ident_b, turned, moved, made, beta_ld, mb = (m.sem(n) for n in (
            "loaded", "w_loaded", "ident_made", "ident_b", "turned", "moved", "made", "beta_ld", "mb"))
        betac = m.sb("betac", [P, 11])
        block = ctx.enter_context(nc.Block())
        ps = g.ps

        @block.sync
        def _(sp):
            with nc.allow_non_contiguous_dma(reason="columns of small vectors"):
                sp.dma_start(nat[:, 0:3, :], w["L0_attn_w_qkv"].rearrange("(c p) d -> p c d", p=P)).then_inc(w_loaded, 16)
                sp.dma_start(nat[:, 3, :], w["L0_attn_w_out"]).then_inc(w_loaded, 16)
                sp.dma_start(nat[:, 4:7, :], w["L1_attn_w_in"].rearrange("(c p) d -> p c d", p=P)).then_inc(w_loaded, 16)
                sp.dma_start(nat[:, 7, :], w["L1_attn_w_out"]).then_inc(w_loaded, 16)
                sp.dma_start(nat[:, 8:16, :], w["L1_ffn_wkv_heavy"].rearrange("(c p) d -> p c d", p=P)).then_inc(w_loaded, 16)
                n = 0
                for dst, src in (
                    (g.xs[:], w["L0_attn_x"].rearrange("b (t p) d -> p (b t) d", p=P)),
                    (g.ws1[:], w["L0_ffn_Ws1"]), (g.ws2[:], w["L0_ffn_Ws2"]), (g.wr[:], w["L0_ffn_Wr"]),
                    (g.w1[:], w["L0_ffn_W1"].rearrange("e d f -> d e f")),
                    (g.w2[:], w["L0_ffn_W2"].rearrange("(c e) f d -> (e f) c d", e=2)),
                    (g.bqkv[:], w["L0_attn_b_qkv"].rearrange("(c p) -> p c", p=P)),
                    (g.bv[:], w["L0_attn_b_qkv"][2 * P:3 * P].rearrange("(a d) -> a d", a=1).to_broadcast([P, P])),
                    (g.bo[:], w["L0_attn_b_out"].rearrange("(a d) -> a d", a=1).to_broadcast([P, P])),
                    (g.gl[:], w["L1_ffn_gamma_light"].rearrange("(p a) -> p a", a=1)),
                    (g.gh[:], w["L1_ffn_gamma_heavy"].rearrange("(p a) -> p a", a=1)),
                    (g.tok[:, 0:1], w["L1_ffn_kv_routing_token"].rearrange("(p a) -> p a", a=1)),
                    (g.tok[:, 1:2], w["L1_ffn_q_routing_token"].rearrange("(p a) -> p a", a=1)),
                    (g.wql[:], w["L1_ffn_wq_light"]), (g.wkvl[:], w["L1_ffn_wkv_light"]),
                    (g.wol[:], w["L1_ffn_wo_light"].rearrange("(c p) d -> p c d", p=P)),
                    (g.wqh[:], w["L1_ffn_wq_heavy"]),
                    (g.woh[:], w["L1_ffn_wo_heavy"].rearrange("(c p) d -> p c d", p=P)),
                ):
                    sp.dma_start(dst, src).then_inc(loaded, 16)
                    n += 1
                for h in range(H0):
                    sp.dma_start(betac[HD0 * h:HD0 * h + HD0, :],
                                 w["L1_attn_beta"][h:h + 1, :].to_broadcast([HD0, 11])).then_inc(beta_ld, 16)
            sp.wait_ge(loaded, 16 * n)

        @block.gpsimd
        def _(pool):
            pool.memset(g.ident[:], 1.0).then_inc(made, 1)
            pool.memset(g.maskb[:], 0.0).then_inc(made, 1)
            pool.memset(g.ones[:], 1.0).then_inc(made, 1)
            pool.memset(g.blk[:], 1.0).then_inc(made, 1)
            pool.wait_ge(made, 4)
            pool.affine_select(out=g.ident[:], in_=g.ident[:], compare_op=ALU.is_equal, fill=0.0, base=0,
                               pattern=[[-1, P]], channel_multiplier=1).then_inc(ident_made, 1)
            pool.affine_select(out=g.maskb[:, 0, :], in_=g.maskb[:, 0, :], compare_op=ALU.is_ge, fill=NEG, base=0,
                               pattern=[[-1, P]], channel_multiplier=1).then_inc(made, 1)
            pool.affine_select(out=g.maskb[:, 1, :], in_=g.maskb[:, 1, :], compare_op=ALU.is_ge, fill=NEG, base=0,
                               pattern=[[1, P]], channel_multiplier=-1).then_inc(made, 1)
            pool.affine_select(out=g.blk[:], in_=g.blk[:], compare_op=ALU.is_ge, fill=0.0, base=0,
                               pattern=[[-HD0, H0], [0, HD0]], channel_multiplier=1).then_inc(made, 1)
            pool.wait_ge(made, 7)
            pool.affine_select(out=g.blk[:], in_=g.blk[:], compare_op=ALU.is_ge, fill=0.0, base=HD0 - 1,
                               pattern=[[HD0, H0], [0, HD0]], channel_multiplier=-1).then_inc(made, 1)
            pool.iota(g.iota[:], pattern=[[1, 256]], base=0, channel_multiplier=0,
                      allow_small_or_imprecise_dtypes=True).then_inc(made, 1)
            pool.memset(g.selm[:], 0.0).then_inc(made, 1)
            for c in range(3):
                pool.wait_ge(made, 10 + c)
                pool.affine_select(out=g.selm[:], in_=g.selm[:], compare_op=ALU.not_equal, fill=-1.0, base=-8 * c,
                                   pattern=[[-1, 8], [0, P]], channel_multiplier=1).then_inc(made, 1)
            pool.wait_ge(made, 13)
            pool.wait_ge(ident_made, 1)
            pool.tensor_copy(g.identb[:], g.ident[:]).then_inc(ident_b, 1)
            pool.wait_ge(made, 9)
            pool.wait_ge(ident_b, 1)

        @block.tensor
        def _(pe):
            pe.wait_ge(ident_made, 1)
            pe.wait_ge(w_loaded, 80)
            for c in range(16):
                ins = pe.transpose(ps[:, c // 4, (c % 4) * P:(c % 4 + 1) * P], nat[:, c, :], g.ident[:])
            ins.then_inc(turned, 1)

        @block.vector
        def _(dve):
            dve.wait_ge(turned, 1)
            dve.tensor_copy(g.wt[:, 0:4, :], ps[:, 0, :]).then_inc(moved, 1)
            dve.tensor_copy(g.wt[:, 4:8, :], ps[:, 1, :]).then_inc(moved, 1)
            for c in (0, 1):
                heads = ps[:, 2 + c, :].rearrange("p (h k d) -> p h k d", h=4, k=2)
                for k, dst in ((0, g.wkh), (1, g.wvh)):
                    dve.tensor_copy(dst[:, c * 256:c * 256 + 256].rearrange("p (h d) -> p h d", h=4),
                                    heads[:, :, k, :]).then_inc(moved, 1)
            dve.wait_ge(made, 9)
            dve.wait_ge(beta_ld, 16 * H0)
            for k in range(11):
                dve.tensor_scalar(g.mbeta[:, k, :], g.blk[:], betac[:, k:k + 1], None, ALU.mult).then_inc(mb, 1)
            dve.wait_ge(mb, 11)
            dve.wait_ge(moved, 6)



PRIME = 3


def upto(b, per, n):
    value = b * per + n + PRIME
    return max(value, 1) if isinstance(value, int) else value


MAX_UNITS = [(3, (h,)) for h in range(4)] + [(2, (h,)) for h in range(4)] + [(1, (0, 1)), (1, (2, 3)), (0, (0, 1, 2, 3))]
GROUPS = H0 // 4
N_MAX = GROUPS * len(MAX_UNITS)
EXP_UNITS = ([[(h, 0, 0)] for h in range(4)] + [[(h, 1, 0), (h, 3, 3 * P)] for h in range(4)]
             + [[(h, 2, 0), (h + 1, 2, 2 * P)] for h in (0, 2)])
LAST_KT = 2
N_GRP = len(EXP_UNITS)
N_EXP = GROUPS * N_GRP
SLOTS = 3


def l0_plan(p2, p1, front):
    at = {}

    def put(u, *step):
        at.setdefault(u, []).append(step)

    if p1:
        put(1, "v"), put(3, "hidden"), put(5, "logits")
        first, step = 4, 42 / N_MAX
        for k in range(N_MAX):
            put(first + k * step, "max", k)
        for grp in range(GROUPS):
            put(first + ((grp + 1) * len(MAX_UNITS) + 0.5) * step, "minus_max", grp)
    if front:
        put(0.5, "norm"), put(7.1, "turn"), put(36, "lay_out") if not p2 else put(40, "lay_out")
        for n, u in enumerate((10.1, 16.1)):
            put(u, "project", n), put(u + 2.5, "split", n, 0), put(u + 5, "split", n, 1)
    if p2:
        for u in range(N_EXP):
            put(u, "scores", u)
            put(u + 2.01, "weigh", u)
        for grp in range(GROUPS):
            put(N_GRP * (grp + 1) + 3.3, "turn_out", grp)
        put(46, "out_turn"), put(48, "out_project")
    return [step for u in sorted(at) for step in at[u]]


def layer0(nc, g, w):
    with ExitStack() as ctx:
        m = Mem(nc, ctx, "l0_")
        ps = g.ps
        st = m.sb("bn_parts", [P, T, 6])
        mv = m.sb("mean_var", [P, T, 2])
        rstd = m.sb("rstd", [P, 3, T])
        xn = m.sb("xn", [P, T, P])
        xnT = m.sb("xnT", [P, S])
        full = m.sb("full", [P, S])
        rest = m.sb("rest", [P, S])
        part = m.sb("part", [P, 2, 3, S], BF16)
        qS = [m.sb(f"qS{a}", [ROWS, H0, S], BF16) for a in range(2)]
        kS = [m.sb(f"kS{a}", [ROWS, H0, S], BF16) for a in range(2)]
        pos = m.sb("pos", [1, S], BF16)
        va = [m.sb(f"va{a}", [P, T, H0, 32]) for a in range(2)]
        bq = m.sb("bq", [P, 1])
        hr = m.sb("hr", [64, S])
        h2 = [m.sb(f"h2{a}", [64, S]) for a in range(2)]
        mx = m.sb("mx", [P, 2, T, 4])
        mrest = m.sb("mrest", [P, T, 4])
        mpart = m.sb("mpart", [P, T, 3, 4], BF16)
        mT = m.sb("mT", [12, S], BF16)
        PT = m.sb("PT", [P, SLOTS, S])
        OT = m.sb("OT", [P, S])
        rsum = m.sb("rsum", [P, T, 4])
        o = m.sb("o", [P, T, P])
        oT = m.sb("oT", [P, S])
        (xn_made, turned, xnT_made, qk_proj, full_made, rest_made, second_made, split, stored, laid,
         v_proj, v_made, h_proj, relu, squared, l_proj, l_made, scored, maxed, m_made, m_turned, mT_made, mlaid,
         st_made, exped, pv_done, OT_made, OT_turned, o_made, o_turned, oT_made, acc_made, x_made, x_bias, xnT_kept) = loop_sems = tuple(
            m.sem(n) for n in (
                "xn_made turned xnT_made qk_proj full_made rest_made second_made split stored laid "
                "v_proj v_made h_proj relu squared l_proj l_made scored maxed m_made m_turned mT_made mlaid "
                "st_made exped pv_done OT_made OT_turned o_made o_turned oT_made acc_made x_made x_bias xnT_kept").split())
        rows_set, pos_laid, bq_made, primed, dch_pre, dch, dch_post, held = (
            m.sem(n) for n in "rows_set pos_laid bq_made primed dch_pre dch dch_post held".split())
        BANK_M, BANK_S, BANK_O = 7, 2, 5
        by_feature = nc.dram_tensor("by_feature", [2, 3, P, S], BF16).ap()
        LOADS = 2 * len(Q_PART)
        EMPTIED = {"v": (v_made, 1), "hidden": (relu, 1), "logits": (l_made, 1), "minus_max": (mT_made, GROUPS),
                   "turn": (xnT_made, 1), "project": (full_made, 2), "turn_out": (o_made, GROUPS),
                   "out_turn": (oT_made, 1), "out_project": (x_made, 1)}
        AHEAD = {"v": 1, "hidden": 1, "logits": 1, "max": 1, "minus_max": 1, "norm": 2, "turn": 2, "project": 2, "split": 2, "lay_out": 2,
                 "scores": 0, "weigh": 0, "turn_out": 0, "out_turn": 0, "out_project": 0}
        block = ctx.enter_context(nc.Block())

        def plan_at(i, k):
            return isinstance(i, int) and i == k

        def turns(eng, turn):
            turn(-2, l0_plan(False, False, True), 0)
            turn(-1, l0_plan(False, True, True), 1)
            with eng.Fori(0, (B - 2) // 2) as j:
                turn(j * 2, l0_plan(True, True, True), 0, j)
                turn(j * 2 + 1, l0_plan(True, True, True), 1, j)
            turn(B - 2, l0_plan(True, True, False), 0)
            turn(B - 1, l0_plan(True, False, False), 1)

        @block.sync
        def _(sp):
            for s in loop_sems:
                sp.sem_inc(s, PRIME)
            sp.wait_ge(rows_set, 7)
            for a in range(2):
                sp.dma_start(kS[a][ROW_POS:ROW_POS + 1, :, :],
                             pos[:].rearrange("p (a s) -> p a s", a=1).to_broadcast([1, H0, S])).then_inc(pos_laid, 16)

            def turn(i, plan, a, j=None):
                for name, *idx in plan:
                    b = i + AHEAD[name]
                    n = idx[0] if idx else 0
                    if name == "minus_max":
                        sp.wait_ge(mT_made, upto(b, GROUPS, n + 1))
                        sp.dma_start(qS[1 - a][ROW_MAX:ROW_MAX + 3, 4 * n:4 * n + 4, :], mT[:]).then_inc(mlaid, 16)
                    elif name == "split" and idx[1] == 1:
                        sp.wait_ge(split, upto(b, 2, n + 1))
                        sp.dma_start(by_feature[n].rearrange("c p s -> p c s"), part[:, n, :, :]).then_inc(stored, 16)
                    elif name == "lay_out":
                        sp.wait_ge(stored, upto(b, 32, 32))
                        sp.sem_inc(held, 1)
                        sp.wait_ge(st_made, upto(b - 2, N_EXP, N_EXP) if j is not None else 1)
                        for rows, side, parts in ((qS[a], 0, Q_PART), (kS[a], 1, K_PART)):
                            for r, c in enumerate(parts):
                                sp.dma_start(rows[HD0 * r:HD0 * r + HD0, :, :],
                                             by_feature[side, c].rearrange("(h d) s -> d h s", d=HD0)).then_inc(laid, 16)

            turns(sp, turn)
            sp.wait_ge(mlaid, upto(B, 16 * GROUPS, 0))

        @block.gpsimd
        def _(pool):
            for a in range(2):
                pool.memset(kS[a][:], -1.0).then_inc(rows_set, 1)
                pool.memset(qS[a][:], 1.0).then_inc(rows_set, 1)
                pool.memset(va[a][:, :, :, HD0:32], 0.0).then_inc(rows_set, 1)
            pool.iota(pos[:], pattern=[[1, S]], base=-S // 2, channel_multiplier=0,
                      allow_small_or_imprecise_dtypes=True).then_inc(rows_set, 1)
            pool.wait_ge(rows_set, 7)
            for a in range(2):
                pool.memset(va[a][:, :, :, HD0:HD0 + 1], 1.0).then_inc(rows_set, 1)

            def turn(i, plan, a, j=None):
                for name, *idx in plan:
                    b = i + AHEAD[name]
                    n = idx[0] if idx else 0
                    if name == "hidden":
                        pool.wait_ge(relu, upto(b, 1, 1))
                        pool.wait_ge(acc_made, upto(b - 1, 1, 0))
                        pool.tensor_tensor(h2[1 - a][:], hr[:], hr[:], ALU.mult).then_inc(squared, 1)
                    elif name == "norm":
                        pool.wait_ge(xn_made, upto(b, 1, 1))
                        x_b = g.xs[:, bass.ds(b * T, T), :]
                        pool.tensor_tensor(x_b, x_b, g.bo[:].rearrange("p (a d) -> p a d", a=1).to_broadcast([P, T, P]),
                                           ALU.add).then_inc(x_bias, 1)
                    elif name == "turn":
                        pool.wait_ge(xnT_made, upto(b, 1, 1))
                        pool.sem_inc(held, 1)
                        pool.tensor_copy(g.xnT_all[:, bass.ds(b * S, S)], xnT[:]).then_inc(xnT_kept, 1)

            turns(pool, turn)

        @block.tensor
        def _(pe):
            pe.wait_ge(pos_laid, 32)
            pe.wait_ge(rows_set, 9)

            def turn(i, plan, a, j=None):
                before = [("project", 0, 1)] if plan_at(i, -1) else [] if plan_at(i, -2) else [
                    ("minus_max", i, GROUPS - 1), ("out_project", i - 1, 0)]
                for name, *idx in plan:
                    b = i + AHEAD[name]
                    n = idx[0] if idx else 0
                    if name in EMPTIED:
                        for last, of, k in before:
                            sem, per = EMPTIED[last]
                            pe.wait_ge(sem, upto(of, per, k + 1))
                        before = [(name, b, n)]
                    if name == "turn":
                        pe.wait_ge(xn_made, upto(b, 1, 1))
                        for t in range(T):
                            ins = pe.transpose(ps[:, BANK_M, t * P:(t + 1) * P], xn[:, t, :], g.ident[:])
                        ins.then_inc(turned, 1)
                    elif name == "project":
                        pe.wait_ge(xnT_made, upto(b, 1, 1))
                        pe.matmul(ps[:, BANK_M, :], lhsT=g.wt[:, n, :], rhs=xnT[:], start=True, stop=True).then_inc(qk_proj, 1)
                    elif name == "v":
                        for t in range(T):
                            ins = pe.matmul(ps[:, BANK_M, t * P:(t + 1) * P], lhsT=xnT[:, t * P:(t + 1) * P], rhs=g.wt[:, 2, :],
                                            start=True, stop=True)
                        ins.then_inc(v_proj, 1)
                    elif name == "hidden":
                        pe.matmul(ps[0:64, BANK_M, :], lhsT=g.ws1[:], rhs=xnT[:], start=True, stop=True).then_inc(h_proj, 1)
                    elif name == "logits":
                        for t in range(T):
                            ins = pe.matmul(ps[:, BANK_M, t * 8:(t + 1) * 8], lhsT=xnT[:, t * P:(t + 1) * P], rhs=g.wr[:],
                                            start=True, stop=True)
                        ins.then_inc(l_proj, 1)
                    elif name == "max":
                        grp, u = divmod(n, len(MAX_UNITS))
                        qt, heads = MAX_UNITS[u]
                        N = (qt + 1) * P
                        if n == 0:
                            pe.wait_ge(laid, upto(b, 16 * LOADS, 16 * LOADS))
                        pe.wait_ge(maxed, upto(b, N_MAX, n - 1))
                        q, k = qS[1 - a], kS[1 - a]
                        for x, hh in enumerate(heads):
                            h = 4 * grp + hh
                            pe.matmul(ps[:, n % 2, x * N:(x + 1) * N], lhsT=q[0:ROW_MAX, h, qt * P:(qt + 1) * P],
                                      rhs=k[0:ROW_MAX, h, 0:N], start=True, stop=False)
                            ins = pe.matmul(ps[:, n % 2, (x + 1) * N - P:(x + 1) * N], lhsT=g.identb[:], rhs=g.maskb[:, 0, :],
                                            start=False, stop=True)
                        ins.then_inc(scored, 1)
                    elif name == "minus_max":
                        pe.wait_ge(m_made, upto(b, GROUPS, n + 1))
                        for t in range(T):
                            ins = pe.transpose(ps[:, BANK_M, :].bitcast(BF16)[0:12, t * P:(t + 1) * P], mpart[:, t, :, :],
                                               g.identb[:])
                        ins.then_inc(m_turned, 1)
                    elif name == "scores":
                        grp, u = divmod(n, N_GRP)
                        if u == 0:
                            pe.wait_ge(mlaid, upto(b, 16 * GROUPS, 16 * (grp + 1)))
                        pe.wait_ge(exped, upto(b, N_EXP, n - SLOTS + 1))
                        for hh, kt, c in EXP_UNITS[u]:
                            h, bank, N = 4 * grp + hh, BANK_S + n % SLOTS, (T - kt) * P
                            pe.matmul(ps[:, bank, c:c + N], lhsT=kS[a][:, h, kt * P:(kt + 1) * P], rhs=qS[a][:, h, kt * P:S],
                                      start=True, stop=False)
                            ins = pe.matmul(ps[:, bank, c:c + P], lhsT=g.identb[:], rhs=g.maskb[:, 1, :], start=False, stop=True)
                        ins.then_inc(st_made, 1)
                    elif name == "weigh":
                        grp, u = divmod(n, N_GRP)
                        pe.wait_ge(exped, upto(b, N_EXP, n + 1))
                        if n == 0:
                            pe.wait_ge(v_made, upto(b, 1, 1))
                        if u == 0:
                            pe.wait_ge(OT_made, upto(b, GROUPS, grp - 1))
                        for hh, kt, c in EXP_UNITS[u]:
                            ins = pe.matmul(ps[32 * hh:32 * hh + 32, BANK_O + grp % 2, kt * P:S], lhsT=va[a][:, kt, 4 * grp + hh, :],
                                            rhs=PT[:, n % SLOTS, c:c + (T - kt) * P], start=kt == 0, stop=kt == LAST_KT)
                        ins.then_inc(pv_done, 1)
                    elif name == "turn_out":
                        pe.wait_ge(OT_made, upto(b, GROUPS, n + 1))
                        for t in range(T):
                            ins = pe.transpose(ps[:, BANK_M, t * P:(t + 1) * P], OT[:, t * P:(t + 1) * P], g.ident[:])
                        ins.then_inc(OT_turned, 1)
                    elif name == "out_turn":
                        pe.wait_ge(o_made, upto(b, GROUPS, GROUPS))
                        for t in range(T):
                            ins = pe.transpose(ps[:, BANK_M, t * P:(t + 1) * P], o[:, t, :], g.ident[:])
                        ins.then_inc(o_turned, 1)
                    elif name == "out_project":
                        pe.wait_ge(oT_made, upto(b, 1, 1))
                        pe.wait_ge(squared, upto(b, 1, 1))
                        for t in range(T):
                            out = ps[:, BANK_M, t * P:(t + 1) * P]
                            pe.matmul(out, lhsT=oT[:, t * P:(t + 1) * P], rhs=g.wt[:, 3, :], start=True, stop=False)
                            ins = pe.matmul(out, lhsT=h2[a][:, t * P:(t + 1) * P], rhs=g.ws2[:], start=False, stop=True)
                        ins.then_inc(acc_made, 1)

            turns(pe, turn)

        @block.scalar
        def _(act):
            act.mul(bq[:], g.bqkv[:, 0:1], HD0 ** -0.5).then_inc(bq_made, 1)
            act.wait_ge(bq_made, 1)

            def turn(i, plan, a, j=None):
                for name, *idx in plan:
                    b = i + AHEAD[name]
                    n = idx[0] if idx else 0
                    if name == "turn":
                        act.wait_ge(turned, upto(b, 1, 1))
                        act.wait_ge(l_proj, upto(b, 1, 0))
                        act.wait_ge(xnT_kept, upto(b, 1, 0))
                        act.copy(xnT[:], ps[:, BANK_M, :]).then_inc(xnT_made, 1)
                    elif name == "project":
                        act.wait_ge(qk_proj, upto(b, 2, n + 1))
                        act.wait_ge(rest_made, upto(b, 2, n))
                        act.wait_ge(stored, upto(b, 32, 16 * n - 16))
                        bias, scale = (bq[:], HD0 ** -0.5) if n == 0 else (g.bqkv[:, 1:2], 1.0)
                        act.activation(full[:], ps[:, BANK_M, :], ACT.Identity, bias=bias, scale=scale)
                        act.activation(part[:, n, 0, :], ps[:, BANK_M, :], ACT.Identity, bias=bias, scale=scale).then_inc(full_made, 1)
                    elif name == "split" and idx[1] == 0:
                        act.wait_ge(rest_made, upto(b, 2, n + 1))
                        act.copy(part[:, n, 1, :], rest[:]).then_inc(second_made, 1)
                    elif name == "hidden":
                        act.wait_ge(h_proj, upto(b, 1, 1))
                        act.wait_ge(squared, upto(b, 1, 0))
                        act.activation(hr[:], ps[0:64, BANK_M, :], ACT.Relu).then_inc(relu, 1)
                    elif name == "minus_max":
                        act.wait_ge(m_turned, upto(b, GROUPS, n + 1))
                        act.wait_ge(mlaid, upto(b, 16 * GROUPS, 16 * n))
                        act.copy(mT[:], ps[:, BANK_M, :].bitcast(BF16)[0:12, 0:S]).then_inc(mT_made, 1)
                    elif name == "scores":
                        act.wait_ge(st_made, upto(b, N_EXP, n + 1))
                        act.wait_ge(pv_done, upto(b, N_EXP, n - SLOTS + 1))
                        act.activation(PT[:, n % SLOTS, :], ps[:, BANK_S + n % SLOTS, :], ACT.Exp).then_inc(exped, 1)
                    elif name == "weigh" and n % N_GRP == N_GRP - 1:
                        grp = n // N_GRP
                        act.wait_ge(pv_done, upto(b, N_EXP, n + 1))
                        act.wait_ge(OT_turned, upto(b, GROUPS, grp))
                        act.copy(OT[:], ps[:, BANK_O + grp % 2, :]).then_inc(OT_made, 1)
                    elif name == "out_turn":
                        act.wait_ge(o_turned, upto(b, 1, 1))
                        act.wait_ge(acc_made, upto(b, 1, 0))
                        act.copy(oT[:], ps[:, BANK_M, :]).then_inc(oT_made, 1)

            turns(act, turn)

        @block.vector
        def _(dve):
            dve.wait_ge(rows_set, 9)
            chains = {}

            def turn(i, plan, a, j=None):
                if j is None:
                    link = chains.setdefault(i < 0, Chain(dve, dch_pre if i < 0 else dch_post))
                else:
                    link = chains.setdefault("loop", Chain(dve, dch, j, 66))
                for name, *idx in plan:
                    b = i + AHEAD[name]
                    n = idx[0] if idx else 0
                    if name == "norm":
                        dve.wait_ge(turned, upto(b, 1, 0))
                        for t in range(T):
                            ins = dve.bn_stats(st[:, t, :], g.xs[:, bass.ds(b * T + t, 1), :])
                        link(ins, held)
                        for t in range(T):
                            ins = dve.bn_aggr(mv[:, t, :], st[:, t, :])
                        link(ins)
                        link(dve.tensor_scalar(rstd[:, 0, :], mv[:, :, 1], EPS, None, ALU.add))
                        inv_sqrt(dve, link, rstd[:, 0, :], rstd[:, 1, :], rstd[:, 2, :])
                        for t in range(T):
                            ins = dve.tensor_scalar(xn[:, t, :], g.xs[:, bass.ds(b * T + t, 1), :], mv[:, t, 0:1],
                                                    rstd[:, 1, t:t + 1], ALU.subtract, ALU.mult)
                        ins.then_inc(xn_made, 1)
                    elif name == "split" and idx[1] == 0:
                        dve.wait_ge(full_made, upto(b, 2, n + 1))
                        dve.wait_ge(split, upto(b, 2, n))
                        dve.tensor_tensor(rest[:], full[:], part[:, n, 0, :], ALU.subtract).then_inc(rest_made, 1)
                    elif name == "split":
                        dve.wait_ge(second_made, upto(b, 2, n + 1))
                        dve.tensor_tensor(part[:, n, 2, :], rest[:], part[:, n, 1, :], ALU.subtract).then_inc(split, 1)
                    elif name == "v":
                        dve.wait_ge(v_proj, upto(b, 1, 1))
                        dve.wait_ge(pv_done, upto(b - 1, N_EXP, 0))
                        for t in range(T):
                            ins = dve.tensor_tensor(va[1 - a][:, t, :, 0:HD0],
                                                    ps[:, BANK_M, t * P:(t + 1) * P].rearrange("p (h d) -> p h d", h=H0),
                                                    g.bv[:].rearrange("p (h d) -> p h d", h=H0), ALU.add)
                        ins.then_inc(v_made, 1)
                    elif name == "logits":
                        dve.wait_ge(l_proj, upto(b, 1, 1))
                        dve.tensor_copy(g.logits[:, bass.ds(b * T, T), :],
                                        ps[:, BANK_M, 0:T * 8].rearrange("p (t e) -> p t e", t=T)).then_inc(l_made, 1)
                    elif name == "max":
                        grp, u = divmod(n, len(MAX_UNITS))
                        qt, heads = MAX_UNITS[u]
                        if u == 0:
                            dve.wait_ge(m_made, upto(b, GROUPS, grp - 1))
                        dve.wait_ge(scored, upto(b, N_MAX, n + 1))
                        dve.tensor_reduce(mx[:, grp % 2, qt, heads[0]:heads[-1] + 1],
                                          ps[:, n % 2, 0:len(heads) * (qt + 1) * P].rearrange("p (h k) -> p h k", h=len(heads)),
                                          AX.X, ALU.max).then_inc(maxed, 1)
                    elif name == "minus_max":
                        dve.wait_ge(maxed, upto(b, N_MAX, (n + 1) * len(MAX_UNITS)))
                        dve.wait_ge(m_turned, upto(b, GROUPS, n))
                        link(dve.tensor_copy(mpart[:, :, 0, :], mx[:, n % 2]))
                        link(dve.tensor_tensor(mrest[:], mx[:, n % 2], mpart[:, :, 0, :], ALU.subtract))
                        link(dve.tensor_copy(mpart[:, :, 1, :], mrest[:]))
                        dve.tensor_tensor(mpart[:, :, 2, :], mrest[:], mpart[:, :, 1, :], ALU.subtract).then_inc(m_made, 1)
                    elif name == "turn_out":
                        dve.wait_ge(OT_turned, upto(b, GROUPS, n + 1))
                        dve.wait_ge(o_turned, upto(b, 1, 0))
                        O = ps[:, BANK_M, :].rearrange("p (t h d) -> p t h d", t=T, h=4)
                        link(dve.reciprocal(rsum[:], O[:, :, :, HD0]))
                        for t in range(T):
                            ins = dve.tensor_tensor(
                                o[:, t, 32 * n:32 * n + 32].rearrange("p (h d) -> p h d", h=4), O[:, t, :, 0:HD0],
                                rsum[:, t, :].rearrange("p (h a) -> p h a", a=1).to_broadcast([P, 4, HD0]), ALU.mult)
                        ins.then_inc(o_made, 1)
                    elif name == "out_project":
                        dve.wait_ge(acc_made, upto(b, 1, 1))
                        dve.wait_ge(x_bias, upto(b, 1, 1))
                        x_b = g.xs[:, bass.ds(b * T, T), :]
                        dve.tensor_tensor(x_b, ps[:, BANK_M, :].rearrange("p (t d) -> p t d", t=T), x_b,
                                          ALU.add).then_inc(x_made, 1)

            turns(dve, turn)
            chains["loop"].close()
            dve.wait_ge(x_made, upto(B, 1, 0))



def gates(nc, g):
    N = B * T
    with ExitStack() as ctx:
        m = Mem(nc, ctx, "gt_")
        top = m.sb("top8", [P, N, 8])
        d = m.sb("gate_d", [P, 4, N])
        total = m.sb("gate_total", [P, 1])
        topped, exped, dch, counted, summed, flagged = (m.sem(n) for n in "topped exped dch counted summed flagged".split())
        block = ctx.enter_context(nc.Block())

        @block.vector
        def _(dve):
            link = Chain(dve, dch)
            for t in range(N):
                ins = dve.max(top[:, t, :], g.logits[:, t, :])
            link(ins)
            dve.tensor_tensor(d[:, 0, :], top[:, :, 1], top[:, :, 0], ALU.subtract).then_inc(topped, 1)
            dve.wait_ge(exped, 1)
            link(dve.tensor_scalar(d[:, 2, :], d[:, 1, :], 1.0, None, ALU.add))
            link(dve.reciprocal(d[:, 3, :], d[:, 2, :]))
            link(dve.tensor_scalar(d[:, 3, :], d[:, 3, :], 1.0, None, ALU.is_ge))
            link(dve.tensor_tensor(g.gate[:], g.logits[:], top[:, :, 0:1].to_broadcast([P, N, 8]), ALU.is_equal))
            link(dve.tensor_tensor(g.gate[:], g.gate[:],
                                   d[:, 3, :].rearrange("p (n a) -> p n a", a=1).to_broadcast([P, N, 8]), ALU.mult))
            dve.tensor_reduce(total[:], g.gate[:], AX.XY, ALU.add).then_inc(counted, 1)
            dve.wait_ge(summed, 1)
            dve.tensor_copy(g.any_gate[:], g.ps[:, 0, 0:1]).then_inc(flagged, 1)
            dve.wait_ge(flagged, 1)

        @block.scalar
        def _(act):
            act.wait_ge(topped, 1)
            act.activation(d[:, 1, :], d[:, 0, :], ACT.Exp).then_inc(exped, 1)

        @block.tensor
        def _(pe):
            pe.wait_ge(counted, 1)
            pe.matmul(g.ps[:, 0, 0:1], lhsT=g.ones[:], rhs=total[:], start=True, stop=True).then_inc(summed, 1)


def routed_experts(nc, g):
    with ExitStack() as ctx:
        m = Mem(nc, ctx, "ex_")
        ps = g.ps
        gate = m.sb("gate_now", [P, T, 8])
        gT = m.sb("gT", [8, S])
        esel = m.sb("esel", [8, 4, 2, 64])
        r = m.sb("r", [P, 4, S])
        r2 = m.sb("r2", [P, 4, S])
        (e_set, gate_copied, g_turned, gT_made, h_made, spread, relu_made, squared, gated, y_made, added) = (
            m.sem(n) for n in (
                "e_set gate_copied g_turned gT_made h_made spread relu_made squared gated y_made added").split())
        block = ctx.enter_context(nc.Block())

        @block.sync
        def _(sp):
            for turns in (added, g_turned, gated, squared, y_made):
                sp.sem_inc(turns, 1)

        @block.gpsimd
        def _(pool):
            with pool.If(pool.value_load(g.any_gate[0:1, 0:1]) > 0):
                pool.memset(esel[:], 1.0).then_inc(e_set, 1)
                pool.wait_ge(e_set, 1)
                pool.affine_select(out=esel[:], in_=esel[:], compare_op=ALU.is_equal, fill=0.0, base=0,
                                   pattern=[[-2, 4], [-1, 2], [0, 64]], channel_multiplier=1).then_inc(e_set, 1)

        @block.tensor
        def _(pe):
            with pe.If(pe.value_load(g.any_gate[0:1, 0:1]) > 0):
                pe.wait_ge(e_set, 2)
                with pe.Fori(0, B) as i:
                    pe.wait_ge(gate_copied, i + 1)
                    for t in range(T):
                        ins = pe.transpose(ps[0:8, 0, t * P:(t + 1) * P], gate[:, t, :], g.ident[:])
                    ins.then_inc(g_turned, 1)
                    pe.wait_ge(gT_made, i + 1)
                    for c in range(4):
                        pe.wait_ge(squared, i * 4 + c + 1)
                        pe.matmul(ps[:, 1 + c % 2, :], lhsT=g.w1[:, 2 * c:2 * c + 2, :],
                                  rhs=g.xnT_all[:, bass.ds(i * S, S)], start=True, stop=True).then_inc(h_made, 1)
                        pe.wait_ge(gated, i * 4 + c + 1)
                        pe.matmul(ps[:, 3 + c % 2, :], lhsT=esel[:, c, :, :], rhs=gT[:], start=True,
                                  stop=True).then_inc(spread, 1)
                    pe.wait_ge(gated, i * 4 + 4 + 1)
                    pe.wait_ge(added, i + 1)
                    for t in range(T):
                        for c in range(4):
                            ins = pe.matmul(ps[:, 5, t * P:(t + 1) * P], lhsT=r2[:, c, t * P:(t + 1) * P], rhs=g.w2[:, c, :],
                                            start=c == 0, stop=c == 3)
                    ins.then_inc(y_made, 1)

        @block.scalar
        def _(act):
            with act.If(act.value_load(g.any_gate[0:1, 0:1]) > 0):
                with act.Fori(0, B) as i:
                    act.wait_ge(g_turned, i + 2)
                    act.copy(gT[:], ps[0:8, 0, :]).then_inc(gT_made, 1)
                    for c in range(4):
                        act.wait_ge(h_made, i * 4 + c + 1)
                        act.wait_ge(gated, i * 4 + 1)
                        act.activation(r[:, c, :], ps[:, 1 + c % 2, :], ACT.Relu).then_inc(relu_made, 1)

        @block.vector
        def _(dve):
            with dve.If(dve.value_load(g.any_gate[0:1, 0:1]) > 0):
                with dve.Fori(0, B) as i:
                    dve.wait_ge(g_turned, i + 1)
                    dve.tensor_copy(gate[:], g.gate[:, bass.ds(i * T, T), :]).then_inc(gate_copied, 1)
                    dve.wait_ge(y_made, i + 1)
                    for c in range(4):
                        dve.wait_ge(relu_made, i * 4 + c + 1)
                        dve.tensor_tensor(r2[:, c, :], r[:, c, :], r[:, c, :], ALU.mult).then_inc(squared, 1)
                        dve.wait_ge(spread, i * 4 + c + 1)
                        dve.wait_ge(squared, i * 4 + c + 2)
                        dve.tensor_tensor(r2[:, c, :], r2[:, c, :], ps[:, 3 + c % 2, :], ALU.mult).then_inc(gated, 1)
                    dve.wait_ge(y_made, i + 2)
                    x_b = g.xs[:, bass.ds(i * T, T), :]
                    dve.tensor_tensor(x_b, ps[:, 5, :].rearrange("p (t d) -> p t d", t=T), x_b, ALU.add).then_inc(added, 1)
                dve.wait_ge(added, B + 1)



def layer1(nc, g):
    HL, HDL = 8, 64
    with ExitStack() as ctx:
        m = Mem(nc, ctx, "l1_")
        ps = g.ps
        st = m.sb("bn_parts", [P, T, 6])
        mv = m.sb("mean_var", [P, T, 2])
        sm = m.sb("small", [P, 8, T])
        xn = m.sb("xn", [P, T, P])
        xr_now = m.sb("xr_now", [P, T, P])
        sq = m.sb("squares", [P, P])
        xnT = m.sb("xnT", [P, S])
        xlT = m.sb("xlT", [P, S])
        s_row = m.sb("s_row", [2, S])
        raw = m.sb("raw", [P, 2, S])
        tq = m.sb("tq", [P, 11, S])
        tk = m.sb("tk", [P, 11, T, P])
        vc = m.sb("vc", [P, T, P])
        kvm = m.sb("kvm", [P, 11, P])
        cT = m.sb("cT", [P, S])
        lq = m.sb("lq", [P, 4, S])
        lk = m.sb("lk", [P, 4, S])
        lv = m.sb("lv", [P, T, HL, HDL + 1])
        mx = m.sb("mx", [P, 8])
        mrest = m.sb("mrest", [P, 8])
        mpart = m.sb("mpart", [P, 3, 8], BF16)
        mT = m.sb("mT", [24, P], BF16)
        PT = m.sb("PT", [P, 2, S])
        rsum = m.sb("rsum", [P, 2, 4])
        o = m.sb("o", [P, 4, 2, HDL])
        oT = m.sb("oT", [P, 4, P])
        (dve_held, pool_held, dch, pch, ones_set, xn_made, turned, xnT_made, xlT_made, c_proj, s_proj, s_out, s_stored, raw_made, vc_made,
         tq1, tk1, tq_made, tk_made, kv_prod, kv_made, c_out, cT_made, lq_proj, lk_proj, lv_proj, lqk_made, lk_made, lv_made,
         scored, maxed, m_turned, mT_made, st_made, exped, pv_done, o_made, o_turned, oT_made, y_made, x_made) = (
            m.sem(n) for n in (
                "dve_held pool_held dch pch ones_set xn_made turned xnT_made xlT_made c_proj s_proj s_out s_stored raw_made vc_made "
                "tq1 tk1 tq_made tk_made kv_prod kv_made c_out cT_made lq_proj lk_proj lv_proj lqk_made lk_made lv_made "
                "scored maxed m_turned mT_made st_made exped pv_done o_made o_turned oT_made y_made x_made").split())
        block = ctx.enter_context(nc.Block())
        STEPS = [(n, n // 2, n - n // 2) for n in range(2, 11)]

        @block.sync
        def _(sp):
            for turns in (c_out, kv_prod, lv_proj, oT_made, o_made, pv_done, s_proj, s_stored, st_made, tk1, tq1, x_made, y_made):
                sp.sem_inc(turns, 1)
            with sp.Fori(0, B) as i:
                sp.wait_ge(s_out, i + 1)
                sp.dma_start(g.s_dram[:, bass.ds(i, 1), :], s_row[:].rearrange("r (a s) -> r a s", a=1)).then_inc(s_stored, 16)
            sp.wait_ge(s_stored, 16 * B + 1)

        @block.gpsimd
        def _(pool):
            pool.memset(tk[:, 0, :, :], 1.0).then_inc(ones_set, 1)
            pool.memset(tq[:, 0, :], 1.0).then_inc(ones_set, 1)
            pool.memset(lv[:], 1.0).then_inc(ones_set, 1)
            pool.wait_ge(ones_set, 3)
            with pool.Fori(0, B) as i:
                link = Chain(pool, pch, i, 22)
                pool.wait_ge(tk1, i + 2)
                pool.wait_ge(kv_prod, i * 3 + 1)
                x = tk[:, 1, :, :]
                for n, a, b in STEPS:
                    t = tk[:, n, :, :]
                    link(pool.tensor_tensor(t, tk[:, a, :, :], tk[:, b, :, :], ALU.mult), pool_held)
                    if n % 2 == 0:
                        link(pool.tensor_scalar(t, t, 2.0, -1.0, ALU.mult, ALU.add))
                    else:
                        link(pool.tensor_scalar(t, t, 2.0, 0.0, ALU.mult, ALU.add))
                        link(pool.tensor_tensor(t, t, x, ALU.subtract))
                pool.sem_inc(tk_made, 1)
                link.close()

        @block.tensor
        def _(pe):
            pe.wait_ge(ones_set, 3)
            with pe.Fori(0, B) as i:
                pe.wait_ge(xn_made, i * 2 + 2)
                for t in range(T):
                    pe.transpose(ps[:, 0, t * P:(t + 1) * P], xn[:, t, :], g.ident[:])
                for t in range(T):
                    ins = pe.transpose(ps[:, 1, t * P:(t + 1) * P], xr_now[:, t, :], g.ident[:])
                ins.then_inc(turned, 1)
                pe.wait_ge(xnT_made, i + 1)
                pe.wait_ge(oT_made, i * T + 1)
                pe.matmul(ps[:, 2, :], lhsT=g.wt[:, 4, :], rhs=xnT[:], start=True, stop=True)
                for t in range(T):
                    ins = pe.matmul(ps[:, 3 + t // 2, (t % 2) * 256:(t % 2) * 256 + 256], lhsT=xnT[:, t * P:(t + 1) * P],
                                    rhs=g.wt[:, 5:7, :], start=True, stop=True)
                ins.then_inc(c_proj, 1)
                pe.matmul(ps[0:2, 5, :], lhsT=g.tok[:], rhs=xnT[:], start=True, stop=True).then_inc(s_proj, 1)
                pe.wait_ge(xlT_made, i + 1)
                BK = (0, 1, 6, 7)
                pe.wait_ge(x_made, i + 1)
                for c in range(4):
                    ins = pe.matmul(ps[:, BK[c], :], lhsT=g.wql[:, c * P:(c + 1) * P], rhs=xlT[:], start=True, stop=True)
                ins.then_inc(lq_proj, 1)
                pe.wait_ge(lqk_made, i * 2 + 1)
                for c in range(4):
                    ins = pe.matmul(ps[:, BK[c], :], lhsT=g.wkvl[:, c * P:(c + 1) * P], rhs=xlT[:], start=True, stop=True)
                ins.then_inc(lk_proj, 1)
                pe.wait_ge(lqk_made, i * 2 + 2)
                for t in range(T):
                    ins = pe.matmul(ps[:, BK[t], :], lhsT=xlT[:, t * P:(t + 1) * P], rhs=g.wkvl[:, 512:1024],
                                    start=True, stop=True)
                ins.then_inc(lv_proj, 1)
                pe.wait_ge(tk_made, i + 1)
                pe.wait_ge(raw_made, i * 2 + 2)
                pe.wait_ge(vc_made, i + 1)
                for n in range(11):
                    for t in range(T):
                        ins = pe.matmul(ps[:, 2 + n // 4, (n % 4) * P:(n % 4 + 1) * P], lhsT=tk[:, n, t, :], rhs=vc[:, t, :],
                                        start=t == 0, stop=t == T - 1)
                    if n % 4 == 3 or n == 10:
                        ins.then_inc(kv_prod, 1)
                    if n == 7:
                        pe.wait_ge(s_out, i + 1)
                        pe.wait_ge(lv_made, i + 1)
                pe.wait_ge(kv_made, i * 3 + 3)
                pe.wait_ge(tq_made, i + 1)
                for n in range(11):
                    ins = pe.matmul(ps[:, 5, :], lhsT=kvm[:, n, :], rhs=tq[:, n, :], start=n == 0, stop=n == 10)
                ins.then_inc(c_out, 1)
                for w in range(T):
                    u = i * T + w
                    tok = slice(w * P, (w + 1) * P)
                    for h in range(HL):
                        c, par = divmod(h, 2)
                        rows = slice(64 * par, 64 * par + 64)
                        ins = pe.matmul(ps[:, par, c * P:(c + 1) * P], lhsT=lq[rows, c, tok], rhs=lk[rows, c, tok],
                                        start=True, stop=True)
                    ins.then_inc(scored, 1)
                    pe.wait_ge(maxed, u + 1)
                    pe.wait_ge(oT_made, u + 1)
                    pe.transpose(ps[:, 6, 0:64].bitcast(BF16)[0:24, 0:P], mpart[:], g.identb[:]).then_inc(m_turned, 1)
                    pe.wait_ge(mT_made, u + 1)
                    pe.wait_ge(kv_made, i * 3 + 3)
                    for h in range(HL):
                        c, par = divmod(h, 2)
                        rows = slice(64 * par, 64 * par + 64)
                        out = ps[:, 2 + par, c * P:(c + 1) * P]
                        pe.matmul(out, lhsT=lk[rows, c, tok], rhs=lq[rows, c, tok], start=True, stop=False)
                        ins = pe.matmul(out, lhsT=g.selm[:, par * 4 + c, :], rhs=mT[:], start=False, stop=True)
                    ins.then_inc(st_made, 1)
                    pe.wait_ge(exped, u + 1)
                    pe.wait_ge(cT_made, i + 1)
                    pe.wait_ge(o_made, u + 1)
                    for h in range(HL):
                        c, par = divmod(h, 2)
                        ins = pe.matmul(ps[:, 4 + par, c * (HDL + 1):(c + 1) * (HDL + 1)], lhsT=PT[:, par, c * P:(c + 1) * P],
                                        rhs=lv[:, w, h, :], start=True, stop=True)
                    ins.then_inc(pv_done, 1)
                    pe.wait_ge(o_made, u + 2)
                    for c in range(4):
                        ins = pe.transpose(ps[:, 6, c * P:(c + 1) * P], o[:, c, :, :], g.ident[:])
                    ins.then_inc(o_turned, 1)
                    pe.wait_ge(oT_made, u + 2)
                    out = ps[:, 7, w * P:(w + 1) * P]
                    pe.matmul(out, lhsT=cT[:, tok], rhs=g.wt[:, 7, :], start=True, stop=False)
                    for c in range(4):
                        ins = pe.matmul(out, lhsT=oT[:, c, :], rhs=g.wol[:, c, :], start=False, stop=c == 3)
                ins.then_inc(y_made, 1)

        @block.scalar
        def _(act):
            with act.Fori(0, B) as i:
                act.wait_ge(turned, i + 1)
                act.wait_ge(lv_proj, i + 1)
                act.wait_ge(s_proj, i + 1)
                act.copy(xnT[:], ps[:, 0, :]).then_inc(xnT_made, 1)
                act.activation(xlT[:], ps[:, 1, :], ACT.Identity, bias=0.0, scale=g.gl[:]).then_inc(xlT_made, 1)
                act.wait_ge(c_proj, i + 1)
                act.wait_ge(tq1, i + 1)
                act.wait_ge(tk1, i + 1)
                act.mul(raw[:, 0, :], ps[:, 2, :], HD0 ** -0.5).then_inc(raw_made, 1)
                kv = ps[:, 3:5, :].rearrange("p b (t s d) -> p (b t) s d", t=2, s=2)
                act.mul(raw[:, 1, :].rearrange("p (t d) -> p t d", t=T), kv[:, :, 0, :], HD0 ** -0.5).then_inc(raw_made, 1)
                act.wait_ge(kv_prod, i * 3 + 1)
                act.copy(vc[:], kv[:, :, 1, :]).then_inc(vc_made, 1)
                act.wait_ge(s_proj, i + 2)
                act.wait_ge(s_stored, i * 16 + 1)
                act.copy(s_row[:], ps[0:2, 5, :]).then_inc(s_out, 1)
                act.wait_ge(lq_proj, i + 1)
                act.wait_ge(st_made, i * T + 1)
                act.mul(lq[:, 0:2, :], ps[:, 0:2, :], HDL ** -0.5)
                act.mul(lq[:, 2:4, :], ps[:, 6:8, :], HDL ** -0.5).then_inc(lqk_made, 1)
                act.wait_ge(lk_proj, i + 1)
                act.copy(lk[:, 0:2, :], ps[:, 0:2, :])
                act.copy(lk[:, 2:4, :], ps[:, 6:8, :]).then_inc(lqk_made, 1)
                act.wait_ge(c_out, i + 2)
                act.wait_ge(y_made, i + 1)
                act.copy(cT[:], ps[:, 5, :]).then_inc(cT_made, 1)
                for w in range(T):
                    u = i * T + w
                    act.wait_ge(m_turned, u + 1)
                    act.wait_ge(st_made, u + 1)
                    act.copy(mT[:], ps[:, 6, 0:64].bitcast(BF16)[0:24, 0:P]).then_inc(mT_made, 1)
                    act.wait_ge(st_made, u + 2)
                    act.wait_ge(pv_done, u + 1)
                    act.activation(PT[:], ps[:, 2:4, :], ACT.Exp).then_inc(exped, 1)
                    act.wait_ge(o_turned, u + 1)
                    if w == 0:
                        act.wait_ge(y_made, i + 1)
                    act.copy(oT[:], ps[:, 6, :]).then_inc(oT_made, 1)

        @block.vector
        def _(dve):
            dve.wait_ge(ones_set, 3)
            with dve.Fori(0, B) as i:
                link = Chain(dve, dch, i, 76)
                x_b = g.xs[:, bass.ds(i * T, T), :]
                for t in range(T):
                    ins = dve.bn_stats(st[:, t, :], g.xs[:, bass.ds(i * T + t, 1), :])
                link(ins, dve_held)
                for t in range(T):
                    ins = dve.bn_aggr(mv[:, t, :], st[:, t, :])
                link(ins)
                link(dve.tensor_scalar(sm[:, 0, :], mv[:, :, 1], EPS, None, ALU.add))
                inv_sqrt(dve, link, sm[:, 0, :], sm[:, 1, :], sm[:, 2, :])
                for t in range(T):
                    ins = dve.tensor_scalar(xn[:, t, :], g.xs[:, bass.ds(i * T + t, 1), :], mv[:, t, 0:1],
                                            sm[:, 1, t:t + 1], ALU.subtract, ALU.mult)
                ins.then_inc(xn_made, 1)
                dve.wait_ge(xn_made, i * 2 + 1)
                for t in range(T):
                    link(dve.tensor_tensor_reduce(sq[:], xn[:, t, :], xn[:, t, :], 1.0, 0.0, ALU.mult, ALU.add, sm[:, 3, t:t + 1]))
                link(dve.tensor_scalar(sm[:, 3, :], sm[:, 3, :], 1e-24, None, ALU.max))
                inv_sqrt(dve, link, sm[:, 3, :], sm[:, 4, :], sm[:, 5, :])
                link(dve.tensor_scalar(sm[:, 4, :], sm[:, 4, :], float(D) ** 0.5, None, ALU.mult))
                for t in range(T):
                    ins = dve.tensor_scalar(xr_now[:, t, :], xn[:, t, :], sm[:, 4, t:t + 1], None, ALU.mult)
                ins.then_inc(xn_made, 1)
                dve.wait_ge(xn_made, i * 2 + 2)
                link(dve.tensor_copy(g.xr[:, bass.ds(i * T, T), :], xr_now[:]))
                dve.wait_ge(raw_made, i * 2 + 2)
                dve.wait_ge(kv_prod, i * 3 + 1)
                dve.wait_ge(c_out, i + 1)
                tk_x = tk[:, 1, :, :].rearrange("p t d -> p (t d)")
                dve.tensor_scalar(tk_x, raw[:, 1, :], 1.0, -1.0, ALU.min, ALU.max).then_inc(tk1, 1)
                dve.tensor_scalar(tq[:, 1, :], raw[:, 0, :], 1.0, -1.0, ALU.min, ALU.max).then_inc(tq1, 1)
                dve.wait_ge(tq1, i + 2)
                for n, a, b in STEPS:
                    link(dve.scalar_tensor_tensor(tq[:, n, :], tq[:, a, :], 2.0, tq[:, b, :], ALU.mult, ALU.mult))
                    if n % 2 == 0:
                        link(dve.tensor_scalar(tq[:, n, :], tq[:, n, :], -1.0, None, ALU.add))
                    else:
                        link(dve.tensor_tensor(tq[:, n, :], tq[:, n, :], tq[:, 1, :], ALU.subtract))
                dve.sem_inc(tq_made, 1)
                dve.wait_ge(lv_proj, i + 2)
                dve.wait_ge(pv_done, i * T + 1)
                for t in range(T):
                    bank = (0, 1, 6, 7)[t]
                    ins = dve.tensor_copy(lv[:, t, :, 0:HDL], ps[:, bank, :].rearrange("p (h d) -> p h d", h=HL))
                ins.then_inc(lv_made, 1)
                for j in range(3):
                    n = 4 if j < 2 else 3
                    dve.wait_ge(kv_prod, i * 3 + j + 2)
                    dve.tensor_tensor(kvm[:, 4 * j:4 * j + n, :],
                                      ps[:, 2 + j, 0:n * P].rearrange("p (n d) -> p n d", n=n),
                                      g.mbeta[:, 4 * j:4 * j + n, :], ALU.mult).then_inc(kv_made, 1)
                for w in range(T):
                    u = i * T + w
                    dve.wait_ge(scored, u + 1)
                    link(dve.tensor_reduce(mx[:], ps[:, 0:2, :].rearrange("p b (c k) -> p (b c) k", c=4), AX.X, ALU.max))
                    link(dve.tensor_copy(mpart[:, 0, :], mx[:]))
                    link(dve.tensor_tensor(mrest[:], mx[:], mpart[:, 0, :], ALU.subtract))
                    link(dve.tensor_copy(mpart[:, 1, :], mrest[:]))
                    dve.tensor_tensor(mpart[:, 2, :], mrest[:], mpart[:, 1, :], ALU.subtract).then_inc(maxed, 1)
                    dve.wait_ge(pv_done, u + 2)
                    O = ps[:, 4:6, 0:4 * (HDL + 1)].rearrange("p b (c d) -> p b c d", c=4)
                    link(dve.reciprocal(rsum[:], O[:, :, :, HDL]))
                    for par in range(2):
                        ins = dve.tensor_tensor(o[:, :, par, :], O[:, par, :, 0:HDL],
                                                rsum[:, par, :].rearrange("p (c a) -> p c a", a=1).to_broadcast([P, 4, HDL]),
                                                ALU.mult)
                    ins.then_inc(o_made, 1)
                dve.wait_ge(y_made, i + 2)
                dve.tensor_tensor(x_b, ps[:, 7, :].rearrange("p (t d) -> p t d", t=T), x_b, ALU.add).then_inc(x_made, 1)
                link.close()
            dve.wait_ge(x_made, B + 1)



KEEP = (256, 128)
FETCH = tuple(min(k * 9.0 / 8.0, S) for k in KEEP)
N_ITERS = 50
OUTER, INNER = 7, 7
CAP = 80.0
ROUTES = 2 * B


def routing(nc, g):
    with ExitStack() as ctx:
        m = Mem(nc, ctx, "rt_")
        ps = g.ps
        s = m.sb("s", [P, 64])
        E = m.sb("E", [P, 64])
        low = m.sb("low", [P, 64])
        part = m.sb("part", [P, 1])
        col = m.sb("col", [P, 8])
        cols_i = m.sb("cols_i", [P, 2], I32)
        row = m.sb("row", [1, P])
        rmax = m.sb("rmax", [1, ROUTES])
        kblk = m.sb("kblk", [P, P])
        sc = m.sb("sc", [ROUTES, S])
        work = m.sb("work", [ROUTES, S])
        work2 = m.sb("work2", [ROUTES, S])
        top = m.sb("top", [ROUTES, 8])
        picked = m.sb("picked", [ROUTES, S])
        count = m.sb("count", [ROUTES, S])
        ones = m.sb("ones", [ROUTES, S])
        kept = m.sb("kept", [ROUTES, S])
        (loaded, dch, dch_loop, dch_end, maxed, max_turned, row_made, max_spread, r_made, exped, summed, parted, score_made, score_out,
         score_in, pos_made, pos_turned, ones_set) = (m.sem(n) for n in (
            "loaded dch dch_loop dch_end maxed max_turned row_made max_spread r_made exped summed parted score_made score_out "
            "score_in pos_made pos_turned ones_set").split())
        NA, NA1, C, NEG_R, RC, MX = range(6)
        block = ctx.enter_context(nc.Block())

        @block.sync
        def _(sp):
            for turns in (summed,):
                sp.sem_inc(turns, 1)
            sp.dma_start(s[:], g.s_dram.rearrange("r b (e n) -> (r b e) n", e=8)).then_inc(loaded, 16)
            sp.wait_ge(score_made, 1)
            sp.dma_start(g.sc_dram.rearrange("r (e n) -> (r e) n", e=8), E[:]).then_inc(score_out, 16)
            sp.wait_ge(score_out, 16)
            sp.dma_start(sc[:], g.sc_dram).then_inc(score_in, 16)

        @block.gpsimd
        def _(pool):
            pool.memset(ones[:], 1.0).then_inc(ones_set, 1)

        @block.tensor
        def _(pe):
            pe.wait_ge(maxed, 1)
            pe.transpose(ps[0:1, 0, 0:P], col[:, MX:MX + 1], g.ident[:]).then_inc(max_turned, 1)
            pe.wait_ge(row_made, 1)
            pe.matmul(ps[:, 1, 0:1], lhsT=row[:], rhs=g.ones[0:1, 0:1], start=True, stop=True).then_inc(max_spread, 1)
            with pe.Fori(0, OUTER) as i:
                for j in range(INNER):
                    pe.wait_ge(parted, i * INNER + j + 1)
                    pe.matmul(ps[:, 2, 0:1], lhsT=kblk[:], rhs=part[:], start=True, stop=True).then_inc(summed, 1)
            pe.wait_ge(pos_made, 2)
            for t in range(T):
                pe.transpose(ps[:, 3, t * ROUTES:(t + 1) * ROUTES], count[:, t * P:(t + 1) * P],
                             g.ident[0:ROUTES, 0:ROUTES])
                ins = pe.transpose(ps[:, 4, t * ROUTES:(t + 1) * ROUTES], kept[:, t * P:(t + 1) * P],
                                   g.ident[0:ROUTES, 0:ROUTES])
            ins.then_inc(pos_turned, 1)

        @block.scalar
        def _(act):
            act.wait_ge(r_made, 1)
            act.activation(col[:, C:C + 1], col[:, NA:NA + 1], ACT.Exp)
            act.activation(E[:], low[:], ACT.Exp).then_inc(exped, 1)
            with act.Fori(0, OUTER) as i:
                act.wait_ge(r_made, i + 2)
                act.activation(E[:], low[:], ACT.Exp).then_inc(exped, 1)

        @block.vector
        def _(dve):
            link = Chain(dve, dch)
            half = P // 2
            for rows, k in ((slice(0, half), FETCH[0]), (slice(half, P), FETCH[1])):
                dve.memset(col[rows, NA1:NA1 + 1], math.log(S) - math.log(k))
                link(dve.tensor_scalar(kblk[rows, :], g.blk[rows, :], 1.0 / k, None, ALU.mult))
            dve.wait_ge(loaded, 16)
            dve.tensor_reduce(col[:, MX:MX + 1], s[:], AX.X, ALU.max).then_inc(maxed, 1)
            dve.wait_ge(max_turned, 1)
            link(dve.tensor_reduce(rmax[:], ps[0:1, 0, 0:P].rearrange("p (r e) -> p r e", e=8), AX.X, ALU.max))
            dve.tensor_copy(row[:].rearrange("p (r e) -> p r e", e=8),
                            rmax[:].rearrange("p (r a) -> p r a", a=1).to_broadcast([1, ROUTES, 8])).then_inc(row_made, 1)
            dve.wait_ge(max_spread, 1)
            neg_r = col[:, NEG_R:NEG_R + 1]
            link(dve.tensor_scalar(neg_r, ps[:, 1, 0:1], col[:, NA1:NA1 + 1], -1.0, ALU.min, ALU.mult))
            dve.tensor_scalar(col[:, NA:NA + 1], col[:, NA1:NA1 + 1], neg_r, CAP, ALU.add, ALU.min)
            dve.tensor_scalar(low[:], s[:], neg_r, CAP, ALU.add, ALU.min).then_inc(r_made, 1)
            dve.wait_ge(exped, 1)
            with dve.Fori(0, OUTER) as i:
                link = Chain(dve, dch_loop, i, 4)
                for j in range(INNER):
                    if j == 0:
                        dve.wait_ge(exped, i + 1)
                        c = col[:, C:C + 1]
                    else:
                        dve.wait_ge(summed, i * INNER + j + 1)
                        c = ps[:, 2, 0:1]
                    dve.tensor_scalar(low[:], E[:], c, 0.0, ALU.min, ALU.add, accum_out=part[:]).then_inc(parted, 1)
                dve.wait_ge(summed, i * INNER + INNER + 1)
                link(dve.tensor_copy(col[:, RC:RC + 1], ps[:, 2, 0:1]))
                bits = col[:, RC:RC + 1].bitcast(I32)
                dve.tensor_scalar(cols_i[:, 0:1], bits, 23, None, ALU.logical_shift_right)
                link(dve.tensor_scalar(col[:, C:C + 1].bitcast(I32), bits, 0x7FFFFF, 0x3F800000, ALU.bitwise_and,
                                       ALU.bitwise_or))
                link(dve.tensor_scalar(col[:, NA:NA + 1], cols_i[:, 0:1], 127.0, math.log(2.0), ALU.subtract, ALU.mult))
                link(dve.tensor_tensor(neg_r, neg_r, col[:, NA:NA + 1], ALU.subtract))
                dve.tensor_scalar(low[:], s[:], neg_r, CAP, ALU.add, ALU.min).then_inc(r_made, 1)
            link = Chain(dve, dch_end)
            link(dve.reciprocal(col[:, RC:RC + 1], col[:, C:C + 1]))
            dve.wait_ge(exped, OUTER + 1)
            dve.tensor_scalar(E[:], E[:], col[:, RC:RC + 1], 1.0, ALU.mult, ALU.min).then_inc(score_made, 1)
            dve.wait_ge(score_in, 16)
            src = sc
            for k in range(KEEP[0] // 8):
                rows = slice(0, ROUTES) if k < KEEP[1] // 8 else slice(0, B)
                link(dve.max(top[rows, :], src[rows, :]))
                link(dve.match_replace(work[rows, :], top[rows, :], src[rows, :], -1.0))
                src = work
            link(dve.tensor_scalar(picked[:], work[:], 0.0, None, ALU.is_lt))
            dve.wait_ge(ones_set, 1)
            link(dve.tensor_tensor_scan(count[:], ones[:], picked[:], 0.0, ALU.mult, ALU.add))
            link(dve.tensor_tensor(count[:], count[:], picked[:], ALU.mult))
            dve.tensor_scalar(count[:], count[:], -1.0, None, ALU.add).then_inc(pos_made, 1)
            link(dve.tensor_scalar(kept[:], sc[:], -1.0, 1.0, ALU.mult, ALU.add))
            dve.tensor_tensor(kept[:], kept[:], sc[:], ALU.add).then_inc(pos_made, 1)
            dve.wait_ge(pos_turned, 1)
            link(dve.tensor_copy(g.place[:], ps[:, 3, 0:T * ROUTES].rearrange("p (t r) -> p t r", t=T)))
            link(dve.tensor_copy(g.weight[:], ps[:, 4, 0:T * ROUTES].rearrange("p (t r) -> p t r", t=T)))


def heavy(nc, g, out):
    HL, HDL = 8, 64
    NK, NQ = KEEP
    KT = NK // P
    with ExitStack() as ctx:
        m = Mem(nc, ctx, "hv_")
        ps = g.ps
        pick = m.sb("pick", [P, T, NK + NQ])
        xg = m.sb("xg", [P, NK + NQ])
        wk = m.sb("wk", [P, KT])
        xgT = m.sb("xgT", [P, NK + NQ])
        q = m.sb("q", [P, 4, NQ])
        k = m.sb("k", [P, 4, NK])
        v = m.sb("v", [P, KT, HL, HDL + 1])
        mx = m.sb("mx", [P, 8])
        mrest = m.sb("mrest", [P, 8])
        mpart = m.sb("mpart", [P, 3, 8], BF16)
        mT = m.sb("mT", [24, P], BF16)
        PT = m.sb("PT", [P, 2, KT, S])
        rsum = m.sb("rsum", [P, 2, 4])
        o = m.sb("o", [P, 4, 2, HDL])
        oT = m.sb("oT", [P, 4, P])
        y = m.sb("y", [P, P])
        pickT = m.sb("pickT", [P, S])
        (dch, ones_set, picked, gathered, xg_made, xg_turned, xgT_made, projected, qkv_made, scored, maxed, m_turned,
         mT_made, st_made, exped, pv_done, o_made, o_turned, oT_made, y_done, y_made, scattered, x_made, stored) = (
            m.sem(n) for n in (
                "dch ones_set picked gathered xg_made xg_turned xgT_made projected qkv_made scored maxed m_turned "
                "mT_made st_made exped pv_done o_made o_turned oT_made y_done y_made scattered x_made stored").split())
        block = ctx.enter_context(nc.Block())

        @block.sync
        def _(sp):
            for turns in (x_made, xg_turned):
                sp.sem_inc(turns, 1)
            with sp.Fori(0, B) as i:
                sp.wait_ge(x_made, i + 2)
                sp.dma_start(out[bass.ds(i, 1)].rearrange("b (t p) d -> p (b t) d", p=P),
                             g.xs[:, bass.ds(i * T, T), :]).then_inc(stored, 16)
            sp.wait_ge(stored, 16 * B)

        @block.tensor
        def _(pe):
            with pe.Fori(0, B) as i:
                pe.wait_ge(picked, i + 1)
                pe.wait_ge(x_made, i + 1)
                for j in range(KT + 1):
                    for t in range(T):
                        pe.matmul(ps[:, 0, j * P:(j + 1) * P], lhsT=pick[:, t, j * P:(j + 1) * P],
                                  rhs=g.xr[:, bass.ds(i * T + t, 1), :], start=t == 0, stop=t == T - 1)
                for j in range(KT):
                    for t in range(T):
                        ins = pe.matmul(ps[:, 1, j:j + 1], lhsT=pick[:, t, j * P:(j + 1) * P],
                                        rhs=g.weight[:, t, bass.ds(i, 1)], start=t == 0, stop=t == T - 1)
                ins.then_inc(gathered, 1)
                pe.wait_ge(xg_made, i + 1)
                for j in range(KT + 1):
                    pe.transpose(ps[:, 2, j * P:(j + 1) * P], xg[:, j * P:(j + 1) * P], g.ident[:])
                for t in range(T):
                    ins = pe.transpose(ps[:, 7, t * P:(t + 1) * P], pick[:, t, NK:NK + NQ], g.ident[:])
                ins.then_inc(xg_turned, 1)
                pe.wait_ge(xgT_made, i + 1)
                for c in range(4):
                    pe.matmul(ps[:, 3, c * NQ:(c + 1) * NQ], lhsT=g.wqh[:, c * P:(c + 1) * P], rhs=xgT[:, NK:NK + NQ],
                              start=True, stop=True)
                for c in range(4):
                    pe.matmul(ps[:, c // 2, (c % 2) * NK:(c % 2 + 1) * NK], lhsT=g.wkh[:, c * P:(c + 1) * P],
                              rhs=xgT[:, 0:NK], start=True, stop=True)
                for j in range(KT):
                    ins = pe.matmul(ps[:, 4 + j, :], lhsT=xgT[:, j * P:(j + 1) * P], rhs=g.wvh[:], start=True, stop=True)
                ins.then_inc(projected, 1)
                pe.wait_ge(qkv_made, i * 3 + 3)
                for h in range(HL):
                    c, par = divmod(h, 2)
                    rows = slice(64 * par, 64 * par + 64)
                    ins = pe.matmul(ps[:, 2 * par + c // 2, (c % 2) * NK:(c % 2 + 1) * NK], lhsT=q[rows, c, :],
                                    rhs=k[rows, c, :], start=True, stop=True)
                ins.then_inc(scored, 1)
                pe.wait_ge(maxed, i + 1)
                pe.transpose(ps[:, 6, 0:64].bitcast(BF16)[0:24, 0:P], mpart[:], g.identb[:]).then_inc(m_turned, 1)
                pe.wait_ge(mT_made, i + 1)
                for j in range(KT):
                    for h in range(HL):
                        c, par = divmod(h, 2)
                        rows = slice(64 * par, 64 * par + 64)
                        dst = ps[:, 2 * par + j, c * P:(c + 1) * P]
                        pe.matmul(dst, lhsT=k[rows, c, j * P:(j + 1) * P], rhs=q[rows, c, :], start=True, stop=False)
                        ins = pe.matmul(dst, lhsT=g.selm[:, par * 4 + c, :], rhs=mT[:], start=False, stop=True)
                ins.then_inc(st_made, 1)
                pe.wait_ge(exped, i + 1)
                for h in range(HL):
                    c, par = divmod(h, 2)
                    for j in range(KT):
                        ins = pe.matmul(ps[:, 4 + par, c * (HDL + 1):(c + 1) * (HDL + 1)],
                                        lhsT=PT[:, par, j, c * P:(c + 1) * P], rhs=v[:, j, h, :],
                                        start=j == 0, stop=j == KT - 1)
                ins.then_inc(pv_done, 1)
                pe.wait_ge(o_made, i + 1)
                for c in range(4):
                    ins = pe.transpose(ps[:, 6, c * P:(c + 1) * P], o[:, c, :, :], g.ident[:])
                ins.then_inc(o_turned, 1)
                pe.wait_ge(oT_made, i + 1)
                for c in range(4):
                    ins = pe.matmul(ps[:, 0, 0:P], lhsT=oT[:, c, :], rhs=g.woh[:, c, :], start=c == 0, stop=c == 3)
                ins.then_inc(y_done, 1)
                pe.wait_ge(y_made, i + 1)
                for t in range(T):
                    ins = pe.matmul(ps[:, 1, t * P:(t + 1) * P], lhsT=pickT[:, t * P:(t + 1) * P], rhs=y[:],
                                    start=True, stop=True)
                ins.then_inc(scattered, 1)

        @block.scalar
        def _(act):
            with act.Fori(0, B) as i:
                act.wait_ge(gathered, i + 1)
                act.copy(wk[:], ps[:, 1, 0:KT])
                act.copy(xg[:], ps[:, 0, 0:NK + NQ]).then_inc(xg_made, 1)
                act.wait_ge(xg_turned, i + 2)
                act.activation(xgT[:], ps[:, 2, 0:NK + NQ], ACT.Identity, bias=0.0, scale=g.gh[:]).then_inc(xgT_made, 1)
                act.copy(pickT[:], ps[:, 7, :])
                act.wait_ge(projected, i + 1)
                act.mul(q[:], ps[:, 3, :].rearrange("p (c n) -> p c n", c=4), HDL ** -0.5).then_inc(qkv_made, 1)
                act.copy(k[:], ps[:, 0:2, :].rearrange("p b (c n) -> p (b c) n", c=2)).then_inc(qkv_made, 1)
                act.wait_ge(m_turned, i + 1)
                act.copy(mT[:], ps[:, 6, 0:64].bitcast(BF16)[0:24, 0:P]).then_inc(mT_made, 1)
                act.wait_ge(st_made, i + 1)
                act.activation(PT[:], ps[:, 0:4, :].rearrange("p (a j) n -> p a j n", a=2), ACT.Exp).then_inc(exped, 1)
                act.wait_ge(o_turned, i + 1)
                act.copy(oT[:], ps[:, 6, :]).then_inc(oT_made, 1)
                act.wait_ge(y_done, i + 1)
                act.copy(y[:], ps[:, 0, 0:P]).then_inc(y_made, 1)

        @block.vector
        def _(dve):
            link = Chain(dve, ones_set)
            link(dve.memset(v[:], 1.0))
            with dve.Fori(0, B) as i:
                link = Chain(dve, dch, i, 5)
                dve.wait_ge(xg_turned, i + 1)
                for t in range(T):
                    dve.tensor_scalar(pick[:, t, 0:NK], g.iota[:], g.place[:, t, bass.ds(i, 1)], None, ALU.is_equal)
                    ins = dve.tensor_scalar(pick[:, t, NK:NK + NQ], g.iota[:, 0:NQ], g.place[:, t, bass.ds(i + B, 1)],
                                            None, ALU.is_equal)
                ins.then_inc(picked, 1)
                dve.wait_ge(projected, i + 1)
                dve.wait_ge(xg_made, i + 1)
                for j in range(KT):
                    ins = dve.tensor_scalar(v[:, j, :, 0:HDL], ps[:, 4 + j, :].rearrange("p (h d) -> p h d", h=HL),
                                            wk[:, j:j + 1], None, ALU.mult)
                ins.then_inc(qkv_made, 1)
                dve.wait_ge(scored, i + 1)
                link(dve.tensor_reduce(mx[:], ps[:, 0:4, :].rearrange("p b (c k) -> p (b c) k", c=2), AX.X, ALU.max))
                link(dve.tensor_copy(mpart[:, 0, :], mx[:]))
                link(dve.tensor_tensor(mrest[:], mx[:], mpart[:, 0, :], ALU.subtract))
                link(dve.tensor_copy(mpart[:, 1, :], mrest[:]))
                dve.tensor_tensor(mpart[:, 2, :], mrest[:], mpart[:, 1, :], ALU.subtract).then_inc(maxed, 1)
                dve.wait_ge(pv_done, i + 1)
                O = ps[:, 4:6, 0:4 * (HDL + 1)].rearrange("p b (c d) -> p b c d", c=4)
                link(dve.reciprocal(rsum[:], O[:, :, :, HDL]))
                for par in range(2):
                    ins = dve.tensor_tensor(o[:, :, par, :], O[:, par, :, 0:HDL],
                                            rsum[:, par, :].rearrange("p (c a) -> p c a", a=1).to_broadcast([P, 4, HDL]),
                                            ALU.mult)
                ins.then_inc(o_made, 1)
                dve.wait_ge(scattered, i + 1)
                for t in range(T):
                    x_t = g.xs[:, bass.ds(i * T + t, 1), :]
                    ins = dve.scalar_tensor_tensor(x_t, ps[:, 1, t * P:(t + 1) * P].rearrange("p (a d) -> p a d", a=1),
                                                   g.weight[:, t, bass.ds(i + B, 1)], x_t, ALU.mult, ALU.add)
                ins.then_inc(x_made, 1)
                link.close()
            dve.wait_ge(x_made, B + 1)


class Shared:

    def __init__(self, nc, ctx):
        m = Mem(nc, ctx)
        self.ps = ctx.enter_context(nc.psum_tensor("ps", [P, 8, 512], F32))
        self.xs = m.sb("xs", [P, B * T, P])
        self.ident = m.sb("ident", [P, P])
        self.identb = m.sb("identb", [P, P], BF16)
        self.maskb = m.sb("maskb", [P, 2, P], BF16)
        self.ones = m.sb("ones", [P, P])
        self.blk = m.sb("blk", [P, P])
        self.iota = m.sb("iota", [P, 256])
        self.selm = m.sb("selm", [24, 8, P], BF16)
        self.mbeta = m.sb("mbeta", [P, 11, P])
        self.wt = m.sb("wt", [P, 8, P])
        self.wkh, self.wvh = m.sb("wkh", [P, 512]), m.sb("wvh", [P, 512])
        self.ws1, self.ws2, self.wr = m.sb("ws1", [P, 64]), m.sb("ws2", [64, P]), m.sb("wr", [P, 8])
        self.w1, self.w2 = m.sb("w1", [P, 8, 64]), m.sb("w2", [P, 4, P])
        self.bqkv, self.bv, self.bo = m.sb("bqkv", [P, 3]), m.sb("bv", [P, P]), m.sb("bo", [P, P])
        self.gl, self.gh, self.tok = m.sb("gl", [P, 1]), m.sb("gh", [P, 1]), m.sb("tok", [P, 2])
        self.wql, self.wkvl, self.wol = m.sb("wql", [P, 512]), m.sb("wkvl", [P, 1024]), m.sb("wol", [P, 4, P])
        self.wqh, self.woh = m.sb("wqh", [P, 512]), m.sb("woh", [P, 4, P])
        self.logits = m.sb("logits", [P, B * T, 8])
        self.gate = m.sb("gate", [P, B * T, 8])
        self.any_gate = m.sb("any_gate", [P, 1], I32)
        self.xnT_all = m.sb("kept_x", [P, B * S])
        self.xr = self.xnT_all[:].rearrange("p (n d) -> p n d", d=D)
        self.place = m.sb("place", [P, T, 2 * B])
        self.weight = m.sb("weight", [P, T, 2 * B])
        self.s_dram = nc.dram_tensor("s_dram", [2, B, S], F32).ap()
        self.sc_dram = nc.dram_tensor("sc_dram", [2 * B, S], F32).ap()


def build(nc, w, out):
    with ExitStack() as ctx:
        g = Shared(nc, ctx)
        setup(nc, g, w)
        layer0(nc, g, w)
        gates(nc, g)
        routed_experts(nc, g)
        layer1(nc, g)
        routing(nc, g)
        heavy(nc, g, out)


_INS = ['L0_attn_x', 'L0_attn_w_qkv', 'L0_attn_b_qkv', 'L0_attn_w_out', 'L0_attn_b_out', 'L0_ffn_Ws1', 'L0_ffn_Ws2',
        'L0_ffn_W1', 'L0_ffn_W2', 'L0_ffn_Wr', 'L1_attn_w_in', 'L1_attn_w_out', 'L1_attn_beta', 'L1_ffn_gamma_light',
        'L1_ffn_wq_light', 'L1_ffn_wkv_light', 'L1_ffn_wo_light', 'L1_ffn_q_routing_token',
        'L1_ffn_kv_routing_token', 'L1_ffn_gamma_heavy', 'L1_ffn_wq_heavy', 'L1_ffn_wkv_heavy', 'L1_ffn_wo_heavy']


def kernel(**inputs):
    import numpy as _np
    import concourse.bacc as _bacc
    from concourse.bass_utils import run_bass_kernel_spmd as _run

    nc = _bacc.Bacc("TRN2", target_bir_lowering=False, num_devices=1)
    arrays, args = {}, {}
    for name in _INS:
        a = _np.ascontiguousarray(inputs[name])
        arrays[f"in_{name}_dram"] = a
        args[name] = nc.dram_tensor(f"in_{name}_dram", a.shape, mybir.dt.from_np(a.dtype), kind="ExternalInput").ap()
    out = nc.dram_tensor("out_0_dram", (B, S, D), F32, kind="ExternalOutput").ap()
    build(nc, args, out)
    r = _run(nc, [arrays], core_ids=[0])
    return r.results[0]["out_0_dram"]
```

```python
import math
from contextlib import ExitStack

import concourse.bass as bass
from concourse import mybir
from concourse.alu_op_type import AluOpType as ALU

ACT = mybir.ActivationFunctionType
F32 = mybir.dt.float32
BF16 = mybir.dt.bfloat16
I32 = mybir.dt.int32
AX = mybir.AxisListType

P = 128
B, S, D = 8, 512, 128
T = S // P
H0, HD0 = 16, 8
NEG = -1e30
EPS = 1e-5

Q_PART = (0, 0, 1, 1, 0, 2)
K_PART = (0, 1, 0, 1, 2, 0)
ROW_POS = HD0 * len(Q_PART)
ROW_MAX = ROW_POS + 1
ROWS = ROW_MAX + 3


class Chain:

    def __init__(self, eng, sem, turn=0, per=0):
        self.eng, self.sem, self.base, self.per, self.n = eng, sem, turn * per, per, 0

    def __call__(self, ins, held=None):
        self.n += 1
        ins.then_inc(self.sem, 1)
        self.eng.wait_ge(self.sem, self.base + self.n)
        if held is not None:
            self.eng.sem_inc(held, 1)

    def close(self):
        assert self.per in (0, self.n), (self.per, self.n)


def inv_sqrt(dve, link, v, y, t, half):
    if half == 0:
        link(dve.tensor_scalar(y.bitcast(I32), v.bitcast(I32), 1, None, ALU.logical_shift_right))
        link(dve.tensor_scalar(y.bitcast(I32), y.bitcast(I32), -1.0, float(0x5F3759DF), ALU.mult, ALU.add))
    for _ in range(2):
        link(dve.tensor_tensor(t, y, y, ALU.mult))
        link(dve.scalar_tensor_tensor(t, t, -0.5, v, ALU.mult, ALU.mult))
        link(dve.scalar_tensor_tensor(y, t, 1.5, y, ALU.add, ALU.mult))


class Mem:

    def __init__(self, nc, ctx, phase=""):
        self.nc, self.ctx, self.phase, self.sems = nc, ctx, phase, []

    def sb(self, name, shape, dt=F32):
        return self.ctx.enter_context(self.nc.sbuf_tensor(self.phase + name, shape, dt))

    def sem(self, name):
        sem = self.ctx.enter_context(self.nc.semaphore(self.phase + name))
        self.sems.append(sem.num)
        return sem


LATE_LOADS = 11


def setup(nc, g, w):
    with ExitStack() as ctx:
        m = Mem(nc, ctx)
        nat = m.sb("nat", [P, 16, P])
        loaded, w_loaded, ident_made, ident_b, turned, moved, made, beta_ld, mb = (m.sem(n) for n in (
            "loaded", "w_loaded", "ident_made", "ident_b", "turned", "moved", "made", "beta_ld", "mb"))
        g.spent_sems = range(min(m.sems), max(m.sems) + 1)
        betac = m.sb("betac", [P, 11])
        block = ctx.enter_context(nc.Block())
        ps = g.ps

        @block.sync
        def _(sp):
            with nc.allow_non_contiguous_dma(reason="columns of small vectors"):
                sp.dma_start(nat[:, 0:3, :], w["L0_attn_w_qkv"].rearrange("(c p) d -> p c d", p=P)).then_inc(w_loaded, 16)
                sp.dma_start(nat[:, 3, :], w["L0_attn_w_out"]).then_inc(w_loaded, 16)
                sp.dma_start(nat[:, 4:7, :], w["L1_attn_w_in"].rearrange("(c p) d -> p c d", p=P)).then_inc(w_loaded, 16)
                sp.dma_start(nat[:, 7, :], w["L1_attn_w_out"]).then_inc(w_loaded, 16)
                sp.dma_start(nat[:, 8:16, :], w["L1_ffn_wkv_heavy"].rearrange("(c p) d -> p c d", p=P)).then_inc(w_loaded, 16)
                n = 0
                x = w["L0_attn_x"].rearrange("b (t p) d -> p (b t) d", p=P)
                for dst, src in (
                    (g.xs[:, 0:2 * T, :], x[:, 0:2 * T, :]),
                    (g.ws1[:], w["L0_ffn_Ws1"]), (g.ws2[:], w["L0_ffn_Ws2"]), (g.wr[:], w["L0_ffn_Wr"]),
                    (g.bqkv[:], w["L0_attn_b_qkv"].rearrange("(c p) -> p c", p=P)),
                    (g.bv[:], w["L0_attn_b_qkv"][2 * P:3 * P].rearrange("(a d) -> a d", a=1).to_broadcast([P, P])),
                    (g.bo[:], w["L0_attn_b_out"].rearrange("(a d) -> a d", a=1).to_broadcast([P, P])),
                ):
                    sp.dma_start(dst, src).then_inc(loaded, 16)
                    n += 1
                sp.dma_start(betac[:], w["L1_attn_beta"].rearrange("h (a m) -> h a m", a=1)
                             .to_broadcast([H0, HD0, 11])).then_inc(beta_ld, 16)
            sp.wait_ge(loaded, 16 * n)

        @block.scalar
        def _(act):
            with nc.allow_non_contiguous_dma(reason="columns of small vectors"):
                x = w["L0_attn_x"].rearrange("b (t p) d -> p (b t) d", p=P)
                act.dma_start(g.xs[:, 2 * T:B * T, :], x[:, 2 * T:B * T, :]).then_inc(g.x_loaded, 16)
                for dst, src in (
                    (g.w1[:], w["L0_ffn_W1"].rearrange("e d f -> d e f")),
                    (g.w2[:], w["L0_ffn_W2"].rearrange("(c e) f d -> (e f) c d", e=2)),
                    (g.gl[:], w["L1_ffn_gamma_light"].rearrange("(p a) -> p a", a=1)),
                    (g.gh[:], w["L1_ffn_gamma_heavy"].rearrange("(p a) -> p a", a=1)),
                    (g.tok[:, 0:1], w["L1_ffn_kv_routing_token"].rearrange("(p a) -> p a", a=1)),
                    (g.tok[:, 1:2], w["L1_ffn_q_routing_token"].rearrange("(p a) -> p a", a=1)),
                    (g.wql[:], w["L1_ffn_wq_light"]), (g.wkvl[:], w["L1_ffn_wkv_light"]),
                    (g.wol[:], w["L1_ffn_wo_light"].rearrange("(c p) d -> p c d", p=P)),
                    (g.wqh[:], w["L1_ffn_wq_heavy"]),
                    (g.woh[:], w["L1_ffn_wo_heavy"].rearrange("(c p) d -> p c d", p=P)),
                ):
                    act.dma_start(dst, src).then_inc(g.late_loaded, 16)

        @block.gpsimd
        def _(pool):
            pool.memset(g.ident[:], 1.0).then_inc(made, 1)
            pool.memset(g.maskb[:], 0.0).then_inc(made, 1)
            pool.memset(g.ones[:], 1.0).then_inc(made, 1)
            pool.memset(g.blk[:], 1.0).then_inc(made, 1)
            pool.wait_ge(made, 4)
            pool.affine_select(out=g.ident[:], in_=g.ident[:], compare_op=ALU.is_equal, fill=0.0, base=0,
                               pattern=[[-1, P]], channel_multiplier=1).then_inc(ident_made, 1)
            pool.affine_select(out=g.maskb[:, 0, :], in_=g.maskb[:, 0, :], compare_op=ALU.is_ge, fill=NEG, base=0,
                               pattern=[[-1, P]], channel_multiplier=1).then_inc(made, 1)
            pool.affine_select(out=g.maskb[:, 1, :], in_=g.maskb[:, 1, :], compare_op=ALU.is_ge, fill=NEG, base=0,
                               pattern=[[1, P]], channel_multiplier=-1).then_inc(made, 1)
            pool.affine_select(out=g.blk[:], in_=g.blk[:], compare_op=ALU.is_ge, fill=0.0, base=0,
                               pattern=[[-HD0, H0], [0, HD0]], channel_multiplier=1).then_inc(made, 1)
            pool.wait_ge(made, 7)
            pool.affine_select(out=g.blk[:], in_=g.blk[:], compare_op=ALU.is_ge, fill=0.0, base=HD0 - 1,
                               pattern=[[HD0, H0], [0, HD0]], channel_multiplier=-1).then_inc(made, 1)
            pool.iota(g.iota[:], pattern=[[1, 256]], base=0, channel_multiplier=0,
                      allow_small_or_imprecise_dtypes=True).then_inc(made, 1)
            pool.memset(g.selm[:], 0.0).then_inc(made, 1)
            for c in range(3):
                pool.wait_ge(made, 10 + c)
                pool.affine_select(out=g.selm[:], in_=g.selm[:], compare_op=ALU.not_equal, fill=-1.0, base=-8 * c,
                                   pattern=[[-1, 8], [0, P]], channel_multiplier=1).then_inc(made, 1)
            pool.wait_ge(made, 13)
            pool.wait_ge(ident_made, 1)
            pool.tensor_copy(g.identb[:], g.ident[:]).then_inc(ident_b, 1)
            pool.wait_ge(made, 9)
            pool.wait_ge(ident_b, 1)

        @block.tensor
        def _(pe):
            pe.wait_ge(ident_made, 1)
            pe.wait_ge(w_loaded, 80)
            for c in range(16):
                ins = pe.transpose(ps[:, c // 4, (c % 4) * P:(c % 4 + 1) * P], nat[:, c, :], g.ident[:])
            ins.then_inc(turned, 1)

        @block.vector
        def _(dve):
            dve.wait_ge(turned, 1)
            dve.tensor_copy(g.wt[:, 0:4, :], ps[:, 0, :]).then_inc(moved, 1)
            dve.tensor_copy(g.wt[:, 4:8, :], ps[:, 1, :]).then_inc(moved, 1)
            for c in (0, 1):
                heads = ps[:, 2 + c, :].rearrange("p (h k d) -> p h k d", h=4, k=2)
                for k, dst in ((0, g.wkh), (1, g.wvh)):
                    dve.tensor_copy(dst[:, c * 256:c * 256 + 256].rearrange("p (h d) -> p h d", h=4),
                                    heads[:, :, k, :]).then_inc(moved, 1)
            dve.wait_ge(made, 9)
            dve.wait_ge(beta_ld, 16)
            for k in range(11):
                dve.tensor_scalar(g.mbeta[:, k, :], g.blk[:], betac[:, k:k + 1], None, ALU.mult).then_inc(mb, 1)
            dve.wait_ge(mb, 11)
            dve.wait_ge(moved, 6)



PRIME = 3


def upto(b, per, n):
    value = b * per + n + PRIME
    return max(value, 1) if isinstance(value, int) else value


def pipelined(eng, turn, plan):
    turn(-2, plan(False, False, True), 0)
    turn(-1, plan(False, True, True), 1)
    with eng.Fori(0, (B - 2) // 2) as j:
        turn(j * 2, plan(True, True, True), 0, j)
        turn(j * 2 + 1, plan(True, True, True), 1, j)
    turn(B - 2, plan(True, True, False), 0)
    turn(B - 1, plan(True, False, False), 1)


MAX_UNITS = [(3, (h,)) for h in range(4)] + [(2, (h,)) for h in range(4)] + [(1, (0, 1)), (1, (2, 3)), (0, (0, 1, 2, 3))]
GROUPS = H0 // 4
N_MAX = GROUPS * len(MAX_UNITS)
EXP_UNITS = ([[(h, 0, 0)] for h in range(4)] + [[(h, 1, 0), (h, 3, 3 * P)] for h in range(4)]
             + [[(h, 2, 0), (h + 1, 2, 2 * P)] for h in (0, 2)])
LAST_KT = 2
N_GRP = len(EXP_UNITS)
N_EXP = GROUPS * N_GRP
SLOTS = 3


L0_AT = {"v": 1, "hidden": 3, "logits": 4.8, "max": (4, 47.5), "parts": 0.3, "minus_max": 2.92, "norm": (0.5, 2.5, 3.5, 4.6), "turn": 8.9,
         "lay_out": 40, "project": (11.01, 18.9), "split": (1.54, 5), "weigh": 2.01, "scores": (-0.2, 40.5), "turn_out": 3.3,
         "out_turn": 46.1, "out_project": 48}


def l0_plan(p2, p1, front):
    at = {}

    def put(u, *step):
        at.setdefault(u, []).append(step)

    if p1:
        put(L0_AT["v"], "v"), put(L0_AT["hidden"], "hidden"), put(L0_AT["logits"], "logits")
        first, end = L0_AT["max"]
        step = (end - first) / N_MAX
        for k in range(N_MAX):
            put(first + k * step, "max", k)
        for grp in range(GROUPS):
            last = first + ((grp + 1) * len(MAX_UNITS) - 1) * step
            put(last + L0_AT["parts"], "parts", grp)
            put(last + L0_AT["minus_max"], "minus_max", grp)
    if front:
        [put(u, "norm", n) for n, u in enumerate(L0_AT["norm"])]
        put(L0_AT["turn"], "turn"), put(L0_AT["lay_out"], "lay_out")
        for n, u in enumerate(L0_AT["project"]):
            put(u, "project", n)
            for x, d in enumerate(L0_AT["split"]):
                put(u + d, "split", n, x)
    if p2:
        first, end = L0_AT["scores"]
        step = (end - first) / N_EXP
        for u in range(N_EXP):
            put(first + u * step, "scores", u)
            put(first + (u + L0_AT["weigh"]) * step, "weigh", u)
        for grp in range(GROUPS):
            put(first + (N_GRP * (grp + 1) + L0_AT["turn_out"]) * step, "turn_out", grp)
        put(L0_AT["out_turn"], "out_turn"), put(L0_AT["out_project"], "out_project")
    return [step for u in sorted(at) for step in at[u]]


def layer0(nc, g, w):
    with ExitStack() as ctx:
        m = Mem(nc, ctx, "l0_")
        ps = g.ps
        st = m.sb("bn_parts", [P, T, 6])
        mv = m.sb("mean_var", [P, T, 2])
        rstd = m.sb("rstd", [P, 3, T])
        xn = m.sb("xn", [P, T, P])
        xnT = m.sb("xnT", [P, S])
        full = m.sb("full", [P, S])
        rest = m.sb("rest", [P, S])
        part = m.sb("part", [P, 2, 3, S], BF16)
        qS = [m.sb(f"qS{a}", [ROWS, H0, S], BF16) for a in range(2)]
        kS = [m.sb(f"kS{a}", [ROWS, H0, S], BF16) for a in range(2)]
        fixed = m.sb("fixed", [1, 3, S], BF16)
        va = [m.sb(f"va{a}", [P, T, H0, 32]) for a in range(2)]
        bq = m.sb("bq", [P, 1])
        hr = m.sb("hr", [64, S])
        h2 = [m.sb(f"h2{a}", [64, S]) for a in range(2)]
        mx = m.sb("mx", [P, 2, T, 4])
        mrest = m.sb("mrest", [P, T, 4])
        mpart = m.sb("mpart", [P, T, 3, 4], BF16)
        mT = m.sb("mT", [12, S], BF16)
        PT = m.sb("PT", [P, SLOTS, S])
        OT = m.sb("OT", [P, S])
        rsum = m.sb("rsum", [P, T, 4])
        o = m.sb("o", [P, T, P])
        oT = m.sb("oT", [P, S])
        (xn_made, turned, xnT_made, qk_proj, full_made, rest_made, second_made, split, stored, laid,
         v_proj, v_made, h_proj, relu, squared, l_proj, l_made, scored, maxed, m_made, m_turned, mT_made, mlaid,
         st_made, exped, pv_done, OT_made, OT_turned, o_made, o_turned, oT_made, acc_made, x_made, x_bias, xnT_kept) = loop_sems = tuple(
            m.sem(n) for n in (
                "xn_made turned xnT_made qk_proj full_made rest_made second_made split stored laid "
                "v_proj v_made h_proj relu squared l_proj l_made scored maxed m_made m_turned mT_made mlaid "
                "st_made exped pv_done OT_made OT_turned o_made o_turned oT_made acc_made x_made x_bias xnT_kept").split())
        rows_set, rows_laid, v_set, bq_made, dch_pre, dch, dch_post, held = (
            m.sem(n) for n in "rows_set rows_laid v_set bq_made dch_pre dch dch_post held".split())
        BANK_M, BANK_S, BANK_O = 7, 2, 5
        by_feature = nc.dram_tensor("by_feature", [2, 3, P, S], BF16).ap()
        LOADS = 2 * len(Q_PART)
        EMPTIED = {"v": (v_made, 1), "hidden": (relu, 1), "logits": (l_made, 1), "minus_max": (mT_made, GROUPS),
                   "turn": (xnT_made, 1), "project": (full_made, 2), "turn_out": (o_made, GROUPS),
                   "out_turn": (oT_made, 1), "out_project": (x_made, 1)}
        AHEAD = {"v": 1, "hidden": 1, "logits": 1, "max": 1, "parts": 1, "minus_max": 1, "norm": 2, "turn": 2, "project": 2, "split": 2, "lay_out": 2,
                 "scores": 0, "weigh": 0, "turn_out": 0, "out_turn": 0, "out_project": 0}
        g.spent_sems = range(g.spent_sems.start, max(m.sems) + 1)
        block = ctx.enter_context(nc.Block())

        @block.sync
        def _(sp):
            for sem in loop_sems:
                sp.sem_inc(sem, PRIME)
            sp.wait_ge(rows_set, 3)
            for a in range(2):
                for rows, r, kind in [(kS[a], ROW_POS, 0), (qS[a], ROW_POS, 1)] + [(kS[a], ROW_MAX + c, 2) for c in range(3)]:
                    sp.dma_start(rows[r:r + 1, :, :], fixed[:, kind:kind + 1, :].to_broadcast([1, H0, S])).then_inc(rows_laid, 16)

            def turn(i, plan, a, j=None):
                for name, *idx in plan:
                    b = i + AHEAD[name]
                    n = idx[0] if idx else 0
                    if name == "minus_max":
                        sp.wait_ge(mT_made, upto(b, GROUPS, n + 1))
                        sp.dma_start(qS[1 - a][ROW_MAX:ROW_MAX + 3, 4 * n:4 * n + 4, :], mT[:]).then_inc(mlaid, 16)
                    elif name == "split" and idx[1] == 1:
                        sp.wait_ge(split, upto(b, 2, n + 1))
                        sp.dma_start(by_feature[n].rearrange("c p s -> p c s"), part[:, n, :, :]).then_inc(stored, 16)
                    elif name == "lay_out":
                        sp.wait_ge(stored, upto(b, 32, 32))
                        sp.sem_inc(held, 1)
                        sp.wait_ge(st_made, upto(b - 2, N_EXP, N_EXP) if j is not None else 1)
                        for rows, side, parts in ((qS[a], 0, Q_PART), (kS[a], 1, K_PART)):
                            for r, c in enumerate(parts):
                                sp.dma_start(rows[HD0 * r:HD0 * r + HD0, :, :],
                                             by_feature[side, c].rearrange("(h d) s -> d h s", d=HD0)).then_inc(laid, 16)

            pipelined(sp, turn, l0_plan)
            sp.wait_ge(mlaid, upto(B, 16 * GROUPS, 0))

        @block.gpsimd
        def _(pool):
            pool.iota(fixed[:, 0, :], pattern=[[1, S]], base=-S // 2, channel_multiplier=0,
                      allow_small_or_imprecise_dtypes=True).then_inc(rows_set, 1)
            pool.memset(fixed[:, 1, :], 1.0).then_inc(rows_set, 1)
            pool.memset(fixed[:, 2, :], -1.0).then_inc(rows_set, 1)
            for a in range(2):
                pool.memset(va[a][:, :, :, HD0:32], 0.0).then_inc(v_set, 1)
            pool.wait_ge(v_set, 2)
            for a in range(2):
                pool.memset(va[a][:, :, :, HD0:HD0 + 1], 1.0).then_inc(v_set, 1)

            def turn(i, plan, a, j=None):
                for name, *idx in plan:
                    b = i + AHEAD[name]
                    n = idx[0] if idx else 0
                    if name == "hidden":
                        pool.wait_ge(relu, upto(b, 1, 1))
                        pool.wait_ge(acc_made, upto(b - 1, 1, 0))
                        pool.tensor_tensor(h2[1 - a][:], hr[:], hr[:], ALU.mult).then_inc(squared, 1)
                    elif name == "norm" and n == 3:
                        pool.wait_ge(xn_made, upto(b, 1, 1))
                        x_b = g.xs[:, bass.ds(b * T, T), :]
                        pool.tensor_tensor(x_b, x_b, g.bo[:].rearrange("p (a d) -> p a d", a=1).to_broadcast([P, T, P]),
                                           ALU.add).then_inc(x_bias, 1)
                    elif name == "turn":
                        pool.wait_ge(xnT_made, upto(b, 1, 1))
                        pool.sem_inc(held, 1)
                        pool.tensor_copy(g.xnT_all[:, bass.ds(b * S, S)], xnT[:]).then_inc(xnT_kept, 1)

            pipelined(pool, turn, l0_plan)

        @block.tensor
        def _(pe):
            pe.wait_ge(v_set, 4)

            def turn(i, plan, a, j=None):
                before = []
                for parts in {-2: (), -1: ((False, False, True),), B - 1: ((True, True, False),)}.get(
                        i if j is None else 0, ((False, True, True), (True, True, True))):
                    name, *idx = [step for step in l0_plan(*parts) if step[0] in EMPTIED][-1]
                    before.append((name, i - 1 + AHEAD[name], idx[0] if idx else 0))
                for name, *idx in plan:
                    b = i + AHEAD[name]
                    n = idx[0] if idx else 0
                    if name in EMPTIED:
                        for last, of, k in before:
                            sem, per = EMPTIED[last]
                            pe.wait_ge(sem, upto(of, per, k + 1))
                        before = [(name, b, n)]
                    if name == "turn":
                        pe.wait_ge(xn_made, upto(b, 1, 1))
                        for t in range(T):
                            ins = pe.transpose(ps[:, BANK_M, t * P:(t + 1) * P], xn[:, t, :], g.ident[:])
                        ins.then_inc(turned, 1)
                    elif name == "project":
                        pe.wait_ge(xnT_made, upto(b, 1, 1))
                        pe.matmul(ps[:, BANK_M, :], lhsT=g.wt[:, n, :], rhs=xnT[:], start=True, stop=True).then_inc(qk_proj, 1)
                    elif name == "v":
                        for t in range(T):
                            ins = pe.matmul(ps[:, BANK_M, t * P:(t + 1) * P], lhsT=xnT[:, t * P:(t + 1) * P], rhs=g.wt[:, 2, :],
                                            start=True, stop=True)
                        ins.then_inc(v_proj, 1)
                    elif name == "hidden":
                        pe.matmul(ps[0:64, BANK_M, :], lhsT=g.ws1[:], rhs=xnT[:], start=True, stop=True).then_inc(h_proj, 1)
                    elif name == "logits":
                        for t in range(T):
                            ins = pe.matmul(ps[:, BANK_M, t * 8:(t + 1) * 8], lhsT=xnT[:, t * P:(t + 1) * P], rhs=g.wr[:],
                                            start=True, stop=True)
                        ins.then_inc(l_proj, 1)
                    elif name == "max":
                        grp, u = divmod(n, len(MAX_UNITS))
                        qt, heads = MAX_UNITS[u]
                        N = (qt + 1) * P
                        if n == 0:
                            pe.wait_ge(rows_laid, 16 * 10)
                            pe.wait_ge(laid, upto(b, 16 * LOADS, 16 * LOADS))
                        pe.wait_ge(maxed, upto(b, N_MAX, n - 1))
                        q, k = qS[1 - a], kS[1 - a]
                        for x, hh in enumerate(heads):
                            h = 4 * grp + hh
                            pe.matmul(ps[:, n % 2, x * N:(x + 1) * N], lhsT=q[0:ROW_MAX, h, qt * P:(qt + 1) * P],
                                      rhs=k[0:ROW_MAX, h, 0:N], start=True, stop=False)
                            ins = pe.matmul(ps[:, n % 2, (x + 1) * N - P:(x + 1) * N], lhsT=g.identb[:], rhs=g.maskb[:, 0, :],
                                            start=False, stop=True)
                        ins.then_inc(scored, 1)
                    elif name == "minus_max":
                        pe.wait_ge(m_made, upto(b, GROUPS, n + 1))
                        for t in range(T):
                            ins = pe.transpose(ps[:, BANK_M, :].bitcast(BF16)[0:12, t * P:(t + 1) * P], mpart[:, t, :, :],
                                               g.identb[:])
                        ins.then_inc(m_turned, 1)
                    elif name == "scores":
                        grp, u = divmod(n, N_GRP)
                        if u == 0:
                            pe.wait_ge(mlaid, upto(b, 16 * GROUPS, 16 * (grp + 1)))
                        pe.wait_ge(exped, upto(b, N_EXP, n - SLOTS + 1))
                        for hh, kt, c in EXP_UNITS[u]:
                            h, bank, N = 4 * grp + hh, BANK_S + n % SLOTS, (T - kt) * P
                            pe.matmul(ps[:, bank, c:c + N], lhsT=kS[a][:, h, kt * P:(kt + 1) * P], rhs=qS[a][:, h, kt * P:S],
                                      start=True, stop=False)
                            ins = pe.matmul(ps[:, bank, c:c + P], lhsT=g.identb[:], rhs=g.maskb[:, 1, :], start=False, stop=True)
                        ins.then_inc(st_made, 1)
                    elif name == "weigh":
                        grp, u = divmod(n, N_GRP)
                        pe.wait_ge(exped, upto(b, N_EXP, n + 1))
                        if n == 0:
                            pe.wait_ge(v_made, upto(b, 1, 1))
                        if u == 0:
                            pe.wait_ge(OT_made, upto(b, GROUPS, grp - 1))
                        for hh, kt, c in EXP_UNITS[u]:
                            ins = pe.matmul(ps[32 * hh:32 * hh + 32, BANK_O + grp % 2, kt * P:S], lhsT=va[a][:, kt, 4 * grp + hh, :],
                                            rhs=PT[:, n % SLOTS, c:c + (T - kt) * P], start=kt == 0, stop=kt == LAST_KT)
                        ins.then_inc(pv_done, 1)
                    elif name == "turn_out":
                        pe.wait_ge(OT_made, upto(b, GROUPS, n + 1))
                        for t in range(T):
                            ins = pe.transpose(ps[:, BANK_M, t * P:(t + 1) * P], OT[:, t * P:(t + 1) * P], g.ident[:])
                        ins.then_inc(OT_turned, 1)
                    elif name == "out_turn":
                        pe.wait_ge(o_made, upto(b, GROUPS, GROUPS))
                        for t in range(T):
                            ins = pe.transpose(ps[:, BANK_M, t * P:(t + 1) * P], o[:, t, :], g.ident[:])
                        ins.then_inc(o_turned, 1)
                    elif name == "out_project":
                        pe.wait_ge(oT_made, upto(b, 1, 1))
                        pe.wait_ge(squared, upto(b, 1, 1))
                        for t in range(T):
                            out = ps[:, BANK_M, t * P:(t + 1) * P]
                            pe.matmul(out, lhsT=oT[:, t * P:(t + 1) * P], rhs=g.wt[:, 3, :], start=True, stop=False)
                            ins = pe.matmul(out, lhsT=h2[a][:, t * P:(t + 1) * P], rhs=g.ws2[:], start=False, stop=True)
                        ins.then_inc(acc_made, 1)

            pipelined(pe, turn, l0_plan)

        @block.scalar
        def _(act):
            act.mul(bq[:], g.bqkv[:, 0:1], HD0 ** -0.5).then_inc(bq_made, 1)
            act.wait_ge(bq_made, 1)

            def turn(i, plan, a, j=None):
                for name, *idx in plan:
                    b = i + AHEAD[name]
                    n = idx[0] if idx else 0
                    if name == "turn":
                        act.wait_ge(turned, upto(b, 1, 1))
                        act.wait_ge(l_proj, upto(b, 1, 0))
                        act.wait_ge(xnT_kept, upto(b, 1, 0))
                        act.copy(xnT[:], ps[:, BANK_M, :]).then_inc(xnT_made, 1)
                    elif name == "project":
                        act.wait_ge(qk_proj, upto(b, 2, n + 1))
                        act.wait_ge(rest_made, upto(b, 2, n))
                        act.wait_ge(stored, upto(b, 32, 16 * n - 16))
                        bias, scale = (bq[:], HD0 ** -0.5) if n == 0 else (g.bqkv[:, 1:2], 1.0)
                        act.activation(full[:], ps[:, BANK_M, :], ACT.Identity, bias=bias, scale=scale)
                        act.activation(part[:, n, 0, :], ps[:, BANK_M, :], ACT.Identity, bias=bias, scale=scale).then_inc(full_made, 1)
                    elif name == "split" and idx[1] == 0:
                        act.wait_ge(rest_made, upto(b, 2, n + 1))
                        act.copy(part[:, n, 1, :], rest[:]).then_inc(second_made, 1)
                    elif name == "hidden":
                        act.wait_ge(h_proj, upto(b, 1, 1))
                        act.wait_ge(squared, upto(b, 1, 0))
                        act.activation(hr[:], ps[0:64, BANK_M, :], ACT.Relu).then_inc(relu, 1)
                    elif name == "minus_max":
                        act.wait_ge(m_turned, upto(b, GROUPS, n + 1))
                        act.wait_ge(mlaid, upto(b, 16 * GROUPS, 16 * n))
                        act.copy(mT[:], ps[:, BANK_M, :].bitcast(BF16)[0:12, 0:S]).then_inc(mT_made, 1)
                    elif name == "scores":
                        act.wait_ge(st_made, upto(b, N_EXP, n + 1))
                        act.wait_ge(pv_done, upto(b, N_EXP, n - SLOTS + 1))
                        act.activation(PT[:, n % SLOTS, :], ps[:, BANK_S + n % SLOTS, :], ACT.Exp).then_inc(exped, 1)
                    elif name == "weigh" and n % N_GRP == N_GRP - 1:
                        grp = n // N_GRP
                        act.wait_ge(pv_done, upto(b, N_EXP, n + 1))
                        act.wait_ge(OT_turned, upto(b, GROUPS, grp))
                        act.copy(OT[:], ps[:, BANK_O + grp % 2, :]).then_inc(OT_made, 1)
                    elif name == "out_turn":
                        act.wait_ge(o_turned, upto(b, 1, 1))
                        act.wait_ge(acc_made, upto(b, 1, 0))
                        act.copy(oT[:], ps[:, BANK_M, :]).then_inc(oT_made, 1)

            pipelined(act, turn, l0_plan)

        @block.vector
        def _(dve):
            chains = {}

            def turn(i, plan, a, j=None):
                if j is None:
                    link = chains.setdefault(i < 0, Chain(dve, dch_pre if i < 0 else dch_post))
                else:
                    link = chains.setdefault("loop", Chain(dve, dch, j, 66))
                for name, *idx in plan:
                    b = i + AHEAD[name]
                    n = idx[0] if idx else 0
                    if name == "norm" and n == 0:
                        if j is not None:
                            dve.wait_ge(g.x_loaded, 16)
                        for t in range(T):
                            ins = dve.bn_stats(st[:, t, :], g.xs[:, bass.ds(b * T + t, 1), :])
                        link(ins, held)
                        for t in range(T):
                            ins = dve.bn_aggr(mv[:, t, :], st[:, t, :])
                        link(ins)
                        link(dve.tensor_scalar(rstd[:, 0, :], mv[:, :, 1], EPS, None, ALU.add))
                    elif name == "norm" and n < 3:
                        inv_sqrt(dve, link, rstd[:, 0, :], rstd[:, 1, :], rstd[:, 2, :], n - 1)
                    elif name == "norm":
                        dve.wait_ge(turned, upto(b, 1, 0))
                        for t in range(T):
                            ins = dve.tensor_scalar(xn[:, t, :], g.xs[:, bass.ds(b * T + t, 1), :], mv[:, t, 0:1],
                                                    rstd[:, 1, t:t + 1], ALU.subtract, ALU.mult)
                        ins.then_inc(xn_made, 1)
                    elif name == "split" and idx[1] == 0:
                        dve.wait_ge(full_made, upto(b, 2, n + 1))
                        dve.wait_ge(split, upto(b, 2, n))
                        dve.tensor_tensor(rest[:], full[:], part[:, n, 0, :], ALU.subtract).then_inc(rest_made, 1)
                    elif name == "split":
                        dve.wait_ge(second_made, upto(b, 2, n + 1))
                        dve.tensor_tensor(part[:, n, 2, :], rest[:], part[:, n, 1, :], ALU.subtract).then_inc(split, 1)
                    elif name == "v":
                        dve.wait_ge(v_set, 4)
                        dve.wait_ge(v_proj, upto(b, 1, 1))
                        dve.wait_ge(pv_done, upto(b - 1, N_EXP, 0))
                        for t in range(T):
                            ins = dve.tensor_tensor(va[1 - a][:, t, :, 0:HD0],
                                                    ps[:, BANK_M, t * P:(t + 1) * P].rearrange("p (h d) -> p h d", h=H0),
                                                    g.bv[:].rearrange("p (h d) -> p h d", h=H0), ALU.add)
                        ins.then_inc(v_made, 1)
                    elif name == "logits":
                        dve.wait_ge(l_proj, upto(b, 1, 1))
                        dve.tensor_copy(g.logits[:, bass.ds(b * T, T), :],
                                        ps[:, BANK_M, 0:T * 8].rearrange("p (t e) -> p t e", t=T)).then_inc(l_made, 1)
                    elif name == "max":
                        grp, u = divmod(n, len(MAX_UNITS))
                        qt, heads = MAX_UNITS[u]
                        if u == 0:
                            dve.wait_ge(m_made, upto(b, GROUPS, grp - 1))
                        dve.wait_ge(scored, upto(b, N_MAX, n + 1))
                        dve.tensor_reduce(mx[:, grp % 2, qt, heads[0]:heads[-1] + 1],
                                          ps[:, n % 2, 0:len(heads) * (qt + 1) * P].rearrange("p (h k) -> p h k", h=len(heads)),
                                          AX.X, ALU.max).then_inc(maxed, 1)
                    elif name == "parts":
                        dve.wait_ge(maxed, upto(b, N_MAX, (n + 1) * len(MAX_UNITS)))
                        dve.wait_ge(m_turned, upto(b, GROUPS, n))
                        link(dve.tensor_copy(mpart[:, :, 0, :], mx[:, n % 2]))
                        link(dve.tensor_tensor(mrest[:], mx[:, n % 2], mpart[:, :, 0, :], ALU.subtract))
                        link(dve.tensor_copy(mpart[:, :, 1, :], mrest[:]))
                        dve.tensor_tensor(mpart[:, :, 2, :], mrest[:], mpart[:, :, 1, :], ALU.subtract).then_inc(m_made, 1)
                    elif name == "turn_out":
                        dve.wait_ge(OT_turned, upto(b, GROUPS, n + 1))
                        dve.wait_ge(o_turned, upto(b, 1, 0))
                        O = ps[:, BANK_M, :].rearrange("p (t h d) -> p t h d", t=T, h=4)
                        link(dve.reciprocal(rsum[:], O[:, :, :, HD0]))
                        for t in range(T):
                            ins = dve.tensor_tensor(
                                o[:, t, 32 * n:32 * n + 32].rearrange("p (h d) -> p h d", h=4), O[:, t, :, 0:HD0],
                                rsum[:, t, :].rearrange("p (h a) -> p h a", a=1).to_broadcast([P, 4, HD0]), ALU.mult)
                        ins.then_inc(o_made, 1)
                    elif name == "out_project":
                        dve.wait_ge(acc_made, upto(b, 1, 1))
                        dve.wait_ge(x_bias, upto(b, 1, 1))
                        x_b = g.xs[:, bass.ds(b * T, T), :]
                        dve.tensor_tensor(x_b, ps[:, BANK_M, :].rearrange("p (t d) -> p t d", t=T), x_b,
                                          ALU.add).then_inc(x_made, 1)

            pipelined(dve, turn, l0_plan)
            chains["loop"].close()
            dve.wait_ge(x_made, upto(B, 1, 0))



def gates(nc, g):
    N = B * T
    with ExitStack() as ctx:
        m = Mem(nc, ctx, "gt_")
        top = m.sb("top8", [P, N, 8])
        d = m.sb("gate_d", [P, 4, N])
        total = m.sb("gate_total", [P, 1])
        topped, exped, dch, counted, summed, flagged = (m.sem(n) for n in "topped exped dch counted summed flagged".split())
        block = ctx.enter_context(nc.Block())

        @block.vector
        def _(dve):
            link = Chain(dve, dch)
            for t in range(N):
                ins = dve.max(top[:, t, :], g.logits[:, t, :])
            link(ins)
            dve.tensor_tensor(d[:, 0, :], top[:, :, 1], top[:, :, 0], ALU.subtract).then_inc(topped, 1)
            dve.wait_ge(exped, 1)
            link(dve.tensor_scalar(d[:, 2, :], d[:, 1, :], 1.0, None, ALU.add))
            link(dve.reciprocal(d[:, 3, :], d[:, 2, :]))
            link(dve.tensor_scalar(d[:, 3, :], d[:, 3, :], 1.0, None, ALU.is_ge))
            link(dve.tensor_tensor(g.gate[:], g.logits[:], top[:, :, 0:1].to_broadcast([P, N, 8]), ALU.is_equal))
            link(dve.tensor_tensor(g.gate[:], g.gate[:],
                                   d[:, 3, :].rearrange("p (n a) -> p n a", a=1).to_broadcast([P, N, 8]), ALU.mult))
            dve.tensor_reduce(total[:], g.gate[:], AX.XY, ALU.add).then_inc(counted, 1)
            dve.wait_ge(summed, 1)
            dve.tensor_copy(g.any_gate[:], g.ps[:, 0, 0:1]).then_inc(flagged, 1)
            dve.wait_ge(flagged, 1)

        @block.scalar
        def _(act):
            act.wait_ge(topped, 1)
            act.activation(d[:, 1, :], d[:, 0, :], ACT.Exp).then_inc(exped, 1)

        @block.sync
        def _(sp):
            sp.wait_ge(g.late_loaded, 16 * LATE_LOADS)

        @block.gpsimd
        def _(pool):
            pool.sem_clear(g.spent_sems)

        @block.tensor
        def _(pe):
            pe.wait_ge(counted, 1)
            pe.matmul(g.ps[:, 0, 0:1], lhsT=g.ones[:], rhs=total[:], start=True, stop=True).then_inc(summed, 1)


def routed_experts(nc, g):
    with ExitStack() as ctx:
        m = Mem(nc, ctx, "ex_")
        ps = g.ps
        gate = m.sb("gate_now", [P, T, 8])
        gT = m.sb("gT", [8, S])
        esel = m.sb("esel", [8, 4, 2, 64])
        r = m.sb("r", [P, 4, S])
        r2 = m.sb("r2", [P, 4, S])
        (e_set, gate_copied, g_turned, gT_made, h_made, spread, relu_made, squared, gated, y_made, added) = (
            m.sem(n) for n in (
                "e_set gate_copied g_turned gT_made h_made spread relu_made squared gated y_made added").split())
        block = ctx.enter_context(nc.Block())

        @block.sync
        def _(sp):
            for turns in (added, g_turned, gated, squared, y_made):
                sp.sem_inc(turns, 1)

        @block.gpsimd
        def _(pool):
            with pool.If(pool.value_load(g.any_gate[0:1, 0:1]) > 0):
                pool.memset(esel[:], 1.0).then_inc(e_set, 1)
                pool.wait_ge(e_set, 1)
                pool.affine_select(out=esel[:], in_=esel[:], compare_op=ALU.is_equal, fill=0.0, base=0,
                                   pattern=[[-2, 4], [-1, 2], [0, 64]], channel_multiplier=1).then_inc(e_set, 1)

        @block.tensor
        def _(pe):
            with pe.If(pe.value_load(g.any_gate[0:1, 0:1]) > 0):
                pe.wait_ge(e_set, 2)
                with pe.Fori(0, B) as i:
                    pe.wait_ge(gate_copied, i + 1)
                    for t in range(T):
                        ins = pe.transpose(ps[0:8, 0, t * P:(t + 1) * P], gate[:, t, :], g.ident[:])
                    ins.then_inc(g_turned, 1)
                    pe.wait_ge(gT_made, i + 1)
                    for c in range(4):
                        pe.wait_ge(squared, i * 4 + c + 1)
                        pe.matmul(ps[:, 1 + c % 2, :], lhsT=g.w1[:, 2 * c:2 * c + 2, :],
                                  rhs=g.xnT_all[:, bass.ds(i * S, S)], start=True, stop=True).then_inc(h_made, 1)
                        pe.wait_ge(gated, i * 4 + c + 1)
                        pe.matmul(ps[:, 3 + c % 2, :], lhsT=esel[:, c, :, :], rhs=gT[:], start=True,
                                  stop=True).then_inc(spread, 1)
                    pe.wait_ge(gated, i * 4 + 4 + 1)
                    pe.wait_ge(added, i + 1)
                    for t in range(T):
                        for c in range(4):
                            ins = pe.matmul(ps[:, 5, t * P:(t + 1) * P], lhsT=r2[:, c, t * P:(t + 1) * P], rhs=g.w2[:, c, :],
                                            start=c == 0, stop=c == 3)
                    ins.then_inc(y_made, 1)

        @block.scalar
        def _(act):
            with act.If(act.value_load(g.any_gate[0:1, 0:1]) > 0):
                with act.Fori(0, B) as i:
                    act.wait_ge(g_turned, i + 2)
                    act.copy(gT[:], ps[0:8, 0, :]).then_inc(gT_made, 1)
                    for c in range(4):
                        act.wait_ge(h_made, i * 4 + c + 1)
                        act.wait_ge(gated, i * 4 + 1)
                        act.activation(r[:, c, :], ps[:, 1 + c % 2, :], ACT.Relu).then_inc(relu_made, 1)

        @block.vector
        def _(dve):
            with dve.If(dve.value_load(g.any_gate[0:1, 0:1]) > 0):
                with dve.Fori(0, B) as i:
                    dve.wait_ge(g_turned, i + 1)
                    dve.tensor_copy(gate[:], g.gate[:, bass.ds(i * T, T), :]).then_inc(gate_copied, 1)
                    dve.wait_ge(y_made, i + 1)
                    for c in range(4):
                        dve.wait_ge(relu_made, i * 4 + c + 1)
                        dve.tensor_tensor(r2[:, c, :], r[:, c, :], r[:, c, :], ALU.mult).then_inc(squared, 1)
                        dve.wait_ge(spread, i * 4 + c + 1)
                        dve.wait_ge(squared, i * 4 + c + 2)
                        dve.tensor_tensor(r2[:, c, :], r2[:, c, :], ps[:, 3 + c % 2, :], ALU.mult).then_inc(gated, 1)
                    dve.wait_ge(y_made, i + 2)
                    x_b = g.xs[:, bass.ds(i * T, T), :]
                    dve.tensor_tensor(x_b, ps[:, 5, :].rearrange("p (t d) -> p t d", t=T), x_b, ALU.add).then_inc(added, 1)
                dve.wait_ge(added, B + 1)



KEEP = (256, 128)
FETCH = tuple(min(k * 9.0 / 8.0, S) for k in KEEP)
N_ITERS = 50
INNER = 7
OUTER = (N_ITERS - 1) // INNER
CAP = 80.0
ROUTES = 2 * B


FIRST_SLOTS = 32


def routing_slots():
    slots = [["fetch 0"], [], ["spread 0"], ["spread 1"], ["start 0"], ["cut 0"]]
    for k in range(OUTER * INNER):
        slots.append([f"sum {k}"])
        if k % INNER < INNER - 1:
            slots[-1].append(f"cut {k + 1}")
        else:
            slots[-1].append(f"rebase {k // INNER}")
            if k < OUTER * INNER - 1:
                slots.append([f"cut {k + 1}"])
    slots += [["score 0"], [], []] + [[f"pick {n}"] for n in range(KEEP[0] // 8)] + [["place 0"], ["place 1"]]
    return [[(name, int(n)) for name, n in (step.split() for step in slot)] for slot in slots]


FRONT = ([("turn_xn", 0), ("turn_xr", 0), ("cheb_k", 0), ("cheb_q", 0), ("cheb_v", 0), ("route", 0)]
         + [(name, c) for name in ("local_q", "local_k", "local_v") for c in range(4)]
         + [("sum_keys", t) for t in range(T)] + [("project_sums", n) for n in range(11)] + [("cheb_out", n) for n in range(11)])
COST = {"sum_keys": 0.75, "project_sums": 0.25}
GAPS = {"scores": 3, "minus_max": 1, "turned_scores": 3, "weigh": 2, "turn_out": 2, "project_out": 0.4}
CHEB = [(n, n // 2, n - n // 2) for n in range(2, 11)]
LATE = 6
BESIDE = {(0, "minus_max"): [("norm", 0)], (0, "turned_scores"): [("norm", 1)], (0, "turn_out"): [("norm", 2), ("norm", 3)],
          (1, "minus_max"): [("key_features", 6), ("key_features", 7)], (1, "turned_scores"): [("key_features", 8), ("key_features", 9)],
          (1, "weigh"): [("key_features", 10)], (1, "turn_out"): [("features", 6)],
          (2, "minus_max"): [("features", 7), ("features", 8)], (2, "turned_scores"): [("features", 9), ("features", 10)],
          (3, "scores"): [("norm", 4)], (3, "minus_max"): [("norm", 5)], (3, "turned_scores"): [("norm", 6)],
          (3, "turn_out"): [("norm", 7)]}


def l1_plan(windows, front, norm):
    pieces = list(FRONT) if front else []
    each = sum(COST.get(name, 1) for name, _ in FRONT) / (T * sum(GAPS.values()))
    steps, due, done = [], 0, 0
    for w in range(T):
        for name, gap in GAPS.items():
            if windows and name == "project_out" and w < T - 1:
                steps.append(("scores", w + 1))
            if windows and (name, w) not in steps:
                steps.append((name, w))
            due += gap * each
            beside = [step for step in BESIDE.get((w, name), ()) if (norm if step[0] == "norm" else front)]
            while pieces and done < due - 1e-6:
                steps.append(pieces.pop(0))
                done += COST.get(steps[-1][0], 1)
                steps.extend(beside[:1])
                beside = beside[1:]
            steps.extend(beside)
    if windows and not norm:
        start = steps.index(("route", 0)) + 1 if front else 0
        slots = routing_slots()
        cut = FIRST_SLOTS
        slots = slots[:cut] if front else slots[cut:]
        spread, each = steps[:start], len(slots) / (len(steps) - start)
        for k, step in enumerate(steps[start:]):
            spread.append(step)
            for slot in slots[int(k * each):int((k + 1) * each)]:
                spread.extend(slot)
        for slot in slots[int((len(steps) - start) * each):]:
            spread.extend(slot)
        steps = spread
    return steps


def layer1(nc, g):
    HL, HDL = 8, 64
    with ExitStack() as ctx:
        m = Mem(nc, ctx, "l1_")
        ps = g.ps
        st = m.sb("bn_parts", [P, T, 6])
        mv = m.sb("mean_var", [P, T, 2])
        sm = m.sb("small", [P, 8, T])
        xn = m.sb("xn", [P, T, P])
        xr_now = m.sb("xr_now", [P, T, P])
        sq = m.sb("squares", [P, P])
        xnT = m.sb("xnT", [P, S])
        xlT = m.sb("xlT", [P, S])
        s_row = m.sb("s_row", [2, S])
        raw = m.sb("raw", [P, 2, S])
        tq = m.sb("tq", [P, 11, S])
        tk = m.sb("tk", [P, 11, T, P])
        vc = m.sb("vc", [P, T, P])
        kvm = m.sb("kvm", [P, 11, P])
        kvT = m.sb("kvT", [P, 11, P])
        lq = [m.sb(f"lq{a}", [P, 4, S]) for a in range(2)]
        lk = [m.sb(f"lk{a}", [P, 4, S]) for a in range(2)]
        lv = [m.sb(f"lv{a}", [P, T, HL, HDL + 1]) for a in range(2)]
        mx = m.sb("mx", [P, 8])
        mrest = m.sb("mrest", [P, 8])
        mpart = m.sb("mpart", [P, 3, 8], BF16)
        mT = m.sb("mT", [24, P], BF16)
        PT = m.sb("PT", [P, 2, S])
        rsum = m.sb("rsum", [P, 2, 4])
        o = m.sb("o", [P, 4, 2, HDL])
        oT = m.sb("oT", [P, 4, P])
        s = m.sb("s", [P, 64])
        E = m.sb("E", [P, 64])
        low = m.sb("low", [P, 64])
        part = m.sb("part", [P, 1])
        col = m.sb("col", [P, 6])
        exponent = m.sb("exponent", [P, 1], I32)
        row = m.sb("row", [1, P])
        rmax = m.sb("rmax", [1, ROUTES])
        kblk = sq
        sc = m.sb("sc", [ROUTES, S])
        work = m.sb("work", [ROUTES, S])
        top = m.sb("top", [ROUTES, 8])
        picked, places = raw[0:ROUTES, 0, :], raw[0:ROUTES, 1, :]
        kept = picked
        (kblk_made, s_loaded, rmax_made, max_turned, row_made, max_spread, r_made, E_made, parted, summed, score_made, score_out, score_in,
         place_made, place_turned) = (m.sem(n) for n in (
             "kblk_made s_loaded rmax_made max_turned row_made max_spread r_made E_made parted summed score_made score_out score_in "
             "place_made place_turned").split())
        NA, NA1, C, NEG_R, RC, MX = range(6)
        (xn_made, xr_made, xn_turned, xr_turned, xnT_made, xlT_made, k_proj, q_proj, v_proj, s_proj, raw_made, vc_made,
         s_out, s_stored, tq1, tk1, tq_made, tk_made, lq_proj, lk_proj, lv_proj, lq_made, lk_made, lv_made,
         tk_late, tq_late, kv_prod, kvT_made, kv_out, kv_made, c_out, cheb_added, scored, m_made, m_turned, mT_made, st_made, exped, pv_done,
         o_made, o_turned, oT_made, y_made, x_made) = loop_sems = tuple(m.sem(n) for n in (
             "xn_made xr_made xn_turned xr_turned xnT_made xlT_made k_proj q_proj v_proj s_proj raw_made vc_made "
             "s_out s_stored tq1 tk1 tq_made tk_made lq_proj lk_proj lv_proj lq_made lk_made lv_made "
             "tk_late tq_late kv_prod kvT_made kv_out kv_made c_out cheb_added scored m_made m_turned mT_made st_made exped pv_done "
             "o_made o_turned oT_made y_made x_made").split())
        dve_held, pool_held, ones_set, dch_pre, dch, dch_post, pch_pre, pch, pch_post = (m.sem(n) for n in (
            "dve_held pool_held ones_set dch_pre dch dch_post pch_pre pch pch_post").split())
        M_COLS = slice(320, 384)
        Y_COLS = slice(384, 512)
        PER = {"sum_keys": T, "project_sums": 11, "cheb_out": 11, "local_q": 4, "local_k": 4, "local_v": 4}
        DONE = {"turn_xn": xn_turned, "turn_xr": xr_turned, "cheb_k": k_proj, "cheb_q": q_proj, "cheb_v": v_proj,
                "route": s_proj, "local_q": lq_proj, "local_k": lk_proj, "local_v": lv_proj, "sum_keys": kv_prod, "project_sums": kv_out,
                "cheb_out": c_out}
        EMPTIED = {"turn_xn": (xnT_made, 1), "turn_xr": (xlT_made, 1), "cheb_k": (raw_made, 2), "cheb_q": (raw_made, 2),
                   "cheb_v": (vc_made, 1), "route": (s_out, 1), "local_q": (lq_made, 4), "local_k": (lk_made, 4),
                   "local_v": (lv_made, 4), "sum_keys": (kvT_made, 1), "project_sums": (kv_made, 3),
                   "cheb_out": (cheb_added, 1)}
        opens, bank_of, filling = [], {}, {}
        for name, n in FRONT:
            if n == 0 or name.startswith("local") or (name == "project_sums" and n % 4 == 0):
                opens.append((name, n))
            bank_of[name, n] = 4 + (len(opens) - 1) % 3
            filling[name, n] = (1 if name == "cheb_q" else n // 4 if name == "project_sums"
                                else 0 if name in ("sum_keys", "cheb_out") else n)
        block = ctx.enter_context(nc.Block())

        def batch_of(i, name):
            return i + (2 if name == "norm" else 1 if name in DONE or name in ("features", "key_features") else 0)

        @block.sync
        def _(sp):
            for sem in loop_sems:
                sp.sem_inc(sem, PRIME)

            def turn(i, plan, a, j=None):
                for name, n in plan:
                    b = batch_of(i, name)
                    if name == "route":
                        sp.wait_ge(s_out, upto(b, 1, 1))
                        sp.dma_start(g.s_dram[:, bass.ds(b, 1), :], s_row[:].rearrange("r (a s) -> r a s", a=1)).then_inc(s_stored, 16)
                    elif name == "fetch":
                        sp.wait_ge(s_stored, upto(B, 16, 0))
                        sp.dma_start(s[:], g.s_dram.rearrange("r b (e n) -> (r b e) n", e=8)).then_inc(s_loaded, 16)
                    elif name == "score":
                        sp.wait_ge(score_made, 1)
                        sp.dma_start(g.sc_dram.rearrange("r (e n) -> (r e) n", e=8), E[:]).then_inc(score_out, 16)
                        sp.wait_ge(score_out, 16)
                        sp.dma_start(sc[:], g.sc_dram).then_inc(score_in, 16)

            pipelined(sp, turn, l1_plan)

        @block.gpsimd
        def _(pool):
            pool.memset(tk[:, 0, :, :], 1.0).then_inc(ones_set, 1)
            pool.memset(tq[:, 0, :], 1.0).then_inc(ones_set, 1)
            for a in range(2):
                pool.memset(lv[a][:], 1.0).then_inc(ones_set, 1)
            pool.memset(kvT[:], 0.0).then_inc(ones_set, 1)
            pool.wait_ge(ones_set, 5)
            chains = {}

            def turn(i, plan, a, j=None):
                if j is None:
                    link = chains.setdefault(i < 0, Chain(pool, pch_pre if i < 0 else pch_post))
                else:
                    link = chains.setdefault("loop", Chain(pool, pch, j, 40))
                for name, n in plan:
                    b = batch_of(i, name)
                    if name == "cheb_k":
                        pool.wait_ge(tk1, upto(b, 1, 1))
                        pool.wait_ge(kv_prod, upto(b, T, 0))
                        x = tk[:, 1, :, :]
                        for order, p, q in CHEB[:LATE - 2]:
                            t = tk[:, order, :, :]
                            link(pool.tensor_tensor(t, tk[:, p, :, :], tk[:, q, :, :], ALU.mult), pool_held)
                            if order % 2 == 0:
                                link(pool.tensor_scalar(t, t, 2.0, -1.0, ALU.mult, ALU.add))
                            else:
                                link(pool.tensor_scalar(t, t, 2.0, 0.0, ALU.mult, ALU.add))
                                link(pool.tensor_tensor(t, t, x, ALU.subtract))
                            pool.sem_inc(tk_made, 1)
                    elif name == "cheb_q":
                        pool.wait_ge(tq1, upto(b, 1, 1))
                        pool.wait_ge(c_out, upto(b, 11, 0))
                        for order, p, q in CHEB[:LATE - 2]:
                            t = tq[:, order, :]
                            link(pool.tensor_tensor(t, tq[:, p, :], tq[:, q, :], ALU.mult), pool_held)
                            if order % 2 == 0:
                                link(pool.tensor_scalar(t, t, 2.0, -1.0, ALU.mult, ALU.add))
                            else:
                                link(pool.tensor_scalar(t, t, 2.0, 0.0, ALU.mult, ALU.add))
                                link(pool.tensor_tensor(t, t, tq[:, 1, :], ALU.subtract))
                            pool.sem_inc(tq_made, 1)

            pipelined(pool, turn, l1_plan)
            chains["loop"].close()

        @block.tensor
        def _(pe):
            pe.wait_ge(ones_set, 5)

            def turn(i, plan, a, j=None):
                nxt = 1 - a
                last = {} if j is None and i < 0 else {bank_of[piece]: (piece, i) for piece in FRONT}
                for name, n in plan:
                    b = batch_of(i, name)
                    tok = slice(n * P, (n + 1) * P)
                    if name in DONE:
                        bank = bank_of[name, n]
                        if (name, n) in opens and bank in last:
                            piece, of = last[bank]
                            sem, per = EMPTIED[piece[0]]
                            pe.wait_ge(sem, upto(of, per, filling[piece] + 1))
                        last[bank] = ((name, n), b)
                        full = ps[:, bank, :]
                    if name == "turn_xn":
                        pe.wait_ge(xn_made, upto(b, 1, 1))
                        for t in range(T):
                            ins = pe.transpose(ps[:, bank, t * P:(t + 1) * P], xn[:, t, :], g.ident[:])
                    elif name == "turn_xr":
                        pe.wait_ge(xr_made, upto(b, 1, 1))
                        for t in range(T):
                            ins = pe.transpose(ps[:, bank, t * P:(t + 1) * P], xr_now[:, t, :], g.ident[:])
                    elif name == "cheb_q":
                        ins = pe.matmul(full, lhsT=g.wt[:, 4, :], rhs=xnT[:], start=True, stop=True)
                    elif name in ("cheb_k", "cheb_v"):
                        pe.wait_ge(xnT_made, upto(b, 1, 1))
                        for t in range(T):
                            ins = pe.matmul(ps[:, bank, t * P:(t + 1) * P], lhsT=xnT[:, t * P:(t + 1) * P],
                                            rhs=g.wt[:, 5 if name == "cheb_k" else 6, :], start=True, stop=True)
                    elif name == "route":
                        ins = pe.matmul(ps[0:2, bank, :], lhsT=g.tok[:], rhs=xnT[:], start=True, stop=True)
                    elif name == "local_q":
                        pe.wait_ge(xlT_made, upto(b, 1, 1))
                        ins = pe.matmul(full, lhsT=g.wql[:, tok], rhs=xlT[:], start=True, stop=True)
                    elif name == "local_k":
                        ins = pe.matmul(full, lhsT=g.wkvl[:, tok], rhs=xlT[:], start=True, stop=True)
                    elif name == "local_v":
                        ins = pe.matmul(full, lhsT=xlT[:, tok], rhs=g.wkvl[:, 512:1024], start=True, stop=True)
                    elif name == "sum_keys":
                        if n == 0:
                            pe.wait_ge(vc_made, upto(b, 1, 1))
                            pe.wait_ge(tk1, upto(b, 1, 1))
                            pe.wait_ge(tk_made, upto(b, LATE - 2, LATE - 2))
                            pe.wait_ge(tk_late, upto(b, 11 - LATE, 11 - LATE))
                        for first in range(0, P, 32):
                            heads = slice(first, first + 32)
                            ins = pe.matmul(ps[heads, bank, 0:11 * 32], lhsT=vc[:, n, heads], rhs=tk[:, :, n, heads],
                                            start=n == 0, stop=n == T - 1)
                    elif name == "project_sums":
                        pe.wait_ge(kvT_made, upto(b, 1, 1))
                        ins = pe.matmul(ps[:, bank, (n % 4) * P:(n % 4 + 1) * P], lhsT=kvT[:, n, :], rhs=g.wt[:, 7, :],
                                        start=True, stop=True)
                    elif name == "cheb_out":
                        if n == 0:
                            pe.wait_ge(kv_made, upto(b, 3, 3))
                            pe.wait_ge(tq_made, upto(b, LATE - 2, LATE - 2))
                            pe.wait_ge(tq_late, upto(b, 11 - LATE, 11 - LATE))
                        for product in range(4 * n, 4 * n + 4):
                            t, order = divmod(product, 11)
                            ins = pe.matmul(ps[:, bank, t * P:(t + 1) * P], lhsT=tq[:, order, t * P:(t + 1) * P],
                                            rhs=kvm[:, order, :], start=order == 0, stop=order == 10)
                    if name in DONE:
                        ins.then_inc(DONE[name], 1)
                    if name == "scores":
                        if n == 0:
                            pe.wait_ge(lk_made, upto(b, 4, 4))
                        pe.wait_ge(oT_made, upto(b, T, n))
                        for h in range(HL):
                            c, par = divmod(h, 2)
                            rows = slice(64 * par, 64 * par + 64)
                            ins = pe.matmul(ps[:, par, c * P:(c + 1) * P], lhsT=lq[a][rows, c, tok], rhs=lk[a][rows, c, tok],
                                            start=True, stop=True)
                        ins.then_inc(scored, 1)
                    elif name == "minus_max":
                        pe.wait_ge(m_made, upto(b, T, n + 1))
                        pe.wait_ge(o_made, upto(b, T, n))
                        pe.transpose(ps[:, 2, M_COLS].bitcast(BF16)[0:24, 0:P], mpart[:], g.identb[:]).then_inc(m_turned, 1)
                    elif name == "turned_scores":
                        pe.wait_ge(mT_made, upto(b, T, n + 1))
                        for h in range(HL):
                            c, par = divmod(h, 2)
                            rows = slice(64 * par, 64 * par + 64)
                            out = ps[:, par, c * P:(c + 1) * P]
                            pe.matmul(out, lhsT=lk[a][rows, c, tok], rhs=lq[a][rows, c, tok], start=True, stop=False)
                            ins = pe.matmul(out, lhsT=g.selm[:, par * 4 + c, :], rhs=mT[:], start=False, stop=True)
                        ins.then_inc(st_made, 1)
                    elif name == "weigh":
                        if n == 0:
                            pe.wait_ge(lv_made, upto(b, 4, 4))
                        pe.wait_ge(exped, upto(b, T, n + 1))
                        pe.wait_ge(x_made, upto(b, T, n))
                        for h in range(HL):
                            c, par = divmod(h, 2)
                            ins = pe.matmul(ps[:, 2 + par, c * (HDL + 1):(c + 1) * (HDL + 1)], lhsT=PT[:, par, c * P:(c + 1) * P],
                                            rhs=lv[a][:, n, h, :], start=True, stop=True)
                        ins.then_inc(pv_done, 1)
                    elif name == "turn_out":
                        pe.wait_ge(o_made, upto(b, T, n + 1))
                        for c in range(4):
                            ins = pe.transpose(ps[:, 0, c * P:(c + 1) * P], o[:, c, :, :], g.ident[:])
                        ins.then_inc(o_turned, 1)
                    elif name == "project_out":
                        pe.wait_ge(oT_made, upto(b, T, n + 1))
                        out = ps[:, 3, Y_COLS]
                        for c in range(4):
                            ins = pe.matmul(out, lhsT=oT[:, c, :], rhs=g.wol[:, c, :], start=c == 0, stop=c == 3)
                        ins.then_inc(y_made, 1)
                    elif name == "spread" and n == 0:
                        pe.wait_ge(rmax_made, 1)
                        pe.transpose(ps[0:1, 7, 0:P], col[:, MX:MX + 1], g.ident[:]).then_inc(max_turned, 1)
                    elif name == "spread":
                        pe.wait_ge(row_made, 1)
                        pe.matmul(ps[:, 7, P:P + 1], lhsT=row[:], rhs=g.ones[0:1, 0:1], start=True, stop=True).then_inc(max_spread, 1)
                    elif name == "sum":
                        pe.wait_ge(parted, n + 1)
                        pe.matmul(ps[:, 7, 0:1], lhsT=kblk[:], rhs=part[:], start=True, stop=True).then_inc(summed, 1)
                    elif name == "place" and n == 1:
                        pe.wait_ge(place_made, 2)
                        for t in range(T):
                            pe.transpose(ps[:, 7, t * ROUTES:(t + 1) * ROUTES], places[:, t * P:(t + 1) * P],
                                         g.ident[0:ROUTES, 0:ROUTES])
                            ins = pe.transpose(ps[:, 7, P + t * ROUTES:P + (t + 1) * ROUTES], kept[:, t * P:(t + 1) * P],
                                               g.ident[0:ROUTES, 0:ROUTES])
                        ins.then_inc(place_turned, 1)

            pipelined(pe, turn, l1_plan)

        @block.scalar
        def _(act):
            def turn(i, plan, a, j=None):
                nxt = 1 - a
                for name, n in plan:
                    b = batch_of(i, name)
                    if name in DONE:
                        full = ps[:, bank_of[name, n], :]
                        if name not in ("sum_keys", "project_sums", "cheb_out", "local_v"):
                            act.wait_ge(DONE[name], upto(b, PER.get(name, 1), n + 1))
                    if name == "turn_xn":
                        act.wait_ge(s_proj, upto(b, 1, 0))
                        act.copy(xnT[:], full).then_inc(xnT_made, 1)
                    elif name == "turn_xr":
                        act.wait_ge(lv_proj, upto(b, 4, 0))
                        act.activation(xlT[:], full, ACT.Identity, bias=0.0, scale=g.gl[:]).then_inc(xlT_made, 1)
                    elif name == "cheb_k":
                        act.wait_ge(tk1, upto(b, 1, 0))
                        act.mul(raw[:, 1, :], full, HD0 ** -0.5).then_inc(raw_made, 1)
                    elif name == "cheb_q":
                        act.wait_ge(tq1, upto(b, 1, 0))
                        act.mul(raw[:, 0, :], full, HD0 ** -0.5).then_inc(raw_made, 1)
                    elif name == "cheb_v":
                        act.wait_ge(kv_prod, upto(b, T, 0))
                        act.copy(vc[:].rearrange("p t d -> p (t d)"), full).then_inc(vc_made, 1)
                    elif name == "route":
                        act.wait_ge(s_stored, upto(b, 16, 0))
                        act.copy(s_row[:], ps[0:2, bank_of[name, n], :]).then_inc(s_out, 1)
                    elif name == "local_q":
                        act.wait_ge(st_made, upto(b - 1, T, 0))
                        act.mul(lq[nxt][:, n, :], full, HDL ** -0.5).then_inc(lq_made, 1)
                    elif name == "local_k":
                        act.copy(lk[nxt][:, n, :], full).then_inc(lk_made, 1)
                    elif name == "project_sums" and (n % 4 == 3 or n == 10):
                        first, count = n - n % 4, n % 4 + 1
                        act.wait_ge(kv_out, upto(b, 11, n + 1))
                        act.wait_ge(c_out, upto(b, 11, 0))
                        act.copy(kvm[:, first:first + count, :],
                                 full[:, 0:count * P].rearrange("p (n d) -> p n d", n=count)).then_inc(kv_made, 1)
                    elif name == "minus_max":
                        act.wait_ge(m_turned, upto(b, T, n + 1))
                        act.wait_ge(st_made, upto(b, T, n))
                        act.copy(mT[:], ps[:, 2, M_COLS].bitcast(BF16)[0:24, 0:P]).then_inc(mT_made, 1)
                    elif name == "turned_scores":
                        act.wait_ge(st_made, upto(b, T, n + 1))
                        act.wait_ge(pv_done, upto(b, T, n))
                        act.activation(PT[:], ps[:, 0:2, :], ACT.Exp).then_inc(exped, 1)
                    elif name == "turn_out":
                        act.wait_ge(o_turned, upto(b, T, n + 1))
                        act.wait_ge(y_made, upto(b, T, n))
                        act.copy(oT[:], ps[:, 0, :]).then_inc(oT_made, 1)
                    elif name == "start":
                        act.wait_ge(r_made, 1)
                        act.activation(col[:, C:C + 1], col[:, NA:NA + 1], ACT.Exp)
                        act.activation(E[:], low[:], ACT.Exp).then_inc(E_made, 1)
                    elif name == "rebase":
                        act.wait_ge(r_made, n + 2)
                        act.activation(E[:], low[:], ACT.Exp).then_inc(E_made, 1)

            pipelined(act, turn, l1_plan)

        @block.vector
        def _(dve):
            dve.wait_ge(ones_set, 5)
            chains = {}

            neg_r = col[:, NEG_R:NEG_R + 1]

            def turn(i, plan, a, j=None):
                nxt = 1 - a
                if j is None:
                    link = chains.setdefault(i < 0, Chain(dve, dch_pre if i < 0 else dch_post))
                else:
                    link = chains.setdefault("loop", Chain(dve, dch, j, 156))
                for name, n in plan:
                    b = batch_of(i, name)
                    if name == "norm" and n == 0:
                        for t in range(T):
                            ins = dve.bn_stats(st[:, t, :], g.xs[:, bass.ds(b * T + t, 1), :])
                        link(ins, dve_held)
                        for t in range(T):
                            ins = dve.bn_aggr(mv[:, t, :], st[:, t, :])
                        link(ins)
                        link(dve.tensor_scalar(sm[:, 0, :], mv[:, :, 1], EPS, None, ALU.add))
                    elif name == "norm" and n in (1, 2):
                        inv_sqrt(dve, link, sm[:, 0, :], sm[:, 1, :], sm[:, 2, :], n - 1)
                    elif name == "norm" and n == 3:
                        dve.wait_ge(xn_turned, upto(b, 1, 0))
                        for t in range(T):
                            ins = dve.tensor_scalar(xn[:, t, :], g.xs[:, bass.ds(b * T + t, 1), :], mv[:, t, 0:1],
                                                    sm[:, 1, t:t + 1], ALU.subtract, ALU.mult)
                        ins.then_inc(xn_made, 1)
                    elif name == "norm" and n == 4:
                        dve.wait_ge(xn_made, upto(b, 1, 1))
                        for t in range(T):
                            link(dve.tensor_tensor_reduce(sq[:], xn[:, t, :], xn[:, t, :], 1.0, 0.0, ALU.mult, ALU.add,
                                                          sm[:, 3, t:t + 1]))
                        link(dve.tensor_scalar(sm[:, 3, :], sm[:, 3, :], 1e-24, None, ALU.max))
                    elif name == "norm" and n in (5, 6):
                        inv_sqrt(dve, link, sm[:, 3, :], sm[:, 4, :], sm[:, 5, :], n - 5)
                    elif name == "norm":
                        dve.wait_ge(xr_turned, upto(b, 1, 0))
                        link(dve.tensor_scalar(sm[:, 4, :], sm[:, 4, :], float(D) ** 0.5, None, ALU.mult))
                        for t in range(T):
                            ins = dve.tensor_scalar(xr_now[:, t, :], xn[:, t, :], sm[:, 4, t:t + 1], None, ALU.mult)
                        ins.then_inc(xr_made, 1)
                        dve.wait_ge(xr_made, upto(b, 1, 1))
                        link(dve.tensor_copy(g.xr[:, bass.ds(b * T, T), 0:D], xr_now[:]))
                    elif name == "cheb_k":
                        dve.wait_ge(raw_made, upto(b, 2, 1))
                        dve.wait_ge(kv_prod, upto(b, T, 0))
                        dve.tensor_scalar(tk[:, 1, :, :].rearrange("p t d -> p (t d)"), raw[:, 1, :], 1.0, -1.0,
                                          ALU.min, ALU.max).then_inc(tk1, 1)
                    elif name == "cheb_q":
                        dve.wait_ge(raw_made, upto(b, 2, 2))
                        dve.wait_ge(c_out, upto(b, 11, 0))
                        dve.tensor_scalar(tq[:, 1, :], raw[:, 0, :], 1.0, -1.0, ALU.min, ALU.max).then_inc(tq1, 1)
                    elif name == "features":
                        dve.wait_ge(tq_made, upto(b, LATE - 2, LATE - 2))
                        _, p, q = CHEB[n - 2]
                        link(dve.scalar_tensor_tensor(tq[:, n, :], tq[:, p, :], 2.0, tq[:, q, :], ALU.mult, ALU.mult))
                        if n % 2 == 0:
                            link(dve.tensor_scalar(tq[:, n, :], tq[:, n, :], -1.0, None, ALU.add))
                        else:
                            link(dve.tensor_tensor(tq[:, n, :], tq[:, n, :], tq[:, 1, :], ALU.subtract))
                        dve.sem_inc(tq_late, 1)
                    elif name == "local_v":
                        dve.wait_ge(lv_proj, upto(b, 4, n + 1))
                        dve.wait_ge(pv_done, upto(b - 1, T, 0))
                        dve.tensor_copy(lv[nxt][:, n, :, 0:HDL],
                                        ps[:, bank_of[name, n], :].rearrange("p (h d) -> p h d", h=HL)).then_inc(lv_made, 1)
                    elif name == "key_features":
                        dve.wait_ge(tk_made, upto(b, LATE - 2, LATE - 2))
                        _, p, q = CHEB[n - 2]
                        x, y, t = (tk[:, order, :, :] for order in (p, q, n))
                        link(dve.scalar_tensor_tensor(t, x, 2.0, y, ALU.mult, ALU.mult))
                        if n % 2 == 0:
                            link(dve.tensor_scalar(t, t, -1.0, None, ALU.add))
                        else:
                            link(dve.tensor_tensor(t, t, tk[:, 1, :, :], ALU.subtract))
                        dve.sem_inc(tk_late, 1)
                    elif name == "sum_keys" and n == T - 1:
                        dve.wait_ge(kv_prod, upto(b, T, T))
                        dve.wait_ge(kv_out, upto(b, 11, 0))
                        for first in range(0, P, 32):
                            heads = slice(first, first + 32)
                            ins = dve.tensor_tensor(kvT[heads, :, heads],
                                                    ps[heads, bank_of[name, n], 0:11 * 32].rearrange("p (n d) -> p n d", n=11),
                                                    g.mbeta[heads, :, heads], ALU.mult)
                        ins.then_inc(kvT_made, 1)
                    elif name == "cheb_out" and n == 10:
                        dve.wait_ge(c_out, upto(b, 11, 11))
                        x_b = g.xs[:, bass.ds(b * T, T), :]
                        dve.tensor_tensor(x_b, ps[:, bank_of[name, n], :].rearrange("p (t d) -> p t d", t=T), x_b,
                                          ALU.add).then_inc(cheb_added, 1)
                    elif name == "scores":
                        dve.wait_ge(scored, upto(b, T, n + 1))
                        dve.wait_ge(m_turned, upto(b, T, n))
                        link(dve.tensor_reduce(mx[:], ps[:, 0:2, :].rearrange("p b (c k) -> p (b c) k", c=4), AX.X, ALU.max))
                        link(dve.tensor_copy(mpart[:, 0, :], mx[:]))
                        link(dve.tensor_tensor(mrest[:], mx[:], mpart[:, 0, :], ALU.subtract))
                        link(dve.tensor_copy(mpart[:, 1, :], mrest[:]))
                        dve.tensor_tensor(mpart[:, 2, :], mrest[:], mpart[:, 1, :], ALU.subtract).then_inc(m_made, 1)
                    elif name == "weigh":
                        dve.wait_ge(pv_done, upto(b, T, n + 1))
                        dve.wait_ge(o_turned, upto(b, T, n))
                        O = ps[:, 2:4, 0:4 * (HDL + 1)].rearrange("p b (c d) -> p b c d", c=4)
                        link(dve.reciprocal(rsum[:], O[:, :, :, HDL]))
                        for par in range(2):
                            ins = dve.tensor_tensor(o[:, :, par, :], O[:, par, :, 0:HDL],
                                                    rsum[:, par, :].rearrange("p (c a) -> p c a", a=1).to_broadcast([P, 4, HDL]),
                                                    ALU.mult)
                        ins.then_inc(o_made, 1)
                    elif name == "project_out":
                        dve.wait_ge(y_made, upto(b, T, n + 1))
                        if n == 0:
                            dve.wait_ge(cheb_added, upto(b, 1, 1))
                        x_t = g.xs[:, bass.ds(b * T + n, 1), :]
                        dve.tensor_tensor(x_t, ps[:, 3, Y_COLS].rearrange("p (a d) -> p a d", a=1), x_t, ALU.add).then_inc(x_made, 1)
                    elif name == "fetch":
                        for rows, k in ((slice(0, P // 2), FETCH[0]), (slice(P // 2, P), FETCH[1])):
                            dve.memset(col[rows, NA1:NA1 + 1], math.log(S) - math.log(k)).then_inc(kblk_made, 1)
                            dve.tensor_scalar(kblk[rows, :], g.blk[rows, :], 1.0 / k, None, ALU.mult).then_inc(kblk_made, 1)
                    elif name == "spread" and n == 0:
                        dve.wait_ge(s_loaded, 16)
                        dve.tensor_reduce(col[:, MX:MX + 1], s[:], AX.X, ALU.max).then_inc(rmax_made, 1)
                    elif name == "spread":
                        dve.wait_ge(max_turned, 1)
                        link(dve.tensor_reduce(rmax[:], ps[0:1, 7, 0:P].rearrange("p (r e) -> p r e", e=8), AX.X, ALU.max))
                        dve.tensor_copy(row[:].rearrange("p (r e) -> p r e", e=8),
                                        rmax[:].rearrange("p (r a) -> p r a", a=1).to_broadcast([1, ROUTES, 8])).then_inc(row_made, 1)
                    elif name == "start":
                        dve.wait_ge(max_spread, 1)
                        dve.wait_ge(kblk_made, 4)
                        link(dve.tensor_scalar(neg_r, ps[:, 7, P:P + 1], col[:, NA1:NA1 + 1], -1.0, ALU.min, ALU.mult))
                        dve.tensor_scalar(col[:, NA:NA + 1], col[:, NA1:NA1 + 1], neg_r, CAP, ALU.add, ALU.min)
                        dve.tensor_scalar(low[:], s[:], neg_r, CAP, ALU.add, ALU.min).then_inc(r_made, 1)
                    elif name == "cut":
                        if n % INNER == 0:
                            dve.wait_ge(E_made, n // INNER + 1)
                            c = col[:, C:C + 1]
                        else:
                            dve.wait_ge(summed, n)
                            c = ps[:, 7, 0:1]
                        dve.tensor_scalar(low[:], E[:], c, 0.0, ALU.min, ALU.add, accum_out=part[:]).then_inc(parted, 1)
                    elif name == "rebase":
                        dve.wait_ge(summed, (n + 1) * INNER)
                        link(dve.tensor_copy(col[:, RC:RC + 1], ps[:, 7, 0:1]))
                        bits = col[:, RC:RC + 1].bitcast(I32)
                        dve.tensor_scalar(exponent[:], bits, 23, None, ALU.logical_shift_right)
                        link(dve.tensor_scalar(col[:, C:C + 1].bitcast(I32), bits, 0x7FFFFF, 0x3F800000, ALU.bitwise_and,
                                               ALU.bitwise_or))
                        link(dve.tensor_scalar(col[:, NA:NA + 1], exponent[:], 127.0, math.log(2.0), ALU.subtract, ALU.mult))
                        link(dve.tensor_tensor(neg_r, neg_r, col[:, NA:NA + 1], ALU.subtract))
                        dve.tensor_scalar(low[:], s[:], neg_r, CAP, ALU.add, ALU.min).then_inc(r_made, 1)
                    elif name == "score":
                        link(dve.reciprocal(col[:, RC:RC + 1], col[:, C:C + 1]))
                        dve.wait_ge(E_made, OUTER + 1)
                        dve.tensor_scalar(E[:], E[:], col[:, RC:RC + 1], 1.0, ALU.mult, ALU.min).then_inc(score_made, 1)
                    elif name == "pick":
                        if n == 0:
                            dve.wait_ge(score_in, 16)
                        src = work if n else sc
                        rows = slice(0, ROUTES) if n < KEEP[1] // 8 else slice(0, B)
                        link(dve.max(top[rows, :], src[rows, :]))
                        link(dve.match_replace(work[rows, :], top[rows, :], src[rows, :], -1.0))
                    elif name == "place" and n == 0:
                        link(dve.tensor_scalar(picked, work[:], 0.0, None, ALU.is_lt))
                        link(dve.tensor_tensor_scan(places, tq[0:ROUTES, 0, :], picked, 0.0, ALU.mult, ALU.add))
                        link(dve.tensor_tensor(places, places, picked, ALU.mult))
                        dve.tensor_scalar(places, places, -1.0, None, ALU.add).then_inc(place_made, 1)
                        link(dve.tensor_scalar(kept[:], sc[:], -1.0, 1.0, ALU.mult, ALU.add))
                        dve.tensor_tensor(kept[:], kept[:], sc[:], ALU.add).then_inc(place_made, 1)
                    elif name == "place":
                        dve.wait_ge(place_turned, 1)
                        link(dve.tensor_copy(g.place[:], ps[:, 7, 0:T * ROUTES].rearrange("p (t r) -> p t r", t=T)))
                        link(dve.tensor_copy(g.weight[:], ps[:, 7, P:P + T * ROUTES].rearrange("p (t r) -> p t r", t=T)))
                        link(dve.tensor_copy(g.xr[:, :, D].rearrange("p (b t) -> p b t", t=T),
                                             g.weight[:, :, 0:B].rearrange("p t b -> p b t")))

            pipelined(dve, turn, l1_plan)
            chains["loop"].close()
            dve.wait_ge(x_made, upto(B, T, 0))



FILLS = [("gather", 0), ("turn_pick", 0), ("turn_xg", 0), ("kept_q", 0), ("kept_k", 0), ("kept_k", 1), ("kept_v", 0), ("kept_v", 1),
         ("scatter", 0)]


def heavy_plan(attend, front, pick):
    order = ["scores 0", "scores 1", "gather 0", "minus_max 0", "turn_pick 0", "turn_xg 0", "turned_scores 0", "turned_scores 1",
             "pick 0", "kept_q 0", "weigh 0", "weigh 1", "kept_k 0", "kept_k 1", "turn_out 0", "kept_v 0",
             "project_out 0", "kept_v 1", "scatter 0"]
    mine = {"gather": front, "turn_xg": front, "turn_pick": front, "kept_q": front, "kept_k": front, "kept_v": front, "pick": pick}
    steps = [(name, int(n)) for name, n in (step.split() for step in order)]
    return [(name, n) for name, n in steps if mine.get(name, attend)]


def heavy(nc, g, out):
    HL, HDL = 8, 64
    NK, NQ = KEEP
    KT = NK // P
    with ExitStack() as ctx:
        m = Mem(nc, ctx, "hv_")
        ps = g.ps
        pick = m.sb("pick", [P, T, NK + NQ])
        xg = m.sb("xg", [P, NK + NQ])
        wk = m.sb("wk", [P, KT])
        xgT = m.sb("xgT", [P, NK + NQ])
        q = [m.sb(f"q{a}", [P, 4, NQ]) for a in range(2)]
        k = [m.sb(f"k{a}", [P, 4, NK]) for a in range(2)]
        v = [m.sb(f"v{a}", [P, KT, HL, HDL + 1]) for a in range(2)]
        pickT = [m.sb(f"pickT{a}", [P, S]) for a in range(2)]
        mx = m.sb("mx", [P, 8])
        mrest = m.sb("mrest", [P, 8])
        mpart = m.sb("mpart", [P, 3, 8], BF16)
        mT = m.sb("mT", [24, P], BF16)
        PT = m.sb("PT", [P, 2, KT, S])
        rsum = m.sb("rsum", [P, 2, 4])
        o = m.sb("o", [P, 4, 2, HDL])
        oT = m.sb("oT", [P, 4, P])
        y = m.sb("y", [P, P])
        (picked, gathered, xg_turned, pick_turned, q_proj, k_proj, v_proj, xg_made, xgT_made, pickT_made, q_made, k_made, v_made,
         scored, m_made, m_turned, mT_made, st_made, exped, pv_done, o_made, o_turned, oT_made, y_done, y_made, scattered,
         x_made) = loop_sems = tuple(m.sem(n) for n in (
             "picked gathered xg_turned pick_turned q_proj k_proj v_proj xg_made xgT_made pickT_made q_made k_made v_made "
             "scored m_made m_turned mT_made st_made exped pv_done o_made o_turned oT_made y_done y_made scattered "
             "x_made").split())
        dch_pre, dch, dch_post, held, ones_set, stored = (m.sem(n) for n in "dch_pre dch dch_post held ones_set stored".split())
        M_COLS = slice(320, 384)
        Y_COLS = slice(384, 512)
        BANK = {fill: 6 + k % 2 for k, fill in enumerate(FILLS)}
        DONE = {"gather": (gathered, xg_made, 1), "turn_xg": (xg_turned, xgT_made, 1), "turn_pick": (pick_turned, pickT_made, 1),
                "kept_q": (q_proj, q_made, 1), "kept_k": (k_proj, k_made, 2), "kept_v": (v_proj, v_made, 2),
                "scatter": (scattered, x_made, 1)}
        block = ctx.enter_context(nc.Block())

        def batch_of(i, name):
            return i + (2 if name == "pick" else 1 if name != "scatter" and name in DONE else 0)

        @block.sync
        def _(sp):
            for sem in loop_sems:
                sp.sem_inc(sem, PRIME)

            def turn(i, plan, a, j=None):
                for name, n in plan:
                    b = batch_of(i, name)
                    if name == "scatter":
                        sp.wait_ge(x_made, upto(b, 1, 1))
                        sp.dma_start(out[bass.ds(b, 1)].rearrange("b (t p) d -> p (b t) d", p=P),
                                     g.xs[:, bass.ds(b * T, T), :]).then_inc(stored, 16)

            pipelined(sp, turn, heavy_plan)
            sp.wait_ge(stored, 16 * B)

        @block.gpsimd
        def _(pool):
            for a in range(2):
                pool.memset(v[a][:], 1.0).then_inc(ones_set, 1)

        @block.tensor
        def _(pe):
            def turn(i, plan, a, j=None):
                last = {} if j is None and i < 0 else {BANK["scatter", 0]: ("scatter", 0, i - 1)}
                for name, n in plan:
                    b = batch_of(i, name)
                    if name in DONE:
                        bank = BANK[name, n]
                        if bank in last:
                            of, k_last, b_last = last[bank]
                            _, emptied, per = DONE[of]
                            pe.wait_ge(emptied, upto(b_last, per, k_last + 1))
                        last[bank] = (name, n, b)
                    if name == "gather":
                        pe.wait_ge(picked, upto(b, 1, 1))
                        pe.wait_ge(v_made, upto(b, 2, 0))
                        for c in range(KT + 1):
                            for t in range(T):
                                ins = pe.matmul(ps[:, bank, c * (D + 1):(c + 1) * (D + 1)], lhsT=pick[:, t, c * P:(c + 1) * P],
                                                rhs=g.xr[:, bass.ds(b * T + t, 1), :], start=t == 0, stop=t == T - 1)
                    elif name == "turn_xg":
                        pe.wait_ge(xg_made, upto(b, 1, 1))
                        for c in range(KT + 1):
                            ins = pe.transpose(ps[:, bank, c * P:(c + 1) * P], xg[:, c * P:(c + 1) * P], g.ident[:])
                    elif name == "turn_pick":
                        for t in range(T):
                            ins = pe.transpose(ps[:, bank, t * P:(t + 1) * P], pick[:, t, NK:NK + NQ], g.ident[:])
                    elif name == "kept_q":
                        pe.wait_ge(xgT_made, upto(b, 1, 1))
                        for c in range(4):
                            ins = pe.matmul(ps[:, bank, c * NQ:(c + 1) * NQ], lhsT=g.wqh[:, c * P:(c + 1) * P],
                                            rhs=xgT[:, NK:NK + NQ], start=True, stop=True)
                    elif name == "kept_k":
                        for c in range(2):
                            first = (2 * n + c) * P
                            ins = pe.matmul(ps[:, bank, c * NK:(c + 1) * NK], lhsT=g.wkh[:, first:first + P],
                                            rhs=xgT[:, 0:NK], start=True, stop=True)
                    elif name == "kept_v":
                        ins = pe.matmul(ps[:, bank, :], lhsT=xgT[:, n * P:(n + 1) * P], rhs=g.wvh[:], start=True, stop=True)
                    elif name == "scatter":
                        pe.wait_ge(y_made, upto(b, 1, 1))
                        for t in range(T):
                            ins = pe.matmul(ps[:, bank, t * P:(t + 1) * P], lhsT=pickT[a][:, t * P:(t + 1) * P], rhs=y[:],
                                            start=True, stop=True)
                    if name in DONE:
                        ins.then_inc(DONE[name][0], 1)
                    if name == "scores":
                        if n == 0:
                            pe.wait_ge(q_made, upto(b, 1, 1))
                            pe.wait_ge(k_made, upto(b, 2, 2))
                            pe.wait_ge(oT_made, upto(b, 1, 0))
                        rows = slice(64 * n, 64 * n + 64)
                        for c in range(4):
                            ins = pe.matmul(ps[:, 2 * n + c // 2, (c % 2) * NK:(c % 2 + 1) * NK], lhsT=q[a][rows, c, :],
                                            rhs=k[a][rows, c, :], start=True, stop=True)
                        ins.then_inc(scored, 1)
                    elif name == "minus_max":
                        pe.wait_ge(m_made, upto(b, 1, 1))
                        pe.wait_ge(o_made, upto(b, 2, 0))
                        pe.transpose(ps[:, 4, M_COLS].bitcast(BF16)[0:24, 0:P], mpart[:], g.identb[:]).then_inc(m_turned, 1)
                    elif name == "turned_scores":
                        pe.wait_ge(mT_made, upto(b, 1, 1))
                        rows = slice(64 * n, 64 * n + 64)
                        for c2 in range(KT):
                            for c in range(4):
                                dst = ps[:, 2 * n + c2, c * P:(c + 1) * P]
                                pe.matmul(dst, lhsT=k[a][rows, c, c2 * P:(c2 + 1) * P], rhs=q[a][rows, c, :], start=True, stop=False)
                                ins = pe.matmul(dst, lhsT=g.selm[:, n * 4 + c, :], rhs=mT[:], start=False, stop=True)
                        ins.then_inc(st_made, 1)
                    elif name == "weigh":
                        pe.wait_ge(exped, upto(b, 2, n + 1))
                        if n == 0:
                            pe.wait_ge(v_made, upto(b, 2, 2))
                        else:
                            pe.wait_ge(y_made, upto(b, 1, 0))
                        for c in range(4):
                            for c2 in range(KT):
                                ins = pe.matmul(ps[:, 4 + n, c * (HDL + 1):(c + 1) * (HDL + 1)],
                                                lhsT=PT[:, n, c2, c * P:(c + 1) * P], rhs=v[a][:, c2, 2 * c + n, :],
                                                start=c2 == 0, stop=c2 == KT - 1)
                        ins.then_inc(pv_done, 1)
                    elif name == "turn_out":
                        pe.wait_ge(o_made, upto(b, 2, 2))
                        for c in range(4):
                            ins = pe.transpose(ps[:, 0, c * P:(c + 1) * P], o[:, c, :, :], g.ident[:])
                        ins.then_inc(o_turned, 1)
                    elif name == "project_out":
                        pe.wait_ge(oT_made, upto(b, 1, 1))
                        for c in range(4):
                            ins = pe.matmul(ps[:, 5, Y_COLS], lhsT=oT[:, c, :], rhs=g.woh[:, c, :], start=c == 0, stop=c == 3)
                        ins.then_inc(y_done, 1)

            pe.wait_ge(ones_set, 2)
            pipelined(pe, turn, heavy_plan)

        @block.scalar
        def _(act):
            def turn(i, plan, a, j=None):
                nxt = 1 - a
                for name, n in plan:
                    b = batch_of(i, name)
                    if name in ("gather", "turn_xg", "kept_q", "kept_k"):
                        done, _, per = DONE[name]
                        act.wait_ge(done, upto(b, per, n + 1))
                        full = ps[:, BANK[name, n], :]
                    if name == "gather":
                        act.wait_ge(xg_turned, upto(b, 1, 0))
                        act.wait_ge(v_made, upto(b, 2, 0))
                        kept = full[:, 0:(KT + 1) * (D + 1)].rearrange("p (c d) -> p c d", d=D + 1)
                        act.copy(wk[:], kept[:, 0:KT, D])
                        act.copy(xg[:].rearrange("p (c d) -> p c d", d=D), kept[:, :, 0:D]).then_inc(xg_made, 1)
                    elif name == "turn_xg":
                        act.wait_ge(v_proj, upto(b, 2, 0))
                        act.activation(xgT[:], full[:, 0:NK + NQ], ACT.Identity, bias=0.0, scale=g.gh[:]).then_inc(xgT_made, 1)
                    elif name == "kept_q":
                        act.wait_ge(st_made, upto(b - 1, 2, 0))
                        act.mul(q[nxt][:], full.rearrange("p (c n) -> p c n", c=4), HDL ** -0.5).then_inc(q_made, 1)
                    elif name == "kept_k":
                        act.copy(k[nxt][:, 2 * n:2 * n + 2, :], full.rearrange("p (c n) -> p c n", c=2)).then_inc(k_made, 1)
                    elif name == "minus_max":
                        act.wait_ge(m_turned, upto(b, 1, 1))
                        act.wait_ge(st_made, upto(b, 2, 0))
                        act.copy(mT[:], ps[:, 4, M_COLS].bitcast(BF16)[0:24, 0:P]).then_inc(mT_made, 1)
                    elif name == "turned_scores":
                        act.wait_ge(st_made, upto(b, 2, n + 1))
                        act.wait_ge(pv_done, upto(b - 1, 2, n + 1))
                        act.activation(PT[:, n], ps[:, 2 * n:2 * n + 2, :], ACT.Exp).then_inc(exped, 1)
                    elif name == "turn_out":
                        act.wait_ge(o_turned, upto(b, 1, 1))
                        act.wait_ge(y_done, upto(b, 1, 0))
                        act.copy(oT[:], ps[:, 0, :]).then_inc(oT_made, 1)
                    elif name == "project_out":
                        act.wait_ge(y_done, upto(b, 1, 1))
                        act.wait_ge(scattered, upto(b, 1, 0))
                        act.copy(y[:], ps[:, 5, Y_COLS]).then_inc(y_made, 1)

            pipelined(act, turn, heavy_plan)

        @block.vector
        def _(dve):
            dve.wait_ge(ones_set, 2)
            chains = {}

            def turn(i, plan, a, j=None):
                nxt = 1 - a
                if j is None:
                    link = chains.setdefault(i < 0, Chain(dve, dch_pre if i < 0 else dch_post))
                else:
                    link = chains.setdefault("loop", Chain(dve, dch, j, 14))
                for name, n in plan:
                    b = batch_of(i, name)
                    if name == "pick":
                        dve.wait_ge(pick_turned, upto(b, 1, 0))
                        for t in range(T):
                            dve.tensor_scalar(pick[:, t, 0:NK], g.iota[:], g.place[:, t, bass.ds(b, 1)], None, ALU.is_equal)
                            ins = dve.tensor_scalar(pick[:, t, NK:NK + NQ], g.iota[:, 0:NQ], g.place[:, t, bass.ds(b + B, 1)],
                                                    None, ALU.is_equal)
                        ins.then_inc(picked, 1)
                    elif name == "turn_pick":
                        dve.wait_ge(pick_turned, upto(b, 1, 1))
                        dve.wait_ge(scattered, upto(b - 1, 1, 0))
                        dve.tensor_copy(pickT[nxt][:], ps[:, BANK[name, n], :]).then_inc(pickT_made, 1)
                    elif name == "kept_v":
                        dve.wait_ge(v_proj, upto(b, 2, n + 1))
                        dve.wait_ge(xg_made, upto(b, 1, 1))
                        dve.wait_ge(pv_done, upto(b - 1, 2, 0))
                        dve.tensor_scalar(v[nxt][:, n, :, 0:HDL], ps[:, BANK[name, n], :].rearrange("p (h d) -> p h d", h=HL),
                                          wk[:, n:n + 1], None, ALU.mult).then_inc(v_made, 1)
                    elif name == "scores":
                        dve.wait_ge(scored, upto(b, 2, n + 1))
                        link(dve.tensor_reduce(mx[:, 4 * n:4 * n + 4], ps[:, 2 * n:2 * n + 2, :].rearrange("p b (c k) -> p (b c) k", c=2),
                                               AX.X, ALU.max))
                        if n == 1:
                            dve.wait_ge(m_turned, upto(b, 1, 0))
                            link(dve.tensor_copy(mpart[:, 0, :], mx[:]))
                            link(dve.tensor_tensor(mrest[:], mx[:], mpart[:, 0, :], ALU.subtract))
                            link(dve.tensor_copy(mpart[:, 1, :], mrest[:]))
                            dve.tensor_tensor(mpart[:, 2, :], mrest[:], mpart[:, 1, :], ALU.subtract).then_inc(m_made, 1)
                    elif name == "weigh":
                        dve.wait_ge(pv_done, upto(b, 2, n + 1))
                        if n == 0:
                            dve.wait_ge(o_turned, upto(b, 1, 0))
                        O = ps[:, 4 + n, 0:4 * (HDL + 1)].rearrange("p (c d) -> p c d", c=4)
                        link(dve.reciprocal(rsum[:, n, :], O[:, :, HDL]))
                        dve.tensor_tensor(o[:, :, n, :], O[:, :, 0:HDL],
                                          rsum[:, n, :].rearrange("p (c a) -> p c a", a=1).to_broadcast([P, 4, HDL]),
                                          ALU.mult).then_inc(o_made, 1)
                    elif name == "scatter":
                        dve.wait_ge(scattered, upto(b, 1, 1))
                        for t in range(T):
                            x_t = g.xs[:, bass.ds(b * T + t, 1), :]
                            ins = dve.scalar_tensor_tensor(
                                x_t, ps[:, BANK[name, n], t * P:(t + 1) * P].rearrange("p (a d) -> p a d", a=1),
                                g.weight[:, t, bass.ds(b + B, 1)], x_t, ALU.mult, ALU.add)
                        ins.then_inc(x_made, 1)

            pipelined(dve, turn, heavy_plan)
            chains["loop"].close()
            dve.wait_ge(x_made, upto(B, 1, 0))


class Shared:

    def __init__(self, nc, ctx):
        m = Mem(nc, ctx)
        self.ps = ctx.enter_context(nc.psum_tensor("ps", [P, 8, 512], F32))
        self.xs = m.sb("xs", [P, B * T, P])
        self.ident = m.sb("ident", [P, P])
        self.identb = m.sb("identb", [P, P], BF16)
        self.maskb = m.sb("maskb", [P, 2, P], BF16)
        self.ones = m.sb("ones", [P, P])
        self.blk = m.sb("blk", [P, P])
        self.iota = m.sb("iota", [P, 256])
        self.selm = m.sb("selm", [24, 8, P], BF16)
        self.mbeta = m.sb("mbeta", [P, 11, P])
        self.wt = m.sb("wt", [P, 8, P])
        self.wkh, self.wvh = m.sb("wkh", [P, 512]), m.sb("wvh", [P, 512])
        self.ws1, self.ws2, self.wr = m.sb("ws1", [P, 64]), m.sb("ws2", [64, P]), m.sb("wr", [P, 8])
        self.w1, self.w2 = m.sb("w1", [P, 8, 64]), m.sb("w2", [P, 4, P])
        self.bqkv, self.bv, self.bo = m.sb("bqkv", [P, 3]), m.sb("bv", [P, P]), m.sb("bo", [P, P])
        self.gl, self.gh, self.tok = m.sb("gl", [P, 1]), m.sb("gh", [P, 1]), m.sb("tok", [P, 2])
        self.wql, self.wkvl, self.wol = m.sb("wql", [P, 512]), m.sb("wkvl", [P, 1024]), m.sb("wol", [P, 4, P])
        self.wqh, self.woh = m.sb("wqh", [P, 512]), m.sb("woh", [P, 4, P])
        self.logits = m.sb("logits", [P, B * T, 8])
        self.gate = m.sb("gate", [P, B * T, 8])
        self.any_gate = m.sb("any_gate", [P, 1], I32)
        self.xnT_all = m.sb("kept_x", [P, B * T * (D + 1)])
        self.spent_sems = range(0)
        self.x_loaded, self.late_loaded = m.sem("x_loaded"), m.sem("late_loaded")
        self.xr = self.xnT_all[:].rearrange("p (n d) -> p n d", d=D + 1)
        self.place = m.sb("place", [P, T, 2 * B])
        self.weight = m.sb("weight", [P, T, 2 * B])
        self.s_dram = nc.dram_tensor("s_dram", [2, B, S], F32).ap()
        self.sc_dram = nc.dram_tensor("sc_dram", [2 * B, S], F32).ap()


def build(nc, w, out):
    with ExitStack() as ctx:
        g = Shared(nc, ctx)
        setup(nc, g, w)
        layer0(nc, g, w)
        gates(nc, g)
        routed_experts(nc, g)
        layer1(nc, g)
        heavy(nc, g, out)


_INS = ['L0_attn_x', 'L0_attn_w_qkv', 'L0_attn_b_qkv', 'L0_attn_w_out', 'L0_attn_b_out', 'L0_ffn_Ws1', 'L0_ffn_Ws2',
        'L0_ffn_W1', 'L0_ffn_W2', 'L0_ffn_Wr', 'L1_attn_w_in', 'L1_attn_w_out', 'L1_attn_beta', 'L1_ffn_gamma_light',
        'L1_ffn_wq_light', 'L1_ffn_wkv_light', 'L1_ffn_wo_light', 'L1_ffn_q_routing_token',
        'L1_ffn_kv_routing_token', 'L1_ffn_gamma_heavy', 'L1_ffn_wq_heavy', 'L1_ffn_wkv_heavy', 'L1_ffn_wo_heavy']


def kernel(**inputs):
    import numpy as _np
    import concourse.bacc as _bacc
    from concourse.bass_utils import run_bass_kernel_spmd as _run

    nc = _bacc.Bacc("TRN2", target_bir_lowering=False, num_devices=1)
    arrays, args = {}, {}
    for name in _INS:
        a = _np.ascontiguousarray(inputs[name])
        arrays[f"in_{name}_dram"] = a
        args[name] = nc.dram_tensor(f"in_{name}_dram", a.shape, mybir.dt.from_np(a.dtype), kind="ExternalInput").ap()
    out = nc.dram_tensor("out_0_dram", (B, S, D), F32, kind="ExternalOutput").ap()
    build(nc, args, out)
    r = _run(nc, [arrays], core_ids=[0])
    return r.results[0]["out_0_dram"]
```
